# Optimizing a Trainium2 kernel written in Bass

```python
import numpy as np
import jax
import jax.numpy as jnp

def _softmax(x, axis=-1):
    return jax.nn.softmax(x, axis=axis)

def _gelu(x):
    return jax.nn.gelu(x, approximate=True)

def _silu(x):
    return jax.nn.silu(x)

def _sigmoid(x):
    return jax.nn.sigmoid(x)

def _layernorm(x, axis=-1, eps=1e-05):
    m = jnp.mean(x, axis=axis, keepdims=True)
    v = jnp.var(x, axis=axis, keepdims=True)
    return (x - m) / jnp.sqrt(v + eps)

def _scatter_add(tgt, idx, src, axis=0):
    return tgt.at[idx].add(src)

def _segment_sum(src, seg, n):
    return jax.ops.segment_sum(src, seg, n)
kernel_name = 'mk_xattn_ffn_d2_seqx_r8_d050d2'

def setup_inputs(seed: int=0):
    np.random.seed(seed)
    _w = jnp.asarray

    def _rec_inputs():
        import jax
        import jax.numpy as jnp
        _rk = jax.random.key(seed)
        x = -0.0002928 + 1 * jax.random.normal(jax.random.fold_in(_rk, 1), (16, 128, 128), jnp.float32)
        _lenS = 128 - jax.random.randint(jax.random.fold_in(_rk, 7), (16,), 0, max(1, 128 // 4) + 1, jnp.int32)
        _lenS2 = 128 - jax.random.randint(jax.random.fold_in(_rk, 8), (16,), 0, max(1, 128 // 4) + 1, jnp.int32)
        _ctx_1024P = jax.random.normal(jax.random.fold_in(_rk, 11), (16, 16, 128), jnp.float32)
        _ctx_1024c = jax.random.dirichlet(jax.random.fold_in(_rk, 511), 0.3 * jnp.ones((16,), jnp.float32), (16, 128))
        _ctx_1024t = jnp.einsum('bsk,bkd->bsd', _ctx_1024c, _ctx_1024P)
        _ctx_1024t = _ctx_1024t * jax.lax.rsqrt(jnp.mean(jnp.square(_ctx_1024t)) + 1e-12) * 0.953939
        ctx_1024 = -1.39393e-06 + 0.999914 * (_ctx_1024t + 0.3 * jax.random.normal(jax.random.fold_in(_rk, 611), (16, 128, 128), jnp.float32))
        fside_BxSx4_0 = jax.random.uniform(jax.random.fold_in(_rk, 12), (16, 128, 4), jnp.float32, 0.0, 0.999884)
        return (x, ctx_1024, fside_BxSx4_0)
    x, ctx_1024, fside_BxSx4_0 = _rec_inputs()

    def _L0_xattn_setup():
        import jax, jax.numpy as jnp
        import numpy as np
        D_MODEL = 128
        H = 16
        D_K = 64
        D_V = 64
        D_G = D_MODEL // H
        WAVE_LEN = 1000.0
        B = 8
        N = 64

        def box_relational_embedding(boxes, dim_g=D_G):
            x_min, y_min, x_max, y_max = jnp.split(boxes, 4, axis=-1)
            cx = (x_min + x_max) * 0.5
            cy = (y_min + y_max) * 0.5
            w = x_max - x_min + 1.0
            h = y_max - y_min + 1.0
            delta_x = jnp.log(jnp.clip(jnp.abs((cx - jnp.swapaxes(cx, 1, 2)) / w), 0.001, None))
            delta_y = jnp.log(jnp.clip(jnp.abs((cy - jnp.swapaxes(cy, 1, 2)) / h), 0.001, None))
            delta_w = jnp.log(w / jnp.swapaxes(w, 1, 2))
            delta_h = jnp.log(h / jnp.swapaxes(h, 1, 2))
            pos = jnp.stack([delta_x, delta_y, delta_w, delta_h], axis=-1)
            n_freq = dim_g // 8
            feat_range = jnp.arange(n_freq, dtype=jnp.float32)
            dim_mat = 1.0 / WAVE_LEN ** (feat_range / n_freq)
            mul = (100.0 * pos)[..., None] * dim_mat
            b, n = (pos.shape[0], pos.shape[1])
            mul = mul.reshape(b, n, n, 4 * n_freq)
            return jnp.concatenate([jnp.sin(mul), jnp.cos(mul)], axis=-1)
        key = jax.random.key(seed)
        ks = jax.random.split(key, 12)
        s = 0.02
        inp = {'queries': jax.random.normal(ks[0], (B, N, D_MODEL), jnp.float32), 'keys': jax.random.normal(ks[1], (B, N, D_MODEL), jnp.float32), 'values': jax.random.normal(ks[2], (B, N, D_MODEL), jnp.float32), 'boxes': jax.random.uniform(ks[3], (B, N, 4), jnp.float32), 'Wq': jax.random.normal(ks[4], (H * D_K, D_MODEL), jnp.float32) * s, 'bq': jnp.zeros((H * D_K,), jnp.float32), 'Wk': jax.random.normal(ks[5], (H * D_K, D_MODEL), jnp.float32) * s, 'bk': jnp.zeros((H * D_K,), jnp.float32), 'Wv': jax.random.normal(ks[6], (H * D_V, D_MODEL), jnp.float32) * s, 'bv': jnp.zeros((H * D_V,), jnp.float32), 'Wo': jax.random.normal(ks[7], (D_MODEL, H * D_V), jnp.float32) * s, 'bo': jnp.zeros((D_MODEL,), jnp.float32), 'Wg': jax.random.normal(ks[8], (H, D_G), jnp.float32) * s, 'bg': jnp.zeros((H,), jnp.float32)}
        return inp
    _L0_xattn_all = _L0_xattn_setup()
    _L0_xattn_in = {k: v for k, v in _L0_xattn_all.items() if k in ('Wq', 'bq', 'Wk', 'bk', 'Wv', 'bv', 'Wo', 'bo', 'Wg', 'bg')}
    del _L0_xattn_all

    def _L0_ffn_setup():
        import jax, jax.numpy as jnp
        import numpy as np
        EPS = 1e-08

        def _ste(x, q):
            return x + jax.lax.stop_gradient(q - x)

        def quant_act_uint8(x):
            s = jax.lax.stop_gradient(jnp.maximum(jnp.max(x), EPS)) / 255.0
            q = jnp.clip(jnp.round(x / s), 0.0, 255.0) * s
            return (_ste(x, q), s)

        def quant_weight_int8_perchannel(w):
            s = jax.lax.stop_gradient(jnp.maximum(jnp.max(jnp.abs(w), axis=1, keepdims=True), EPS)) / 127.0
            q = jnp.clip(jnp.round(w / s), -128.0, 127.0) * s
            return (_ste(w, q), s[:, 0])

        def quant_bias_int32(b, s_in, s_w):
            s = jax.lax.stop_gradient(s_in * s_w)
            q = jnp.round(b / s) * s
            return _ste(b, q)

        def quant_linear(x, w, b):
            xq, s_in = quant_act_uint8(x)
            wq, s_w = quant_weight_int8_perchannel(w)
            bq = quant_bias_int32(b, s_in, s_w)
            return jnp.einsum('btd,fd->btf', xq, wq) + bq
        key = jax.random.key(seed)
        k1, k2, k3, k4, k5 = jax.random.split(key, 5)
        B, S, D, F = (4, 256, 128, 512)
        return {'x': jax.random.normal(k1, (B, S, D), dtype=jnp.float32), 'w1': jax.random.normal(k2, (F, D), dtype=jnp.float32) * (1.0 / np.sqrt(D)), 'b1': jax.random.normal(k3, (F,), dtype=jnp.float32) * 0.01, 'w2': jax.random.normal(k4, (D, F), dtype=jnp.float32) * (1.0 / np.sqrt(F)), 'b2': jax.random.normal(k5, (D,), dtype=jnp.float32) * 0.01}
    _L0_ffn_all = _L0_ffn_setup()
    _L0_ffn_in = {k: v for k, v in _L0_ffn_all.items() if k in ('w1', 'b1', 'w2', 'b2')}
    del _L0_ffn_all

    def _L1_xattn_setup():
        import jax, jax.numpy as jnp
        import numpy as np
        EMB = 128
        NH = 8
        HD = EMB // NH
        EPS = 1e-06

        def _mlstm_head(q, k, v, ig, fg):
            S, DH = q.shape
            log_fg = jax.nn.log_sigmoid(fg)
            cs = jnp.concatenate([jnp.zeros((1, 1), q.dtype), jnp.cumsum(log_fg, axis=0)], axis=0)
            fg_mat_full = cs - cs.T
            ltr = jnp.tril(jnp.ones((S, S), bool))
            log_fg_matrix = jnp.where(ltr, fg_mat_full[1:, 1:], -jnp.inf)
            log_D = log_fg_matrix + ig.T
            max_log_D = jnp.max(log_D, axis=-1, keepdims=True)
            D = jnp.exp(log_D - max_log_D)
            qk = q @ (k.T / jnp.sqrt(jnp.asarray(DH, q.dtype)))
            C = qk * D
            normalizer = jnp.maximum(jnp.abs(C.sum(-1, keepdims=True)), jnp.exp(-max_log_D))
            return C / (normalizer + EPS) @ v
        key = jax.random.key(seed)
        ks = jax.random.split(key, 6)
        B, S = (2, 256)
        q = jax.random.normal(ks[0], (B, S, EMB), jnp.float32)
        k = jax.random.normal(ks[1], (B, S, EMB), jnp.float32)
        v = jax.random.normal(ks[2], (B, S, EMB), jnp.float32)
        igate_kernel = jax.random.normal(ks[3], (3 * EMB, NH), jnp.float32) * 0.02
        igate_bias = jax.random.normal(ks[4], (NH,), jnp.float32) * 0.1
        fgate_kernel = jax.random.normal(ks[5], (3 * EMB, NH), jnp.float32) * 0.02
        fgate_bias = jnp.linspace(3.0, 6.0, NH).astype(jnp.float32)
        return dict(q=q, k=k, v=v, igate_kernel=igate_kernel, igate_bias=igate_bias, fgate_kernel=fgate_kernel, fgate_bias=fgate_bias)
    _L1_xattn_all = _L1_xattn_setup()
    _L1_xattn_in = {k: v for k, v in _L1_xattn_all.items() if k in ('igate_kernel', 'igate_bias', 'fgate_kernel', 'fgate_bias')}
    del _L1_xattn_all

    def _L1_ffn_setup():
        import jax, jax.numpy as jnp
        import numpy as np
        B, S, H = (2, 256, 128)
        E, K, F_EXP, F_SHARED = (16, 2, 64, 128)
        key = jax.random.key(seed)
        ks = jax.random.split(key, 9)
        sc = 1.0 / np.sqrt(H)
        scf = 1.0 / np.sqrt(F_EXP)
        scfs = 1.0 / np.sqrt(F_SHARED)
        return {'x': jax.random.normal(ks[0], (B, S, H), dtype=jnp.float32), 'router_w': jax.random.normal(ks[1], (H, E), dtype=jnp.float32) * sc, 'gate_w': jax.random.normal(ks[2], (E, H, F_EXP), dtype=jnp.float32) * sc, 'up_w': jax.random.normal(ks[3], (E, H, F_EXP), dtype=jnp.float32) * sc, 'down_w': jax.random.normal(ks[4], (E, F_EXP, H), dtype=jnp.float32) * scf, 'shared_gate_w': jax.random.normal(ks[5], (H, F_SHARED), dtype=jnp.float32) * sc, 'shared_up_w': jax.random.normal(ks[6], (H, F_SHARED), dtype=jnp.float32) * sc, 'shared_down_w': jax.random.normal(ks[7], (F_SHARED, H), dtype=jnp.float32) * scfs}
    _L1_ffn_all = _L1_ffn_setup()
    _L1_ffn_in = {k: v for k, v in _L1_ffn_all.items() if k in ('router_w', 'gate_w', 'up_w', 'down_w', 'shared_gate_w', 'shared_up_w', 'shared_down_w')}
    del _L1_ffn_all
    return {'x': x, 'ctx_1024': ctx_1024, 'fside_BxSx4_0': fside_BxSx4_0, 'L0_xattn_Wq': _L0_xattn_in['Wq'], 'L0_xattn_bq': _L0_xattn_in['bq'], 'L0_xattn_Wk': _L0_xattn_in['Wk'], 'L0_xattn_bk': _L0_xattn_in['bk'], 'L0_xattn_Wv': _L0_xattn_in['Wv'], 'L0_xattn_bv': _L0_xattn_in['bv'], 'L0_xattn_Wo': _L0_xattn_in['Wo'], 'L0_xattn_bo': _L0_xattn_in['bo'], 'L0_xattn_Wg': _L0_xattn_in['Wg'], 'L0_xattn_bg': _L0_xattn_in['bg'], 'L0_ffn_w1': _L0_ffn_in['w1'], 'L0_ffn_b1': _L0_ffn_in['b1'], 'L0_ffn_w2': _L0_ffn_in['w2'], 'L0_ffn_b2': _L0_ffn_in['b2'], 'L1_xattn_igate_kernel': _L1_xattn_in['igate_kernel'], 'L1_xattn_igate_bias': _L1_xattn_in['igate_bias'], 'L1_xattn_fgate_kernel': _L1_xattn_in['fgate_kernel'], 'L1_xattn_fgate_bias': _L1_xattn_in['fgate_bias'], 'L1_ffn_router_w': _L1_ffn_in['router_w'], 'L1_ffn_gate_w': _L1_ffn_in['gate_w'], 'L1_ffn_up_w': _L1_ffn_in['up_w'], 'L1_ffn_down_w': _L1_ffn_in['down_w'], 'L1_ffn_shared_gate_w': _L1_ffn_in['shared_gate_w'], 'L1_ffn_shared_up_w': _L1_ffn_in['shared_up_w'], 'L1_ffn_shared_down_w': _L1_ffn_in['shared_down_w']}

def reference(x, ctx_1024, fside_BxSx4_0, L0_xattn_Wq, L0_xattn_bq, L0_xattn_Wk, L0_xattn_bk, L0_xattn_Wv, L0_xattn_bv, L0_xattn_Wo, L0_xattn_bo, L0_xattn_Wg, L0_xattn_bg, L0_ffn_w1, L0_ffn_b1, L0_ffn_w2, L0_ffn_b2, L1_xattn_igate_kernel, L1_xattn_igate_bias, L1_xattn_fgate_kernel, L1_xattn_fgate_bias, L1_ffn_router_w, L1_ffn_gate_w, L1_ffn_up_w, L1_ffn_down_w, L1_ffn_shared_gate_w, L1_ffn_shared_up_w, L1_ffn_shared_down_w):
    import jax
    import jax.numpy as jnp

    def _L0_xattn_ref(queries, keys, values, boxes, Wq, bq, Wk, bk, Wv, bv, Wo, bo, Wg, bg):
        import jax, jax.numpy as jnp
        import numpy as np
        D_MODEL = 128
        H = 16
        D_K = 64
        D_V = 64
        D_G = D_MODEL // H
        WAVE_LEN = 1000.0
        B = 8
        N = 64

        def box_relational_embedding(boxes, dim_g=D_G):
            x_min, y_min, x_max, y_max = jnp.split(boxes, 4, axis=-1)
            cx = (x_min + x_max) * 0.5
            cy = (y_min + y_max) * 0.5
            w = x_max - x_min + 1.0
            h = y_max - y_min + 1.0
            delta_x = jnp.log(jnp.clip(jnp.abs((cx - jnp.swapaxes(cx, 1, 2)) / w), 0.001, None))
            delta_y = jnp.log(jnp.clip(jnp.abs((cy - jnp.swapaxes(cy, 1, 2)) / h), 0.001, None))
            delta_w = jnp.log(w / jnp.swapaxes(w, 1, 2))
            delta_h = jnp.log(h / jnp.swapaxes(h, 1, 2))
            pos = jnp.stack([delta_x, delta_y, delta_w, delta_h], axis=-1)
            n_freq = dim_g // 8
            feat_range = jnp.arange(n_freq, dtype=jnp.float32)
            dim_mat = 1.0 / WAVE_LEN ** (feat_range / n_freq)
            mul = (100.0 * pos)[..., None] * dim_mat
            b, n = (pos.shape[0], pos.shape[1])
            mul = mul.reshape(b, n, n, 4 * n_freq)
            return jnp.concatenate([jnp.sin(mul), jnp.cos(mul)], axis=-1)
        b, nq, _ = queries.shape
        nk = keys.shape[1]
        emb = box_relational_embedding(boxes)
        g = jax.nn.relu(jnp.einsum('bnmd,hd->bhnm', emb, Wg) + bg[None, :, None, None])
        q = (queries @ Wq.T + bq).reshape(b, nq, H, D_K).transpose(0, 2, 1, 3)
        k = (keys @ Wk.T + bk).reshape(b, nk, H, D_K).transpose(0, 2, 1, 3)
        v = (values @ Wv.T + bv).reshape(b, nk, H, D_V).transpose(0, 2, 1, 3)
        a = jnp.einsum('bhqd,bhkd->bhqk', q, k) / jnp.sqrt(jnp.float32(D_K))
        mn = jax.nn.softmax(jnp.log(jnp.clip(g, 1e-06, None)) + a, axis=-1)
        out = jnp.einsum('bhqk,bhkd->bqhd', mn, v).reshape(b, nq, H * D_V)
        return out @ Wo.T + bo

    def _L0_ffn_ref(x, w1, b1, w2, b2):
        import jax, jax.numpy as jnp
        import numpy as np
        EPS = 1e-08

        def _ste(x, q):
            return x + jax.lax.stop_gradient(q - x)

        def quant_act_uint8(x):
            s = jax.lax.stop_gradient(jnp.maximum(jnp.max(x), EPS)) / 255.0
            q = jnp.clip(jnp.round(x / s), 0.0, 255.0) * s
            return (_ste(x, q), s)

        def quant_weight_int8_perchannel(w):
            s = jax.lax.stop_gradient(jnp.maximum(jnp.max(jnp.abs(w), axis=1, keepdims=True), EPS)) / 127.0
            q = jnp.clip(jnp.round(w / s), -128.0, 127.0) * s
            return (_ste(w, q), s[:, 0])

        def quant_bias_int32(b, s_in, s_w):
            s = jax.lax.stop_gradient(s_in * s_w)
            q = jnp.round(b / s) * s
            return _ste(b, q)

        def quant_linear(x, w, b):
            xq, s_in = quant_act_uint8(x)
            wq, s_w = quant_weight_int8_perchannel(w)
            bq = quant_bias_int32(b, s_in, s_w)
            return jnp.einsum('btd,fd->btf', xq, wq) + bq
        h = jax.nn.relu(quant_linear(x, w1, b1))
        return quant_linear(h, w2, b2)

    def _L1_xattn_ref(q, k, v, igate_kernel, igate_bias, fgate_kernel, fgate_bias):
        import jax, jax.numpy as jnp
        import numpy as np
        EMB = 128
        NH = 8
        HD = EMB // NH
        EPS = 1e-06

        def _mlstm_head(q, k, v, ig, fg):
            S, DH = q.shape
            log_fg = jax.nn.log_sigmoid(fg)
            cs = jnp.concatenate([jnp.zeros((1, 1), q.dtype), jnp.cumsum(log_fg, axis=0)], axis=0)
            fg_mat_full = cs - cs.T
            ltr = jnp.tril(jnp.ones((S, S), bool))
            log_fg_matrix = jnp.where(ltr, fg_mat_full[1:, 1:], -jnp.inf)
            log_D = log_fg_matrix + ig.T
            max_log_D = jnp.max(log_D, axis=-1, keepdims=True)
            D = jnp.exp(log_D - max_log_D)
            qk = q @ (k.T / jnp.sqrt(jnp.asarray(DH, q.dtype)))
            C = qk * D
            normalizer = jnp.maximum(jnp.abs(C.sum(-1, keepdims=True)), jnp.exp(-max_log_D))
            return C / (normalizer + EPS) @ v
        B, S, H = q.shape
        x = jnp.concatenate([q, k, v], axis=-1)
        ig = x @ igate_kernel + igate_bias
        fg = x @ fgate_kernel + fgate_bias
        qh = q.reshape(B, S, NH, HD).swapaxes(1, 2)
        kh = k.reshape(B, S, NH, HD).swapaxes(1, 2)
        vh = v.reshape(B, S, NH, HD).swapaxes(1, 2)
        igp = ig.swapaxes(1, 2)[..., None]
        fgp = fg.swapaxes(1, 2)[..., None]
        h = jax.vmap(jax.vmap(_mlstm_head))(qh, kh, vh, igp, fgp)
        hf = h.astype(jnp.float32)
        h = (hf * jax.lax.rsqrt(jnp.mean(jnp.square(hf), axis=-1, keepdims=True) + 1e-06)).astype(h.dtype)
        return h.swapaxes(1, 2).reshape(B, S, H)

    def _L1_ffn_ref(x, router_w, gate_w, up_w, down_w, shared_gate_w, shared_up_w, shared_down_w):
        import jax, jax.numpy as jnp
        import numpy as np
        B, S, H = (2, 256, 128)
        E, K, F_EXP, F_SHARED = (16, 2, 64, 128)
        b, s, h = x.shape
        T = b * s
        x_flat = x.reshape(T, h)
        shared_out = jax.nn.silu(x @ shared_gate_w) * (x @ shared_up_w) @ shared_down_w
        router_probs = jax.nn.softmax(x_flat @ router_w, axis=-1)
        topk_probs, topk_idx = jax.lax.top_k(router_probs, K)
        coeff = jnp.einsum('tk,tke->te', topk_probs, jax.nn.one_hot(topk_idx, E, dtype=x.dtype))

        def expert_step(acc, ws):
            g, u, d, c = ws
            inter = jax.nn.silu(x_flat @ g) * (x_flat @ u)
            return (acc + inter @ d * c[:, None], None)
        routed, _ = jax.lax.scan(expert_step, jnp.zeros((T, h), dtype=x.dtype), (gate_w, up_w, down_w, coeff.T))
        return routed.reshape(b, s, h) + shared_out
    x = x + _L0_xattn_ref(_layernorm(x, axis=-1), ctx_1024, ctx_1024, fside_BxSx4_0, L0_xattn_Wq, L0_xattn_bq, L0_xattn_Wk, L0_xattn_bk, L0_xattn_Wv, L0_xattn_bv, L0_xattn_Wo, L0_xattn_bo, L0_xattn_Wg, L0_xattn_bg)
    x = x + _L0_ffn_ref(_layernorm(x, axis=-1), L0_ffn_w1, L0_ffn_b1, L0_ffn_w2, L0_ffn_b2)
    x = x + _L1_xattn_ref(_layernorm(x, axis=-1), ctx_1024, ctx_1024, L1_xattn_igate_kernel, L1_xattn_igate_bias, L1_xattn_fgate_kernel, L1_xattn_fgate_bias)
    x = x + _L1_ffn_ref(_layernorm(x, axis=-1), L1_ffn_router_w, L1_ffn_gate_w, L1_ffn_up_w, L1_ffn_down_w, L1_ffn_shared_gate_w, L1_ffn_shared_up_w, L1_ffn_shared_down_w)
    return x

_drawn_inputs = setup_inputs


def setup_inputs(seed=0):
    import zlib

    import numpy as np

    out = dict(_drawn_inputs(seed))
    spreads = {'L0_xattn_bq': (0.0, 0.8),
     'L0_xattn_bk': (0.0, 2.0),
     'L0_xattn_bv': (0.0, 0.1),
     'L0_xattn_bo': (0.0, 0.1),
     'L0_xattn_bg': (0.0, 0.1)}
    factors = {'L0_xattn_Wq': 8.0,
     'L0_xattn_Wk': 8.0,
     'L0_ffn_b1': 4.983,
     'L0_ffn_b2': 4.744,
     'L1_xattn_igate_bias': 64.0,
     'L1_xattn_fgate_kernel': 3.946}
    for name, (base, spread) in spreads.items():
        noise = np.random.default_rng([zlib.crc32(name.encode()), seed]).standard_normal(out[name].shape)
        drawn = base * np.exp(spread * noise) if base else spread * noise
        out[name] = jnp.asarray(drawn.astype(out[name].dtype))
    for name, factor in factors.items():
        out[name] = (out[name] * factor).astype(out[name].dtype)
    return out
```

```python
from contextlib import ExitStack
import math

import concourse.bass as bass
from concourse import mybir

F32 = mybir.dt.float32
BF16 = mybir.dt.bfloat16
F16 = mybir.dt.float16
ALU = mybir.AluOpType
ACT = mybir.ActivationFunctionType
AX = mybir.AxisListType
RMAX = bass.bass_isa.ReduceOp.max

P = 128
B = 16
H0 = 16
DK = 64
HD = H0 * DK
CH = HD // P
HG = 4
UN = H0 // HG
NG = 8
GN = P // NG
F1 = 512
FC = F1 // P
H1 = 8
HW1 = P // H1
E1 = 16
FX = 64
EC = E1 * FX // P
LN_EPS = 1e-5
Q_EPS = 1e-8
ROUND = 1.5 * 2.0 ** 23
TURN = 6.2831845
COS_SHIFT = math.exp(math.pi / 2 / 100.0)
MASKED = -1e30
NSPLIT = 3
SROW = [0, 32, 64]
KB = SROW[-1] + 1


def after(eng, sem, value):
    if isinstance(value, int) and value <= 0:
        return
    eng.wait_ge(sem, value)


class Order:

    def __init__(self, eng, sem):
        self.eng, self.sem, self.n = eng, sem, 0

    def add(self, ins):
        self.n += 1
        ins.then_inc(self.sem, 1)

    def sync(self):
        self.eng.wait_ge(self.sem, self.n)

    def then(self, ins):
        self.add(ins)
        self.sync()


def over_batches(eng, slots):
    for b in range(2):
        slots(b, b)
    with eng.Fori(2, B - 2, 2) as i:
        for par in range(2):
            slots(i + par, par)
    for b in range(B - 2, B):
        slots(b, b % 2)


def known(b, value):
    return isinstance(b, int) and b == value


def build(nc, T, out, stage):
    ctx = ExitStack()
    with ctx:
        def sb(name, shape, dt=F32, where=ctx):
            return where.enter_context(nc.sbuf_tensor(name, shape, dt))

        x_sb = sb("x_sb", [P, B, P])
        ctx_sb = sb("ctx_sb", [P, B, P])
        ctxT = sb("ctxT", [P, B, P])
        ident = sb("ident", [P, P])
        identb = sb("identb", [P, P], BF16)
        bnst = sb("bnst", [P, B, 6])
        mv = sb("mv", [P, B, 2])
        rstd = sb("rstd", [P, B])
        for_attention = ExitStack()
        with for_attention:
            attention_phases(nc, T, sb, for_attention, x_sb, ctx_sb, ctxT, ident, identb, bnst, mv, rstd)
        if stage >= 2:
            with ExitStack() as scope:
                ffn_phase(nc, T, sb, scope, x_sb, ident, identb, bnst, mv, rstd)
        if stage >= 3:
            with ExitStack() as scope:
                mlstm_phase(nc, T, sb, scope, x_sb, ctx_sb, ctxT, ident, identb, bnst, mv, rstd)
        if stage >= 4:
            with ExitStack() as scope:
                moe_phase(nc, T, sb, scope, x_sb, ident, identb, bnst, mv, rstd, out)
        else:
            s_out = ctx.enter_context(nc.semaphore("s_out"))
            with nc.Block() as block:
                @block.sync
                def _(sp):
                    sp.dma_start(out.rearrange("b s d -> s b d"), x_sb[:]).then_inc(s_out, 16)
                    sp.wait_ge(s_out, 16)


def attention_phases(nc, T, sb, scope, x_sb, ctx_sb, ctxT, ident, identb, bnst, mv, rstd):
    emb = sb("emb", [P, B, NG, P], F32, scope)
    xnT = sb("xnT", [P, B, P], F32, scope)
    wT = sb("wT", [P, 4, CH, P], F32, scope)
    kron = sb("kron", [P, H0, GN], F32, scope)
    bias3 = sb("bias3", [KB, 3 * HD + P], BF16, scope)
    bg3 = sb("bg3", [KB, H0, P], BF16, scope)
    ones3 = sb("ones3", [KB, P], BF16, scope)
    with ExitStack() as prep:
        prepare_phase(nc, T, sb, prep, x_sb, ctx_sb, ctxT, ident, identb, bnst, mv, rstd,
                      emb, xnT, wT, kron, bias3, bg3, ones3)
    with ExitStack() as loop:
        attention_loop(nc, sb, loop, x_sb, ctxT, identb, ident, bnst, emb, xnT, wT, kron, bias3, bg3, ones3)


def prepare_phase(nc, T, sb, scope, x_sb, ctx_sb, ctxT, ident, identb, bnst, mv, rstd,
                  emb, xnT, wT, kron, bias3, bg3, ones3):
    NBIAS = 3 * HD + P

    def sem(name):
        return scope.enter_context(nc.semaphore(name))

    raw = sb("raw", [P, 4, CH, P], F32, scope)
    xn = sb("xn", [P, B, P], F32, scope)
    box = sb("box", [P, B, 4], F32, scope)
    fbeta = sb("fbeta", [P, B, 4], F32, scope)
    falpha = sb("falpha", [P, B, 4], F32, scope)
    fgamma = sb("fgamma", [P, B, 4], F32, scope)
    repeat = sb("repeat", [P, NG, P], F32, scope)
    kinds = sb("kinds", [P, B, P], F32, scope)
    kind4 = sb("kind4", [P, 4], F32, scope)
    delta16 = sb("delta16", [P, GN], F32, scope)
    picked = sb("picked", [P, NG, B, 4], F32, scope)
    alpha = sb("alpha", [P, B, NG], F32, scope)
    gamma = sb("gamma", [P, B, NG], F32, scope)
    shift = sb("shift", [P, 1], F32, scope)
    least = sb("least", [P, 1], F32, scope)
    wgp = sb("wgp", [P, H0], F32, scope)
    whole = sb("whole", [P, 2, NG, P], F32, scope)
    brow = sb("brow", [KB, NBIAS], F32, scope)
    bgrow = sb("bgrow", [KB, H0], F32, scope)
    part = sb("part", [KB, NBIAS], BF16, scope)
    bgpart = sb("bgpart", [KB, H0], BF16, scope)

    psT = scope.enter_context(nc.psum_tensor("psT", [P, 3, 4, P], F32))
    psB = scope.enter_context(nc.psum_tensor("psB", [P, B, P], F32))
    psA = scope.enter_context(nc.psum_tensor("psA", [P, NG, B, 4], F32))

    x_in, ctx_in, w_in, wo_in, box_in, wg_in, brow_in = (
        sem(n) for n in ("x_in", "ctx_in", "w_in", "wo_in", "box_in", "wg_in", "brow_in"))
    pool_order, dve_order, act_order = sem("pool_order"), sem("dve_order"), sem("act_order")
    ident_ready = sem("ident_ready")
    var_ready, std_ready, xn_ready = sem("var_ready"), sem("std_ready"), sem("xn_ready")
    boxes_ready, beta_psum, picked_psum, picked_read = (
        sem(n) for n in ("boxes_ready", "beta_psum", "picked_psum", "picked_read"))
    tr_psum = sem("tr_psum")
    tr_read = [sem("tr_read_act"), sem("tr_read_dve")]
    arg_step, arg_ready, log_ready = sem("arg_step"), sem("arg_ready"), sem("log_ready")
    cyc_step, cyc_ready = sem("cyc_step"), sem("cyc_ready")

    NTR = 4 + 4 + 8

    def transposed(n):
        if n < 4:
            return ctxT[:, 4 * n:4 * n + 4]
        if n < 8:
            return xnT[:, 4 * n - 16:4 * n - 12]
        k, half = divmod(n - 8, 2)
        return wT[:, k, 4 * half:4 * half + 4]

    with nc.Block() as block:
        @block.sync
        def _(sp):
            sp.dma_start(box[:], T["fside_BxSx4_0"].rearrange("b s c -> s b c")).then_inc(box_in, 16)
            sp.dma_start(ctx_sb[:], T["ctx_1024"].rearrange("b s d -> s b d")).then_inc(ctx_in, 16)
            for k, name in enumerate(("L0_xattn_Wq", "L0_xattn_Wk", "L0_xattn_Wv")):
                sp.dma_start(raw[:, k], T[name].rearrange("(c p) d -> p c d", p=P)).then_inc(w_in, 16)

        @block.scalar
        def _(act):
            act.dma_start(x_sb[:], T["x"].rearrange("b s d -> s b d")).then_inc(x_in, 16)
            act.dma_start(raw[:, 3], T["L0_xattn_Wo"].rearrange("p (c d) -> p c d", d=P)).then_inc(wo_in, 16)
            act.wait_ge(var_ready, 1)
            nc.scalar.activation(rstd[:], rstd[:], ACT.Sqrt).then_inc(std_ready, 1)
            for n in range(0, NTR, 2):
                act.wait_ge(tr_psum, n + 1)
                nc.scalar.copy(transposed(n), psT[:, n % 3]).then_inc(tr_read[0], 1)
            with nc.scalar.Fori(0, B) as b:
                act.wait_ge(arg_ready, b + 1)
                nc.scalar.activation(emb[:, b], emb[:, b], ACT.Ln).then_inc(log_ready, 1)
            with nc.scalar.Fori(0, B) as b:
                act.wait_ge(cyc_ready, b + 1)
                nc.scalar.activation(emb[:, b], emb[:, b], ACT.Sin, scale=TURN).then_inc(act_order, 1)

        @block.gpsimd
        def _(pool):
            with nc.allow_non_contiguous_dma(reason="2048 words of Wg, once"):
                for kind in range(8):
                    pool.dma_start(wgp[16 * kind:16 * kind + 16, :],
                                   T["L0_xattn_Wg"].rearrange("h k -> k h")[kind:kind + 1, :]
                                   .to_broadcast([16, H0])).then_inc(wg_in, 16)
            bias_names = ("L0_xattn_bq", "L0_xattn_bk", "L0_xattn_bv", "L0_xattn_bo")
            order = Order(pool, pool_order)
            at = 0
            for name in bias_names:
                n = T[name].shape[0]
                pool.dma_start(brow[:, at:at + n], T[name].rearrange("(o n) -> o n", o=1)
                               .to_broadcast([KB, n])).then_inc(brow_in, 16)
                at += n
            pool.dma_start(bgrow[:], T["L0_xattn_bg"].rearrange("(o n) -> o n", o=1)
                           .to_broadcast([KB, H0])).then_inc(brow_in, 16)
            order.add(nc.gpsimd.memset(ident[:], 0.0))
            order.add(nc.gpsimd.memset(identb[:], 0.0))
            order.add(nc.gpsimd.memset(falpha[:], 0.0))
            order.sync()
            nc.gpsimd.affine_select(out=ident[:], in_=ident[:], compare_op=ALU.not_equal, fill=1.0,
                                    base=0, pattern=[[-1, P]], channel_multiplier=1).then_inc(ident_ready, 1)
            nc.gpsimd.affine_select(out=identb[:], in_=identb[:], compare_op=ALU.not_equal, fill=1.0,
                                    base=0, pattern=[[-1, P]], channel_multiplier=1).then_inc(ident_ready, 1)

        @block.vector
        def _(dve):
            order = Order(dve, dve_order)
            dve.wait_ge(box_in, 16)
            dve.wait_ge(ident_ready, 2)
            v = nc.vector
            order.add(v.tensor_tensor(fbeta[:, :, 0:2], box[:, :, 0:2], box[:, :, 2:4], ALU.add))
            order.add(v.tensor_tensor(fgamma[:, :, 2:4], box[:, :, 2:4], box[:, :, 0:2], ALU.subtract))
            order.add(v.tensor_reduce(kind4[:], ident[:].rearrange("p (a t n) -> p t a n", a=2, t=4),
                                      AX.XY, ALU.add))
            order.add(v.tensor_reduce(delta16[:], ident[:].rearrange("p (d n) -> p n d", n=GN),
                                      AX.X, ALU.add))
            order.add(v.tensor_reduce(shift[:], ident[:, P // 2:], AX.X, ALU.add))
            order.sync()
            order.add(v.tensor_scalar(fbeta[:, :, 0:2], fbeta[:, :, 0:2], 0.5, None, ALU.mult))
            order.add(v.tensor_scalar(fgamma[:, :, 2:4], fgamma[:, :, 2:4], 1.0, None, ALU.add))
            order.add(v.tensor_scalar(shift[:], shift[:], COS_SHIFT - 1.0, 1.0, ALU.mult, ALU.add))
            order.add(v.tensor_tensor(least[:], kind4[:, 0:1], kind4[:, 1:2], ALU.add))
            order.sync()
            order.add(v.reciprocal(fgamma[:, :, 0:2], fgamma[:, :, 2:4]))
            order.add(v.tensor_copy(falpha[:, :, 0:2], fbeta[:, :, 0:2]))
            order.add(v.tensor_scalar(least[:], least[:], 1e-3, 1e-18, ALU.mult, ALU.add))
            order.sync()
            order.add(v.tensor_copy(fbeta[:, :, 2:4], fgamma[:, :, 0:2]))
            order.add(v.tensor_tensor(least[:], least[:], shift[:], ALU.mult))
            order.sync()
            order.add(v.tensor_copy(repeat[:].rearrange("p g (k n) -> p g k n", n=GN),
                                    ident[:].rearrange("p (g n) -> p g n", n=GN).unsqueeze(2)
                                    .to_broadcast([P, NG, NG, GN])))
            for half in range(2):
                order.add(v.tensor_copy(kinds[:, :, 64 * half:64 * half + 64]
                                        .rearrange("p b (t n) -> p b t n", n=GN),
                                        fbeta[:].unsqueeze(3).to_broadcast([P, B, 4, GN])))
            order.sync()
            v.engine_nop().then_inc(boxes_ready, 1)
            dve.wait_ge(x_in, 16)
            for b in range(B):
                order.add(v.bn_stats(bnst[:, b], x_sb[:, b]))
            order.sync()
            for b in range(B):
                order.add(v.bn_aggr(mv[:, b], bnst[:, b]))
            order.sync()
            v.tensor_scalar(rstd[:], mv[:, :, 1], LN_EPS, None, ALU.add).then_inc(var_ready, 1)
            for k, dest in enumerate((alpha, gamma)):
                dve.wait_ge(picked_psum, k + 1)
                order.then(v.tensor_tensor(picked[:].rearrange("p g b t -> p (g b) t"),
                                           psA[:].rearrange("p g b t -> p (g b) t"),
                                           kind4[:].unsqueeze(1).to_broadcast([P, NG * B, 4]), ALU.mult))
                order.then(v.tensor_reduce(dest[:].rearrange("p b g -> p g b"), picked[:], AX.X, ALU.add))
                v.engine_nop().then_inc(picked_read, 1)
            order.then(v.tensor_scalar(gamma[:], gamma[:], shift[:, 0:1], None, ALU.mult))
            dve.wait_ge(std_ready, 1)
            order.then(v.reciprocal(rstd[:], rstd[:]))
            for b in range(B):
                v.tensor_scalar(xn[:, b], x_sb[:, b], mv[:, b, 0:1], rstd[:, b:b + 1],
                                ALU.subtract, ALU.mult).then_inc(xn_ready, 1)
            for n in range(1, NTR, 2):
                dve.wait_ge(tr_psum, n + 1)
                v.tensor_copy(transposed(n), psT[:, n % 3]).then_inc(tr_read[1], 1)
            dve.wait_ge(wg_in, 16 * 8)
            order.add(v.tensor_tensor(kron[:], wgp[:].unsqueeze(2).to_broadcast([P, H0, GN]),
                                      delta16[:].unsqueeze(1).to_broadcast([P, H0, GN]), ALU.mult))
            dve.wait_ge(brow_in, 16 * 5)
            order.add(v.memset(bias3[:], 0.0))
            order.add(v.memset(bg3[:], 0.0))
            order.add(v.memset(ones3[:], 0.0))
            order.sync()
            for row in SROW:
                order.add(v.memset(ones3[row:row + 1, :], 1.0))
            for k, row in enumerate(SROW):
                order.add(v.tensor_copy(part[:], brow[:]))
                order.add(v.tensor_copy(bgpart[:], bgrow[:]))
                order.sync()
                order.add(v.tensor_copy(bias3[row:row + 1, :], part[row:row + 1, :]))
                order.add(v.tensor_copy(bg3[row:row + 1], bgpart[row:row + 1, :].unsqueeze(2)
                                        .to_broadcast([1, H0, P])))
                if k < NSPLIT - 1:
                    order.add(v.tensor_tensor(brow[:], brow[:], part[:], ALU.subtract))
                    order.add(v.tensor_tensor(bgrow[:], bgrow[:], bgpart[:], ALU.subtract))
                order.sync()
            dve.wait_ge(beta_psum, 1)
            with v.Fori(0, B) as b:
                v.tensor_tensor(emb[:, b], psB[:, b].unsqueeze(1).to_broadcast([P, NG, P]),
                                alpha[:, b].unsqueeze(2).to_broadcast([P, NG, P]),
                                ALU.subtract).then_inc(arg_step, 1)
                dve.wait_ge(arg_step, 3 * b + 1)
                v.tensor_tensor(emb[:, b], emb[:, b], gamma[:, b].unsqueeze(2).to_broadcast([P, NG, P]),
                                ALU.mult).then_inc(arg_step, 1)
                dve.wait_ge(arg_step, 3 * b + 2)
                bits = emb[:, b].bitcast(mybir.dt.int32)
                v.tensor_scalar(bits, bits, 0x7FFFFFFF, None, ALU.bitwise_and).then_inc(arg_step, 1)
                dve.wait_ge(arg_step, 3 * b + 3)
                v.tensor_scalar(emb[:, b], emb[:, b], least[:, 0:1], None, ALU.max).then_inc(arg_ready, 1)
            with v.Fori(0, B // 2) as i:
                for par in range(2):
                    b = 2 * i + par
                    dve.wait_ge(log_ready, b + 1)
                    v.tensor_scalar(whole[:, par], emb[:, b], 100.0 / (2 * math.pi), ROUND,
                                    ALU.mult, ALU.add).then_inc(cyc_step, 1)
                    dve.wait_ge(cyc_step, 2 * b + 1)
                    v.tensor_scalar(whole[:, par], whole[:, par], ROUND, None,
                                    ALU.subtract).then_inc(cyc_step, 1)
                    dve.wait_ge(cyc_step, 2 * b + 2)
                    v.scalar_tensor_tensor(out=emb[:, b].rearrange("p g m -> p (g m)"),
                                           in0=emb[:, b].rearrange("p g m -> p (g m)"),
                                           scalar=100.0 / (2 * math.pi),
                                           in1=whole[:, par].rearrange("p g m -> p (g m)"),
                                           op0=ALU.mult, op1=ALU.subtract).then_inc(cyc_ready, 1)

        @block.tensor
        def _(pe):
            pe.wait_ge(ident_ready, 2)
            pe.wait_ge(boxes_ready, 1)
            for k, src in enumerate((falpha, fgamma)):
                if k:
                    pe.wait_ge(picked_read, k)
                for g in range(NG):
                    mm = nc.tensor.matmul(psA[:, g], repeat[:, g], src[:], start=(g == 0), stop=(g == NG - 1),
                                          skip_group_check=True)
                mm.then_inc(picked_psum, 1)
            for b in range(B):
                mm = nc.tensor.matmul(psB[:, b], kinds[:, b], ident[:], start=True, stop=True)
            mm.then_inc(beta_psum, 1)

            def turn(n, blocks):
                if n >= 3:
                    pe.wait_ge(tr_read[(n - 3) % 2], (n - 3) // 2 + 1)
                for j, block_in in enumerate(blocks):
                    mm = nc.tensor.transpose(psT[:, n % 3, j], block_in, ident[:])
                mm.then_inc(tr_psum, 1)

            pe.wait_ge(ctx_in, 16)
            for n in range(4):
                turn(n, [ctx_sb[:, 4 * n + j] for j in range(4)])
            for n in range(4):
                pe.wait_ge(xn_ready, 4 * n + 4)
                turn(4 + n, [xn[:, 4 * n + j] for j in range(4)])
            pe.wait_ge(w_in, 16 * 3)
            pe.wait_ge(wo_in, 16)
            for n in range(8):
                turn(8 + n, [raw[:, n // 2, 4 * (n % 2) + j] for j in range(4)])


def attention_loop(nc, sb, scope, x_sb, ctxT, identb, ident, bnst, emb, xnT, wT, kron, bias3, bg3, ones3):
    def sem(name):
        return scope.enter_context(nc.semaphore(name))

    ctx_now = sb("ctx_now", [P, 2, P], F32, scope)
    emb_now = sb("emb_now", [P, 2, NG, P], F32, scope)
    qpad = sb("qpad", [P, 2, CH, 2, P], F32, scope)
    kT = sb("kT", [P, 2, CH, P], F32, scope)
    vx = sb("vx", [P, 2, H0, DK + 1], F32, scope)
    negmax = sb("negmax", [P, 2, HG], BF16, scope)
    prob = sb("prob", [P, 2, HG, P], F32, scope)
    gprob = sb("gprob", [P, 2, HG, P], F32, scope)
    rsum = sb("rsum", [P, 2, HG], F32, scope)
    att = sb("att", [P, 2, H0, DK], F32, scope)
    attT = sb("attT", [P, CH, P], F32, scope)

    def bank(name):
        return scope.enter_context(nc.psum_tensor(name, [P, HG, P], F32))

    psM, psG, psV = bank("psM"), bank("psG"), bank("psV")
    psS = [bank("psS0"), bank("psS1")]
    aux = [bank("aux0"), bank("aux1"), bank("aux2")]

    zeroed, staged, pool_gate = sem("zeroed"), sem("staged"), sem("pool_gate")
    qp_psum, q_ready, kp_psum, k_ready, vp_psum, v_ready = (
        sem(n) for n in ("qp_psum", "q_ready", "kp_psum", "k_ready", "vp_psum", "v_ready"))
    max_psum, negmax_ready, score_psum, prob_ready, geo_psum, gprob_ready = (
        sem(n) for n in ("max_psum", "negmax_ready", "score_psum", "prob_ready", "geo_psum", "gprob_ready"))
    pv_psum, rsum_ready, att_ready, attT_psum, attT_ready, op_psum, x1_ready, stat_ready = (
        sem(n) for n in ("pv_psum", "rsum_ready", "att_ready", "attT_psum", "attT_ready", "op_psum",
                         "x1_ready", "stat_ready"))

    with nc.Block() as block:
        @block.gpsimd
        def _(pool):
            nc.gpsimd.memset(qpad[:], 0.0).then_inc(zeroed, 1)
            nc.gpsimd.memset(vx[:], 1.0).then_inc(zeroed, 1)
            pool.wait_ge(zeroed, 2)

            def set_up():
                pool.sem_inc(pool_gate, 1)

            def stage(b, par):
                after(pool, vp_psum, 2 * b - 2)
                set_up()
                nc.gpsimd.tensor_copy(ctx_now[:, par], ctxT[:, b]).then_inc(staged, 1)
                after(pool, geo_psum, UN * (b - 1))
                set_up()
                nc.gpsimd.tensor_copy(emb_now[:, par], emb[:, b]).then_inc(staged, 1)

            stage(0, 0)

            def slots(b, par):
                if not known(b, B - 1):
                    stage(b + 1, 1 - par)

            over_batches(nc.gpsimd, slots)

        @block.tensor
        def _(pe):
            mm_ = nc.tensor.matmul

            def upper(a):
                return a.bitcast(BF16).rearrange("p (n two) -> p n two", two=2)[:, :, 1]

            def q_proj(b, par, half, into):
                mm_first = True
                for j in range(4):
                    c = 4 * half + j
                    mm_(aux[into][:, j], bias3[:, c * P:(c + 1) * P], ones3[:], start=mm_first, stop=False,
                        skip_group_check=True)
                    mm_first = False
                    mm = mm_(aux[into][:, j], wT[:, 0, c], xnT[:, b], start=False, stop=(j == 3),
                             skip_group_check=True)
                mm.then_inc(qp_psum, 1)

            def k_proj(b, par, half, into):
                for j in range(4):
                    c = 4 * half + j
                    mm_(aux[into][:, j], bias3[:, HD + c * P:HD + (c + 1) * P], ones3[:], start=(j == 0),
                        stop=False, skip_group_check=True)
                    mm = mm_(aux[into][:, j], wT[:, 1, c], ctxT[:, b], start=False, stop=(j == 3),
                             skip_group_check=True)
                mm.then_inc(kp_psum, 1)

            def v_proj(b, par, half, into):
                mm_(aux[into][:], ones3[:], bias3[:, 2 * HD + half * 512:2 * HD + half * 512 + 512],
                    start=True, stop=False)
                mm_(aux[into][:], ctx_now[:, par], wT[:, 2, 4 * half:4 * half + 4], start=False,
                    stop=True).then_inc(vp_psum, 1)

            def maxima(b, par, u):
                for j in range(HG):
                    h = HG * u + j
                    mm = mm_(psM[:, j], upper(qpad[:, par, h // 2, h % 2]), upper(kT[:, par, h // 2]),
                             start=True, stop=True)
                mm.then_inc(max_psum, 1)

            def scores(b, par, u):
                for c in range(HG // 2):
                    cc = (HG * u) // 2 + c
                    mm_(psS[u % 2][:, 2 * c:2 * c + 2], kT[:, par, cc], qpad[:, par, cc], start=(c == 0),
                        stop=False, skip_group_check=True)
                for j in range(HG):
                    mm = mm_(psS[u % 2][:, j], negmax[:, u % 2, j:j + 1].to_broadcast([P, P]), identb[:],
                             start=False, stop=(j == HG - 1), skip_group_check=True)
                mm.then_inc(score_psum, 1)

            def geometry(b, par, u):
                mm_(psG[:], ones3[:], bg3[:, HG * u:HG * u + HG], start=True, stop=False, skip_group_check=True)
                for g in range(NG):
                    mm = mm_(psG[:, :, GN * g:GN * g + GN], emb_now[:, par, g], kron[:, HG * u:HG * u + HG],
                             start=False, stop=(g == NG - 1), skip_group_check=True)
                mm.then_inc(geo_psum, 1)

            def pv(b, par, u):
                v = psV[:].rearrange("p a m -> p (a m)")
                for j in range(HG):
                    mm = mm_(v[:, j * (DK + 1):(j + 1) * (DK + 1)], gprob[:, u % 2, j], vx[:, par, HG * u + j],
                             start=(j == 0), stop=(j == HG - 1), skip_group_check=True)
                mm.then_inc(pv_psum, 1)

            def att_turn(b, par, half, into):
                for j in range(4):
                    c = 4 * half + j
                    mm = nc.tensor.transpose(aux[into][:, j], att[:, par, 2 * c:2 * c + 2], ident[:])
                mm.then_inc(attT_psum, 1)

            def out_proj(b, into):
                mm_(aux[into][:, 0], ones3[:], bias3[:, 3 * HD:3 * HD + P], start=True, stop=False)
                for c in range(CH):
                    mm = mm_(aux[into][:, 0], attT[:, c], wT[:, 3, c], start=False, stop=(c == CH - 1))
                mm.then_inc(op_psum, 1)

            def wait_pv(b, u):
                pe.wait_ge(v_ready, 2 * b + u // 2 + 1)
                pe.wait_ge(gprob_ready, UN * b + u + 1)
                after(pe, att_ready, UN * b + u)

            pe.wait_ge(zeroed, 2)
            q_proj(0, 0, 0, 2)
            q_proj(0, 0, 1, 0)
            k_proj(0, 0, 0, 1)
            pe.wait_ge(q_ready, 2)
            k_proj(0, 0, 1, 2)
            pe.wait_ge(q_ready, 4)
            pe.wait_ge(k_ready, 2)
            maxima(0, 0, 0)

            def slots(b, par):
                first, last = known(b, 0), known(b, B - 1)
                nxt = 1 - par
                for u in range(UN):
                    pe.wait_ge(negmax_ready, UN * b + u + 1)
                    after(pe, prob_ready, UN * b + u - 1)
                    if u == 0:
                        pe.wait_ge(k_ready, 2 * b + 2)
                        pe.wait_ge(q_ready, 4 * b + 4)
                    scores(b, par, u)
                    if u < UN - 1:
                        maxima(b, par, u + 1)
                    elif not last:
                        pe.wait_ge(q_ready, 4 * (b + 1) + 4)
                        pe.wait_ge(k_ready, 2 * (b + 1) + 2)
                        maxima(b + 1, nxt, 0)
                    if u == 0:
                        pe.wait_ge(staged, 2 * b + 2)
                    after(pe, gprob_ready, UN * b + u)
                    geometry(b, par, u)
                    if u > 0:
                        wait_pv(b, u - 1)
                        pv(b, par, u - 1)
                    elif not first:
                        wait_pv(b - 1, UN - 1)
                        pv(b - 1, nxt, UN - 1)
                    if u == 0:
                        after(pe, x1_ready, b - 1)
                        v_proj(b, par, 0, 0)
                        pe.wait_ge(k_ready, 2 * b + 1)
                        v_proj(b, par, 1, 1)
                    if u == 1:
                        if not first:
                            pe.wait_ge(att_ready, UN * b)
                            pe.wait_ge(v_ready, 2 * b + 1)
                            att_turn(b - 1, nxt, 0, 0)
                            pe.wait_ge(v_ready, 2 * b + 2)
                            att_turn(b - 1, nxt, 1, 1)
                        if not last:
                            pe.wait_ge(k_ready, 2 * b + 2)
                            q_proj(b + 1, nxt, 0, 2)
                    if u == 2 and not last:
                        pe.wait_ge(v_ready, 2 * b + 2)
                        after(pe, attT_ready, 2 * b)
                        q_proj(b + 1, nxt, 1, 0)
                        k_proj(b + 1, nxt, 0, 1)
                        pe.wait_ge(q_ready, 4 * (b + 1) + 2)
                        k_proj(b + 1, nxt, 1, 2)
                    if u == 3 and not first:
                        after(pe, attT_ready, 2 * b)
                        if not last:
                            pe.wait_ge(q_ready, 4 * (b + 1) + 4)
                        out_proj(b - 1, 0)

            over_batches(nc.tensor, slots)
            wait_pv(B - 1, UN - 1)
            pv(B - 1, (B - 1) % 2, UN - 1)
            pe.wait_ge(att_ready, UN * B)
            pe.wait_ge(x1_ready, B - 1)
            for half in range(2):
                att_turn(B - 1, (B - 1) % 2, half, half)
            pe.wait_ge(attT_ready, 2 * B)
            out_proj(B - 1, 0)

        @block.scalar
        def _(act):
            def q_out(b, par, half, frm):
                act.wait_ge(qp_psum, 2 * b + half + 1)
                for odd in range(2):
                    rows = slice(64 * odd, 64 * odd + 64)
                    nc.scalar.copy(qpad[rows, par, 4 * half:4 * half + 4, odd],
                                   aux[frm][rows]).then_inc(q_ready, 1)

            def k_out(b, par, half, frm):
                act.wait_ge(kp_psum, 2 * b + half + 1)
                nc.scalar.copy(kT[:, par, 4 * half:4 * half + 4], aux[frm][:]).then_inc(k_ready, 1)

            def attT_out(b, half):
                act.wait_ge(attT_psum, 2 * b + half + 1)
                after(act, op_psum, b)
                nc.scalar.copy(attT[:, 4 * half:4 * half + 4], aux[half][:]).then_inc(attT_ready, 1)

            act.wait_ge(zeroed, 2)
            q_out(0, 0, 0, 2)
            q_out(0, 0, 1, 0)
            k_out(0, 0, 0, 1)
            k_out(0, 0, 1, 2)

            def slots(b, par):
                first, last = known(b, 0), known(b, B - 1)
                for u in range(UN):
                    act.wait_ge(score_psum, UN * b + u + 1)
                    after(act, gprob_ready, UN * b + u - 1)
                    nc.scalar.activation(prob[:, u % 2], psS[u % 2][:], ACT.Exp,
                                         scale=DK ** -0.5).then_inc(prob_ready, 1)
                    if u == 1:
                        if not first:
                            attT_out(b - 1, 0)
                            attT_out(b - 1, 1)
                        if not last:
                            after(act, score_psum, UN * b)
                            q_out(b + 1, 1 - par, 0, 2)
                    if u == 2 and not last:
                        q_out(b + 1, 1 - par, 1, 0)
                        k_out(b + 1, 1 - par, 0, 1)
                        k_out(b + 1, 1 - par, 1, 2)

            over_batches(nc.scalar, slots)
            attT_out(B - 1, 0)
            attT_out(B - 1, 1)

        @block.vector
        def _(dve):
            v = nc.vector

            def neg_max(b, u):
                dve.wait_ge(max_psum, UN * b + u + 1)
                after(dve, score_psum, UN * b + u - 1)
                v.tensor_reduce(negmax[:, u % 2], psM[:], AX.X, ALU.max, negate=True).then_inc(negmax_ready, 1)

            def weigh(b, u):
                dve.wait_ge(prob_ready, UN * b + u + 1)
                dve.wait_ge(geo_psum, UN * b + u + 1)
                after(dve, pv_psum, UN * b + u - 1)
                v.scalar_tensor_tensor(out=gprob[:, u % 2].rearrange("p h q -> p (h q)"),
                                       in0=psG[:].rearrange("p h q -> p (h q)"), scalar=1e-6,
                                       in1=prob[:, u % 2].rearrange("p h q -> p (h q)"),
                                       op0=ALU.max, op1=ALU.mult).then_inc(gprob_ready, 1)

            def normalise(b, par, u):
                dve.wait_ge(pv_psum, UN * b + u + 1)
                got = psV[:].rearrange("p a m -> p (a m)")[:, 0:HG * (DK + 1)].rearrange("p (h e) -> p h e", h=HG)
                v.reciprocal(rsum[:, u % 2], got[:, :, DK]).then_inc(rsum_ready, 1)
                dve.wait_ge(rsum_ready, UN * b + u + 1)
                after(dve, attT_psum, 2 * b - 2)
                v.tensor_tensor(att[:, par, HG * u:HG * u + HG], got[:, :, 0:DK],
                                rsum[:, u % 2].unsqueeze(2).to_broadcast([P, HG, DK]),
                                ALU.mult).then_inc(att_ready, 1)

            def v_out(b, par, half):
                dve.wait_ge(vp_psum, 2 * b + half + 1)
                v.tensor_copy(vx[:, par, 8 * half:8 * half + 8, 0:DK],
                              aux[half][:].rearrange("p a m -> p (a m)").rearrange("p (h e) -> p h e", e=DK)
                              ).then_inc(v_ready, 1)

            def residual(b):
                dve.wait_ge(op_psum, b + 1)
                v.tensor_tensor(x_sb[:, b], x_sb[:, b], aux[0][:, 0], ALU.add).then_inc(x1_ready, 1)
                dve.wait_ge(x1_ready, b + 1)
                v.bn_stats(bnst[:, b], x_sb[:, b]).then_inc(stat_ready, 1)

            dve.wait_ge(zeroed, 2)
            neg_max(0, 0)

            def slots(b, par):
                first, last = known(b, 0), known(b, B - 1)
                for u in range(UN):
                    if u < UN - 1:
                        neg_max(b, u + 1)
                    elif not last:
                        neg_max(b + 1, 0)
                    weigh(b, u)
                    if u > 0:
                        normalise(b, par, u - 1)
                    elif not first:
                        normalise(b - 1, 1 - par, UN - 1)
                    if u == 0:
                        v_out(b, par, 0)
                        v_out(b, par, 1)
                    if u == 3 and not first:
                        residual(b - 1)

            over_batches(nc.vector, slots)
            normalise(B - 1, (B - 1) % 2, UN - 1)
            residual(B - 1)


def layernorm_all(v, act_sem_pair, order, dve, x_sb, bnst, mv, rstd, eps=LN_EPS):
    asked, given = act_sem_pair
    for b in range(B):
        order.add(v.bn_aggr(mv[:, b], bnst[:, b]))
    order.sync()
    v.tensor_scalar(rstd[:], mv[:, :, 1], eps, None, ALU.add).then_inc(asked, 1)
    dve.wait_ge(given, 1)
    order.then(v.reciprocal(rstd[:], rstd[:]))


def ffn_phase(nc, T, sb, scope, x_sb, ident, identb, bnst, mv, rstd):
    TG = 4
    NT = B // TG

    def sem(name):
        return scope.enter_context(nc.semaphore(name))

    w1 = sb("w1", [P, FC, P], F32, scope)
    w2 = sb("w2", [P, FC, P], F32, scope)
    q1 = sb("q1", [P, FC, P], BF16, scope)
    q2 = sb("q2", [P, FC, P], BF16, scope)
    q1T = sb("q1T", [P, FC, P], BF16, scope)
    q2T = sb("q2T", [P, FC, P], BF16, scope)
    b1 = sb("b1", [P, FC], F32, scope)
    b2 = sb("b2", [P, 1], F32, scope)
    ws = sb("ws", [P, FC + 1], F32, scope)
    wr = sb("wr", [P, FC + 1], F32, scope)
    sc1 = sb("sc1", [P, FC], F32, scope)
    rc1 = sb("rc1", [P, FC], F32, scope)
    sc2 = sb("sc2", [P, 2], F32, scope)
    xn = sb("xn2", [P, B, P], F32, scope)
    xq = sb("xq", [P, B, P], BF16, scope)
    xf = sb("xf", [P, 2, TG * P], F32, scope)
    hid = sb("hid", [P, NT, FC, TG * P], F32, scope)
    hq = sb("hq", [P, NT, FC, TG * P], BF16, scope)
    hmax = sb("hmax", [P, NT * FC], F32, scope)
    top = sb("top", [P, 2], F32, scope)
    topall = sb("topall", [P, 2], F32, scope)
    inv = sb("inv", [P, 2], F32, scope)
    step = sb("step", [P, 2], F32, scope)
    row2 = sb("row2", [P, 2, P], F32, scope)

    psT = [scope.enter_context(nc.psum_tensor(f"psFT{i}", [P, TG, P], F32)) for i in range(2)]
    psW = scope.enter_context(nc.psum_tensor("psFW", [P, FC, 2 * P], BF16))
    psH = [scope.enter_context(nc.psum_tensor(f"psFH{i}", [P, TG * P], F32)) for i in range(2)]
    psY = [scope.enter_context(nc.psum_tensor(f"psFY{i}", [P, TG, P], F32)) for i in range(2)]
    psR = scope.enter_context(nc.psum_tensor("psFR", [P, 2, P], F32))

    w_in, dve_order, var_ready, std_ready, xn_ready = (
        sem(n) for n in ("ffn_w_in", "ffn_dve_order", "ffn_var_ready", "ffn_std_ready", "ffn_xn_ready"))
    top_ready, topall_ready, inv_ready, q_ready, qT_psum, qT_ready = (
        sem(n) for n in ("ffn_top_ready", "ffn_topall_ready", "ffn_inv_ready", "ffn_q_ready", "ffn_qT_psum",
                         "ffn_qT_ready"))
    xT_psum, xf_ready, xq_ready, h_psum, hid_ready, sc1_ready = (
        sem(n) for n in ("ffn_xT_psum", "ffn_xf_ready", "ffn_xq_ready", "ffn_h_psum", "ffn_hid_ready",
                         "ffn_sc1_ready"))
    hr_ready, hq_ready, y_psum, sc2_ready, row_psum, y_done = (
        sem(n) for n in ("ffn_hr_ready", "ffn_hq_ready", "ffn_y_psum", "ffn_sc2_ready", "ffn_row_psum",
                         "ffn_y_done"))

    with nc.Block() as block:
        @block.sync
        def _(sp):
            sp.dma_start(w1[:], T["L0_ffn_w1"].rearrange("(c p) d -> p c d", p=P)).then_inc(w_in, 16)
            sp.dma_start(w2[:], T["L0_ffn_w2"].rearrange("p (c d) -> p c d", d=P)).then_inc(w_in, 16)
            with nc.allow_non_contiguous_dma(reason="640 words of biases, once"):
                sp.dma_start(b1[:], T["L0_ffn_b1"].rearrange("(c p) -> p c", p=P)).then_inc(w_in, 16)
                sp.dma_start(b2[:], T["L0_ffn_b2"].rearrange("(p o) -> p o", o=1)).then_inc(w_in, 16)

        @block.gpsimd
        def _(pool):
            for k in range(2):
                pool.wait_ge(top_ready, k + 1)
                nc.gpsimd.partition_all_reduce(topall[:, k:k + 1], top[:, k:k + 1], P, RMAX).then_inc(topall_ready, 1)

        @block.scalar
        def _(act):
            act.wait_ge(var_ready, 1)
            nc.scalar.activation(rstd[:], rstd[:], ACT.Sqrt).then_inc(std_ready, 1)
            act.wait_ge(qT_psum, 1)
            nc.scalar.copy(q1T[:], psW[:, :, 0:P]).then_inc(qT_ready, 1)
            act.wait_ge(qT_psum, 2)
            nc.scalar.copy(q2T[:], psW[:, :, 0:P]).then_inc(qT_ready, 1)
            act.wait_ge(inv_ready, 1)
            for t in range(NT):
                act.wait_ge(xT_psum, t + 1)
                if t >= 2:
                    act.wait_ge(xq_ready, t - 1)
                nc.scalar.activation(xf[:, t % 2], psT[t % 2][:].rearrange("p b d -> p (b d)"), ACT.Relu,
                                     scale=inv[:, 0:1]).then_inc(xf_ready, 1)
            act.wait_ge(sc1_ready, 1)
            for t in range(NT):
                for c in range(FC):
                    n = FC * t + c
                    act.wait_ge(h_psum, n + 1)
                    nc.scalar.activation(hid[:, t, c], psH[n % 2][:], ACT.Relu, bias=b1[:, c:c + 1],
                                         scale=sc1[:, c:c + 1]).then_inc(hid_ready, 1)

        @block.vector
        def _(dve):
            v = nc.vector
            order = Order(dve, dve_order)
            layernorm_all(v, (var_ready, std_ready), order, dve, x_sb, bnst, mv, rstd)
            for b in range(B):
                v.tensor_scalar(xn[:, b], x_sb[:, b], mv[:, b, 0:1], rstd[:, b:b + 1],
                                ALU.subtract, ALU.mult).then_inc(xn_ready, 1)
            dve.wait_ge(xn_ready, B)
            v.tensor_reduce(top[:, 0:1], xn[:], AX.XY, ALU.max).then_inc(top_ready, 1)

            dve.wait_ge(w_in, 16 * 4)
            order.add(v.tensor_reduce(ws[:, 0:FC], w1[:], AX.X, ALU.max, apply_absolute_value=True))
            order.add(v.tensor_reduce(ws[:, FC:], w2[:], AX.XY, ALU.max, apply_absolute_value=True))
            order.sync()
            order.then(v.tensor_scalar(ws[:], ws[:], Q_EPS, 1.0 / 127.0, ALU.max, ALU.mult))
            order.then(v.reciprocal(wr[:], ws[:]))
            for c in range(FC):
                order.add(v.tensor_scalar(w1[:, c], w1[:, c], wr[:, c:c + 1], ROUND, ALU.mult, ALU.add))
            order.add(v.tensor_scalar(w2[:], w2[:], wr[:, FC:], ROUND, ALU.mult, ALU.add))
            order.sync()
            for w in (w1, w2):
                order.add(v.tensor_scalar(w[:], w[:], ROUND, -128.0, ALU.subtract, ALU.max))
            order.sync()
            for w, q in ((w1, q1), (w2, q2)):
                v.tensor_scalar(q[:], w[:], 127.0, None, ALU.min).then_inc(q_ready, 1)

            def scales(k):
                dve.wait_ge(topall_ready, k + 1)
                order.then(v.tensor_scalar(step[:, k:k + 1], topall[:, k:k + 1], Q_EPS, 1.0 / 255.0,
                                           ALU.max, ALU.mult))
                order.then(v.reciprocal(inv[:, k:k + 1], step[:, k:k + 1]))
                v.engine_nop().then_inc(inv_ready, 1)

            def quant_bias(bias, sc, rc):
                order.then(v.reciprocal(rc, sc))
                order.then(v.tensor_tensor(bias, bias, rc, ALU.mult))
                order.then(v.tensor_scalar(bias, bias, ROUND, None, ALU.add))
                order.then(v.tensor_scalar(bias, bias, ROUND, None, ALU.subtract))
                order.then(v.tensor_tensor(bias, bias, sc, ALU.mult))

            scales(0)
            order.then(v.tensor_scalar(sc1[:], ws[:, 0:FC], step[:, 0:1], None, ALU.mult))
            quant_bias(b1[:], sc1[:], rc1[:])
            v.engine_nop().then_inc(sc1_ready, 1)
            for t in range(NT):
                dve.wait_ge(xf_ready, t + 1)
                order.then(v.tensor_scalar(xf[:, t % 2], xf[:, t % 2], 255.0, ROUND, ALU.min, ALU.add))
                v.tensor_scalar(xq[:, TG * t:TG * t + TG].rearrange("p b d -> p (b d)"), xf[:, t % 2], ROUND,
                                None, ALU.subtract).then_inc(xq_ready, 1)
            for n in range(NT * FC):
                dve.wait_ge(hid_ready, n + 1)
                order.add(v.tensor_reduce(hmax[:, n:n + 1], hid[:, n // FC, n % FC], AX.X, ALU.max))
            order.sync()
            v.tensor_reduce(top[:, 1:2], hmax[:], AX.X, ALU.max).then_inc(top_ready, 1)
            scales(1)
            order.then(v.tensor_scalar(sc2[:, 0:1], ws[:, FC:], step[:, 1:2], None, ALU.mult))
            order.then(v.tensor_copy(sc2[:, 1:2], b2[:]))
            quant_bias(sc2[:, 1:2], sc2[:, 0:1], rc1[:, 0:1])
            v.engine_nop().then_inc(sc2_ready, 1)
            for t in range(NT):
                for c in range(FC):
                    v.tensor_scalar(hid[:, t, c], hid[:, t, c], inv[:, 1:2], ROUND, ALU.mult,
                                    ALU.add).then_inc(hr_ready, 1)
                dve.wait_ge(hr_ready, FC * (t + 1))
                v.tensor_scalar(hq[:, t], hid[:, t], ROUND, 255.0, ALU.subtract, ALU.min).then_inc(hq_ready, 1)
            dve.wait_ge(row_psum, 1)
            order.then(v.tensor_copy(row2[:], psR[:]))
            for t in range(NT):
                xs = x_sb[:, TG * t:TG * t + TG]
                dve.wait_ge(y_psum, t + 1)
                order.add(v.tensor_tensor(xn[:, TG * t:TG * t + TG], psY[t % 2][:],
                                          row2[:, 0].unsqueeze(1).to_broadcast([P, TG, P]), ALU.mult))
                order.add(v.tensor_tensor(xs, xs, row2[:, 1].unsqueeze(1).to_broadcast([P, TG, P]), ALU.add))
                order.sync()
                v.tensor_tensor(xs, xs, xn[:, TG * t:TG * t + TG], ALU.add).then_inc(y_done, 1)
                dve.wait_ge(y_done, t + 1)
                for b in range(TG * t, TG * t + TG):
                    order.add(v.bn_stats(bnst[:, b], x_sb[:, b]))

        @block.tensor
        def _(pe):
            mm_ = nc.tensor.matmul
            for k, q in enumerate((q1, q2)):
                pe.wait_ge(q_ready, k + 1)
                if k:
                    pe.wait_ge(qT_ready, k)
                for c in range(FC):
                    mm = nc.tensor.transpose(psW[:, c, 0:P], q[:, c], identb[:])
                mm.then_inc(qT_psum, 1)
            for t in range(NT):
                pe.wait_ge(xn_ready, TG * (t + 1))
                if t >= 2:
                    pe.wait_ge(xf_ready, t - 1)
                for j in range(TG):
                    mm = nc.tensor.transpose(psT[t % 2][:, j], xn[:, TG * t + j], ident[:])
                mm.then_inc(xT_psum, 1)
            pe.wait_ge(qT_ready, 2)
            for t in range(NT):
                pe.wait_ge(xq_ready, t + 1)
                for c in range(FC):
                    n = FC * t + c
                    if n >= 2:
                        pe.wait_ge(hid_ready, n - 1)
                    mm_(psH[n % 2][:], q1T[:, c], xq[:, TG * t:TG * t + TG], start=True,
                        stop=True).then_inc(h_psum, 1)
            pe.wait_ge(sc2_ready, 1)
            for k in range(2):
                mm = mm_(psR[:, k], sc2[:, k:k + 1].to_broadcast([P, P]), ident[:], start=True, stop=True)
            mm.then_inc(row_psum, 1)
            for t in range(NT):
                pe.wait_ge(hq_ready, t + 1)
                if t >= 2:
                    pe.wait_ge(y_done, t - 1)
                for j in range(TG):
                    for c in range(FC):
                        mm = mm_(psY[t % 2][:, j], hq[:, t, c, j * P:(j + 1) * P], q2T[:, c],
                                 start=(c == 0), stop=(c == FC - 1))
                mm.then_inc(y_psum, 1)


def mlstm_phase(nc, T, sb, scope, x_sb, ctx_sb, ctxT, ident, identb, bnst, mv, rstd):
    G = 2
    GH = H1 // G
    VW = HW1 + 1

    def sem(name):
        return scope.enter_context(nc.semaphore(name))

    xn = sb("xn3", [P, B, P], F32, scope)
    qT = sb("qT3", [P, B, P], F32, scope)
    gk = sb("gk", [P, 3, 2, H1], F32, scope)
    gb = sb("gb", [H1, 2], F32, scope)
    gate = sb("gate", [H1, 2, B * P], F32, scope)
    low = sb("low", [H1, B * P], F32, scope)
    soft = sb("soft", [H1, B * P], F32, scope)
    keep = sb("keep", [H1, B, P], F32, scope)
    floor = sb("floor", [H1, B, P], F32, scope)
    csum = sb("csum", [H1, B * P], F32, scope)
    gain = sb("gain", [H1, B, P], F32, scope)
    peak = sb("peak", [H1, B, P], F32, scope)
    guard = sb("guard", [H1, B * P], F32, scope)
    eguard = sb("eguard", [P, B, H1], F32, scope)
    negone = sb("negone", [H1, H1, P], F32, scope)
    argl = sb("argl", [SROW[1] + H1, 2, P], F32, scope)
    argr = sb("argr", [SROW[1] + H1, 2, H1, P], F32, scope)
    future = sb("future", [P, P], BF16, scope)
    headm = sb("headm", [P, H1], F32, scope)
    ctx_now = sb("ctx_now3", [P, 2, P], F32, scope)
    qm = sb("qm", [P, 2, H1, P], F32, scope)
    v1 = sb("v1", [P, B, H1, VW], F32, scope)
    decay = sb("decay", [P, G, GH, P], F32, scope)
    cmat = sb("cmat", [P, 2, H1, P], F32, scope)
    num = sb("num", [P, B, H1, VW], F32, scope)
    square = sb("square", [P, 2, H1, HW1], F32, scope)
    msq = sb("msq", [P, B, H1], F32, scope)
    factor = sb("factor", [P, B, H1], F32, scope)
    tmp = sb("tmp3", [P, B, H1], F32, scope)

    with ExitStack() as prep, nc.Block() as block:
        psT = [prep.enter_context(nc.psum_tensor(f"psMT{i}", [P, 4, P], F32)) for i in range(2)]
        psI = [prep.enter_context(nc.psum_tensor(f"psMI{i}", [P, 4 * P], F32)) for i in range(2)]
        psE = prep.enter_context(nc.psum_tensor("psME", [P, B, H1], F32))
        w_in, dve_order, pool_order, var_ready, std_ready, xn_ready = (
            sem(n) for n in ("ml_w_in", "ml_dve_order", "ml_pool_order", "ml_var_ready", "ml_std_ready",
                             "ml_xn_ready"))
        qT_psum, qT_ready, gate_psum, gate_ready, abs_ready, soft_ready, guard_ready, guard_psum, eg_ready = (
            sem(n) for n in ("ml_qT_psum", "ml_qT_ready", "ml_gate_psum", "ml_gate_ready", "ml_abs_ready",
                             "ml_soft_ready", "ml_guard_ready", "ml_guard_psum", "ml_eg_ready"))

        @block.sync
        def _(sp):
            for k, name in enumerate(("L1_xattn_igate", "L1_xattn_fgate")):
                with nc.allow_non_contiguous_dma(reason="small gate weights, once"):
                    sp.dma_start(gk[:, :, k], T[name + "_kernel"].rearrange("(s p) h -> p s h", p=P)).then_inc(w_in, 16)
                    sp.dma_start(gb[:, k:k + 1], T[name + "_bias"].rearrange("(h o) -> h o", o=1)).then_inc(w_in, 16)

        @block.gpsimd
        def _(pool):
            order = Order(pool, pool_order)
            order.add(nc.gpsimd.memset(negone[:], 0.0))
            order.add(nc.gpsimd.memset(argl[:], 1.0))
            order.add(nc.gpsimd.memset(argr[:], 0.0))
            order.add(nc.gpsimd.memset(future[:], MASKED))
            order.add(nc.gpsimd.memset(headm[:], HW1 ** -0.5))
            order.add(nc.gpsimd.memset(v1[:], 1.0))
            order.sync()
            hh = [[-1, H1], [0, P]]
            order.add(nc.gpsimd.affine_select(out=negone[:], in_=negone[:], compare_op=ALU.not_equal,
                                              fill=-1.0, base=0, pattern=hh, channel_multiplier=1))
            for k in range(2):
                order.add(nc.gpsimd.affine_select(out=argr[0:H1, k], in_=argr[0:H1, k],
                                                  compare_op=ALU.not_equal, fill=1.0, base=0,
                                                  pattern=hh, channel_multiplier=1))
            order.add(nc.gpsimd.affine_select(out=future[:], in_=future[:], compare_op=ALU.is_gt, fill=0.0,
                                              base=0, pattern=[[-1, P]], channel_multiplier=1))
            order.add(nc.gpsimd.affine_select(out=headm[:], in_=headm[:], compare_op=ALU.is_ge, fill=0.0,
                                              base=0, pattern=[[-HW1, H1]], channel_multiplier=1))
            order.sync()
            order.add(nc.gpsimd.affine_select(out=headm[:], in_=headm[:], compare_op=ALU.is_ge, fill=0.0,
                                              base=HW1 - 1, pattern=[[HW1, H1]], channel_multiplier=-1))
            order.add(nc.gpsimd.tensor_copy(v1[:, :, :, 0:HW1],
                                            ctx_sb[:].rearrange("p b (h e) -> p b h e", h=H1)))

        @block.scalar
        def _(act):
            act.wait_ge(var_ready, 1)
            nc.scalar.activation(rstd[:], rstd[:], ACT.Sqrt).then_inc(std_ready, 1)
            for t in range(4):
                act.wait_ge(qT_psum, t + 1)
                nc.scalar.copy(qT[:, 4 * t:4 * t + 4], psT[t % 2][:]).then_inc(qT_ready, 1)
            act.wait_ge(abs_ready, 1)
            nc.scalar.activation(soft[:], soft[:], ACT.Exp, scale=-1.0).then_inc(soft_ready, 1)
            act.wait_ge(soft_ready, 1)
            nc.scalar.activation(soft[:], soft[:], ACT.Ln, bias=1.0).then_inc(soft_ready, 1)
            act.wait_ge(guard_psum, 1)
            nc.scalar.activation(eguard[:], psE[:], ACT.Exp, scale=-1.0).then_inc(eg_ready, 1)

        @block.vector
        def _(dve):
            v = nc.vector
            order = Order(dve, dve_order)
            order.add(v.memset(keep[:], 1.0))
            layernorm_all(v, (var_ready, std_ready), order, dve, x_sb, bnst, mv, rstd)
            for b in range(B):
                v.tensor_scalar(xn[:, b], x_sb[:, b], mv[:, b, 0:1], rstd[:, b:b + 1],
                                ALU.subtract, ALU.mult).then_inc(xn_ready, 1)
            order.add(v.memset(keep[:, :, 0:1], 0.0))
            order.sync()
            order.add(v.tensor_scalar(floor[:], keep[:], 1.0, -MASKED, ALU.subtract, ALU.mult))
            dve.wait_ge(w_in, 16 * 4)
            for n in range(8):
                t, k = divmod(n, 2)
                dve.wait_ge(gate_psum, n + 1)
                v.tensor_scalar(gate[:, k, 4 * P * t:4 * P * (t + 1)], psI[k][0:H1, :], gb[:, k:k + 1], None,
                                ALU.add).then_inc(gate_ready, 1)
            dve.wait_ge(gate_ready, 8)
            order.then(v.tensor_scalar(low[:], gate[:, 1], 0.0, None, ALU.min))
            v.scalar_tensor_tensor(out=soft[:], in0=low[:], scalar=-2.0, in1=gate[:, 1], op0=ALU.mult,
                                   op1=ALU.add).then_inc(abs_ready, 1)
            dve.wait_ge(soft_ready, 2)
            order.then(v.tensor_tensor(low[:], low[:], soft[:], ALU.subtract))
            order.then(v.tensor_tensor_scan(csum[:], keep[:].rearrange("h b i -> h (b i)"), low[:], 0.0,
                                            ALU.mult, ALU.add))
            order.then(v.tensor_tensor(gain[:].rearrange("h b i -> h (b i)"), gate[:, 0], csum[:], ALU.subtract))
            order.then(v.tensor_tensor_scan(peak[:].rearrange("h b i -> h (b i)"),
                                            floor[:].rearrange("h b i -> h (b i)"),
                                            gain[:].rearrange("h b i -> h (b i)"), MASKED, ALU.add, ALU.max))
            v.tensor_tensor(guard[:], csum[:], peak[:].rearrange("h b i -> h (b i)"),
                            ALU.add).then_inc(guard_ready, 1)

        @block.tensor
        def _(pe):
            mm_ = nc.tensor.matmul
            for t in range(4):
                pe.wait_ge(xn_ready, 4 * t + 4)
                if t >= 2:
                    pe.wait_ge(qT_ready, t - 1)
                for j in range(4):
                    mm = nc.tensor.transpose(psT[t % 2][:, j], xn[:, 4 * t + j], ident[:])
                mm.then_inc(qT_psum, 1)
            pe.wait_ge(w_in, 16 * 4)
            for n in range(8):
                t, k = divmod(n, 2)
                pe.wait_ge(qT_ready, t + 1)
                if n >= 2:
                    pe.wait_ge(gate_ready, n - 1)
                for s, src in enumerate((qT, ctxT, ctxT)):
                    mm = mm_(psI[k][0:H1, :], gk[:, s, k], src[:, 4 * t:4 * t + 4], start=(s == 0), stop=(s == 2))
                mm.then_inc(gate_psum, 1)
            pe.wait_ge(guard_ready, 1)
            for b in range(B):
                mm = nc.tensor.transpose(psE[:, b], guard[:, b * P:(b + 1) * P], ident[0:H1, 0:H1])
            mm.then_inc(guard_psum, 1)

    with ExitStack() as loop, nc.Block() as block:
        psS = [loop.enter_context(nc.psum_tensor(f"psMS{i}", [P, GH, P], F32)) for i in range(G)]
        psA = [loop.enter_context(nc.psum_tensor(f"psMA{i}", [P, GH, P], F32)) for i in range(G)]
        psN = loop.enter_context(nc.psum_tensor("psMN", [P, H1, VW], F32))
        gate_, staged, argl_ready, argr_ready, s_psum, a_psum, d_ready, c_ready, n_psum, n_ready, sq_ready = (
            sem(n) for n in ("ml_pool_gate", "ml_staged", "ml_argl_ready", "ml_argr_ready", "ml_s_psum",
                             "ml_a_psum", "ml_d_ready", "ml_c_ready", "ml_n_psum", "ml_n_ready", "ml_sq_ready"))
        ms_ready, f_order, var_asked, std_given, x_ready = (
            sem(n) for n in ("ml_ms_ready", "ml_f_order", "ml_var_asked", "ml_std_given", "ml_x_ready"))

        @block.gpsimd
        def _(pool):
            def stage(b, par):
                after(pool, s_psum, 2 * b - 2)
                pool.sem_inc(gate_, 1)
                nc.gpsimd.tensor_copy(ctx_now[:, par], ctxT[:, b]).then_inc(staged, 1)
                nc.gpsimd.tensor_tensor(qm[:, par], qT[:, b].unsqueeze(1).to_broadcast([P, H1, P]),
                                        headm[:].unsqueeze(2).to_broadcast([P, H1, P]),
                                        ALU.mult).then_inc(staged, 1)
            over_batches(nc.gpsimd, stage)

        @block.tensor
        def _(pe):
            mm_ = nc.tensor.matmul

            def values(b, par):
                pe.wait_ge(c_ready, 2 * b + 2)
                after(pe, n_ready, b)
                for h in range(H1):
                    mm = mm_(psN[:, h], cmat[:, par, h], v1[:, b, h], start=(h == 0), stop=(h == H1 - 1),
                             skip_group_check=True)
                mm.then_inc(n_psum, 1)

            def slots(b, par):
                pe.wait_ge(argl_ready, b + 1)
                pe.wait_ge(argr_ready, b + 1)
                for g in range(G):
                    after(pe, d_ready, 2 * b + g - 1)
                    mm_(psA[g][:], argl[:, par], argr[:, par, GH * g:GH * g + GH], start=True, stop=False)
                    mm_(psA[g][:], identb[:], future[:].unsqueeze(1).to_broadcast([P, GH, P]), start=False,
                        stop=True).then_inc(a_psum, 1)
                pe.wait_ge(staged, 2 * b + 2)
                for g in range(G):
                    after(pe, c_ready, 2 * b + g - 1)
                    mm_(psS[g][:], ctx_now[:, par], qm[:, par, GH * g:GH * g + GH], start=True,
                        stop=True).then_inc(s_psum, 1)
                if not known(b, 0):
                    values(b - 1, 1 - par)

            over_batches(nc.tensor, slots)
            values(B - 1, (B - 1) % 2)

        @block.scalar
        def _(act):
            def keys(b, par):
                after(act, a_psum, 2 * b - 2)
                nc.scalar.copy(argl[0:H1, par], gain[:, b]).then_inc(argl_ready, 1)

            def sums(b):
                act.wait_ge(n_psum, b + 1)
                nc.scalar.copy(num[:, b], psN[:]).then_inc(n_ready, 1)

            keys(0, 0)

            def slots(b, par):
                if not known(b, B - 1):
                    keys(b + 1, 1 - par)
                for g in range(G):
                    act.wait_ge(a_psum, 2 * b + g + 1)
                    after(act, c_ready, 2 * b + g - 1)
                    nc.scalar.activation(decay[:, g], psA[g][:], ACT.Exp).then_inc(d_ready, 1)
                if not known(b, 0):
                    sums(b - 1)

            over_batches(nc.scalar, slots)
            sums(B - 1)
            act.wait_ge(var_asked, 1)
            nc.scalar.activation(tmp[:], tmp[:], ACT.Sqrt).then_inc(std_given, 1)

        @block.vector
        def _(dve):
            v = nc.vector

            def peaks(b, par):
                after(dve, a_psum, 2 * b - 2)
                v.tensor_tensor(argr[SROW[1]:SROW[1] + H1, par], peak[:, b].unsqueeze(1).to_broadcast([H1, H1, P]),
                                negone[:], ALU.mult).then_inc(argr_ready, 1)

            def squares(b, par):
                dve.wait_ge(n_ready, b + 1)
                v.tensor_tensor(square[:, par], num[:, b, :, 0:HW1], num[:, b, :, 0:HW1],
                                ALU.mult).then_inc(sq_ready, 1)
                dve.wait_ge(sq_ready, b + 1)
                v.tensor_reduce(msq[:, b], square[:, par], AX.X, ALU.add).then_inc(ms_ready, 1)

            peaks(0, 0)

            def slots(b, par):
                if not known(b, B - 1):
                    peaks(b + 1, 1 - par)
                after(dve, n_psum, b - 1)
                for g in range(G):
                    dve.wait_ge(d_ready, 2 * b + g + 1)
                    dve.wait_ge(s_psum, 2 * b + g + 1)
                    v.tensor_tensor(cmat[:, par, GH * g:GH * g + GH], psS[g][:], decay[:, g],
                                    ALU.mult).then_inc(c_ready, 1)
                if not known(b, 0):
                    squares(b - 1, 1 - par)

            over_batches(nc.vector, slots)
            squares(B - 1, (B - 1) % 2)
            dve.wait_ge(ms_ready, B)
            order = Order(dve, f_order)
            total = num[:, :, :, HW1]
            order.then(v.scalar_tensor_tensor(out=factor[:], in0=total, scalar=-1.0, in1=total,
                                              op0=ALU.mult, op1=ALU.max))
            order.then(v.tensor_tensor(factor[:], factor[:], eguard[:], ALU.max))
            order.then(v.tensor_scalar(factor[:], factor[:], 1e-6, None, ALU.add))
            order.then(v.reciprocal(factor[:], factor[:]))
            order.then(v.tensor_tensor(tmp[:], factor[:], factor[:], ALU.mult))
            order.then(v.tensor_tensor(tmp[:], tmp[:], msq[:], ALU.mult))
            v.tensor_scalar(tmp[:], tmp[:], 1.0 / HW1, 1e-6, ALU.mult, ALU.add).then_inc(var_asked, 1)
            dve.wait_ge(std_given, 1)
            order.then(v.reciprocal(tmp[:], tmp[:]))
            order.then(v.tensor_tensor(factor[:], factor[:], tmp[:], ALU.mult))
            for t in range(4):
                bs = slice(4 * t, 4 * t + 4)
                xs = x_sb[:, bs].rearrange("p b (h e) -> p b h e", h=H1)
                hs = xn[:, bs].rearrange("p b (h e) -> p b h e", h=H1)
                order.then(v.tensor_tensor(hs, num[:, bs, :, 0:HW1],
                                           factor[:, bs].unsqueeze(3).to_broadcast([P, 4, H1, HW1]), ALU.mult))
                v.tensor_tensor(x_sb[:, bs], x_sb[:, bs], xn[:, bs], ALU.add).then_inc(x_ready, 1)
                dve.wait_ge(x_ready, t + 1)
                for b in range(4 * t, 4 * t + 4):
                    order.add(v.bn_stats(bnst[:, b], x_sb[:, b]))


def moe_phase(nc, T, sb, scope, x_sb, ident, identb, bnst, mv, rstd, out):
    TG = 4
    NT = B // TG
    NC = EC + 1
    K3 = NSPLIT * E1

    def sem(name):
        return scope.enter_context(nc.semaphore(name))

    gw = sb("gw", [P, NC, P], F32, scope)
    uw = sb("uw", [P, NC, P], F32, scope)
    dw = sb("dw", [P, NC, P], F32, scope)
    rw = sb("rw", [P, E1], F32, scope)
    xn = sb("xn4", [P, B, P], F32, scope)
    xT = sb("xT4", [P, B, P], F32, scope)
    order_i = sb("order_i", [P, E1], mybir.dt.int32, scope)
    desc = sb("desc", [P, E1], F32, scope)
    prob = sb("prob4", [P, B, E1], F32, scope)
    best = sb("best", [P, B], F32, scope)
    key = sb("key", [P, B, E1], F32, scope)
    pick = sb("pick", [P, 2, B, E1], F32, scope)
    rest = sb("rest", [P, B, E1], F32, scope)
    coef3 = sb("coef3", [P, B, NSPLIT, E1], BF16, scope)
    coefT = sb("coefT", [P, B, P], BF16, scope)
    spread = sb("spread", [P, EC, 2, FX], BF16, scope)
    act_g = sb("act_g", [P, 2, TG * P], F32, scope)
    prod = sb("prod", [P, 2, TG * P], F32, scope)
    inter = sb("inter", [P, 2, TG * P], F32, scope)

    psG = [scope.enter_context(nc.psum_tensor(f"psEG{i}", [P, TG * P], F32)) for i in range(2)]
    psU = [scope.enter_context(nc.psum_tensor(f"psEU{i}", [P, TG * P], F32)) for i in range(2)]
    psC = [scope.enter_context(nc.psum_tensor(f"psEC{i}", [P, TG * P], F32)) for i in range(2)]
    psY = scope.enter_context(nc.psum_tensor("psEY", [P, TG, P], F32))
    psR = scope.enter_context(nc.psum_tensor("psER", [P, B, E1], F32))

    w_in, pool_order, dve_order, var_ready, std_ready, xn_ready = (
        sem(n) for n in ("moe_w_in", "moe_pool_order", "moe_dve_order", "moe_var_ready", "moe_std_ready",
                         "moe_xn_ready"))
    const_ready, xT_psum, xT_ready, r_psum, shifted, exp_ready, coef_ready, coef_psum, coefT_ready = (
        sem(n) for n in ("moe_const_ready", "moe_xT_psum", "moe_xT_ready", "moe_r_psum", "moe_shifted",
                         "moe_exp_ready", "moe_coef_ready", "moe_coef_psum", "moe_coefT_ready"))
    gu_psum, g_ready, prod_ready, c_psum, inter_ready, down_done, y_ready, stored = (
        sem(n) for n in ("moe_gu_psum", "moe_g_ready", "moe_prod_ready", "moe_c_psum", "moe_inter_ready",
                         "moe_down_done", "moe_y_ready", "moe_stored"))
    NW = 7

    def turned(t):
        return psG[t % 2][:].rearrange("p (b d) -> p b d", b=TG)

    def coef_bank(b):
        bank = psC[b // 8][:].bitcast(BF16)
        return bank[0:K3, (b % 8) * P:(b % 8 + 1) * P]

    with nc.Block() as block:
        @block.sync
        def _(sp):
            sp.dma_start(rw[:], T["L1_ffn_router_w"]).then_inc(w_in, 16)
            for name, dest in (("gate", gw), ("up", uw)):
                sp.dma_start(dest[:, 0:EC].rearrange("p c (two f) -> p (c two) f", two=2),
                             T[f"L1_ffn_{name}_w"].rearrange("e p f -> p e f")).then_inc(w_in, 16)
                sp.dma_start(dest[:, EC], T[f"L1_ffn_shared_{name}_w"]).then_inc(w_in, 16)
            sp.dma_start(dw[:, 0:EC], T["L1_ffn_down_w"].rearrange("e f d -> (e f) d")
                         .rearrange("(c p) d -> p c d", p=P)).then_inc(w_in, 16)
            sp.dma_start(dw[:, EC], T["L1_ffn_shared_down_w"]).then_inc(w_in, 16)
            for t in range(NT):
                sp.wait_ge(y_ready, t + 1)
                sp.dma_start(out[TG * t:TG * t + TG].rearrange("b s d -> s b d"),
                             x_sb[:, TG * t:TG * t + TG]).then_inc(stored, 16)
            sp.wait_ge(stored, 16 * NT)

        @block.gpsimd
        def _(pool):
            order = Order(pool, pool_order)
            order.add(nc.gpsimd.iota(order_i[:], pattern=[[-1, E1]], base=E1, channel_multiplier=0))
            order.add(nc.gpsimd.memset(spread[:], 0.0))
            order.add(nc.gpsimd.memset(coefT[:], 0.0))
            order.sync()
            nc.gpsimd.tensor_copy(desc[:], order_i[:]).then_inc(const_ready, 1)
            for part in range(NSPLIT):
                order.then(nc.gpsimd.affine_select(out=spread[:], in_=spread[:], compare_op=ALU.not_equal,
                                                   fill=1.0, base=-E1 * part,
                                                   pattern=[[-2, EC], [-1, 2], [0, FX]], channel_multiplier=1))
            pool.sem_inc(const_ready, 1)

        @block.scalar
        def _(act):
            act.wait_ge(var_ready, 1)
            nc.scalar.activation(rstd[:], rstd[:], ACT.Sqrt).then_inc(std_ready, 1)
            for t in range(NT):
                act.wait_ge(xT_psum, t + 1)
                nc.scalar.copy(xT[:, TG * t:TG * t + TG], turned(t)).then_inc(xT_ready, 1)
            act.wait_ge(shifted, 1)
            nc.scalar.activation(prob[:], prob[:], ACT.Exp).then_inc(exp_ready, 1)
            act.wait_ge(coef_psum, 1)
            act.wait_ge(const_ready, 2)
            for k in range(2):
                nc.scalar.copy(coefT[0:K3, 8 * k:8 * k + 8].rearrange("k b s -> k (b s)"),
                               psC[k][:].bitcast(BF16)[0:K3]).then_inc(coefT_ready, 1)

            def slots(t):
                for e in range(NC):
                    n = NC * t + e
                    act.wait_ge(gu_psum, n + 1)
                    after(act, prod_ready, n - 1 if e else n)
                    nc.scalar.activation(act_g[:, e % 2], psG[e % 2][:], ACT.Silu).then_inc(g_ready, 1)

            slots(0)
            with nc.scalar.Fori(1, NT) as t:
                slots(t)

        @block.vector
        def _(dve):
            v = nc.vector
            order = Order(dve, dve_order)
            layernorm_all(v, (var_ready, std_ready), order, dve, x_sb, bnst, mv, rstd)
            for b in range(B):
                v.tensor_scalar(xn[:, b], x_sb[:, b], mv[:, b, 0:1], rstd[:, b:b + 1],
                                ALU.subtract, ALU.mult).then_inc(xn_ready, 1)
            wide = [P, B, E1]

            def over(col):
                return col[:].unsqueeze(2).to_broadcast(wide)

            dve.wait_ge(r_psum, 1)
            order.then(v.tensor_reduce(best[:], psR[:], AX.X, ALU.max))
            v.tensor_tensor(prob[:], psR[:], over(best), ALU.subtract).then_inc(shifted, 1)
            dve.wait_ge(exp_ready, 1)
            order.then(v.tensor_reduce(best[:], prob[:], AX.X, ALU.add))
            order.then(v.reciprocal(best[:], best[:]))
            order.then(v.tensor_tensor(prob[:], prob[:], over(best), ALU.mult))
            dve.wait_ge(const_ready, 2)
            left = prob
            for k in range(2):
                order.then(v.tensor_reduce(best[:], left[:], AX.X, ALU.max))
                order.then(v.tensor_tensor(key[:], left[:], over(best), ALU.is_equal))
                order.then(v.tensor_tensor(key[:], key[:], desc[:].unsqueeze(1).to_broadcast(wide), ALU.mult))
                order.then(v.tensor_reduce(best[:], key[:], AX.X, ALU.max))
                order.then(v.tensor_tensor(pick[:, k], key[:], over(best), ALU.is_equal))
                if k == 0:
                    order.then(v.scalar_tensor_tensor(out=rest[:].rearrange("p b e -> p (b e)"),
                                                      in0=pick[:, 0].rearrange("p b e -> p (b e)"), scalar=-2.0,
                                                      in1=prob[:].rearrange("p b e -> p (b e)"),
                                                      op0=ALU.mult, op1=ALU.add))
                    left = rest
            order.then(v.tensor_tensor(pick[:, 0], pick[:, 0], pick[:, 1], ALU.add))
            order.then(v.tensor_tensor(prob[:], prob[:], pick[:, 0], ALU.mult))
            for part in range(NSPLIT):
                order.then(v.tensor_copy(coef3[:, :, part], prob[:]))
                if part < NSPLIT - 1:
                    order.then(v.tensor_tensor(prob[:], prob[:], coef3[:, :, part], ALU.subtract))
            v.engine_nop().then_inc(coef_ready, 1)

            def slots(t):
                for e in range(NC):
                    n = NC * t + e
                    free = n - 1 if e else n
                    dve.wait_ge(g_ready, n + 1)
                    if e < EC:
                        v.tensor_tensor(prod[:, e % 2], act_g[:, e % 2], psU[e % 2][:],
                                        ALU.mult).then_inc(prod_ready, 1)
                        dve.wait_ge(prod_ready, n + 1)
                        dve.wait_ge(c_psum, EC * t + e + 1)
                        after(dve, down_done, free)
                        v.tensor_tensor(inter[:, e % 2], prod[:, e % 2], psC[e % 2][:],
                                        ALU.mult).then_inc(inter_ready, 1)
                    else:
                        after(dve, down_done, free)
                        v.tensor_tensor(inter[:, e % 2], act_g[:, e % 2], psU[e % 2][:],
                                        ALU.mult).then_inc(prod_ready, 1)
                        dve.wait_ge(prod_ready, n + 1)
                        dve.sem_inc(inter_ready, 1)
                dve.wait_ge(down_done, NC * t + NC)
                if isinstance(t, int):
                    xs = x_sb[:, TG * t:TG * t + TG]
                else:
                    xs = x_sb[:, bass.ds(TG * t, TG)]
                v.tensor_tensor(xs, xs, psY[:], ALU.add).then_inc(y_ready, 1)

            slots(0)
            with v.Fori(1, NT) as t:
                slots(t)

        @block.tensor
        def _(pe):
            mm_ = nc.tensor.matmul
            for t in range(NT):
                pe.wait_ge(xn_ready, TG * (t + 1))
                if t >= 2:
                    pe.wait_ge(xT_ready, t - 1)
                for j in range(TG):
                    mm = nc.tensor.transpose(turned(t)[:, j], xn[:, TG * t + j], ident[:])
                mm.then_inc(xT_psum, 1)
            pe.wait_ge(w_in, 16 * NW)
            pe.wait_ge(xT_ready, NT)
            for b in range(B):
                mm = mm_(psR[:, b], xT[:, b], rw[:], start=True, stop=True)
            mm.then_inc(r_psum, 1)
            pe.wait_ge(coef_ready, 1)
            for b in range(B):
                mm = nc.tensor.transpose(coef_bank(b), coef3[:, b].rearrange("p k e -> p (k e)"), identb[:])
            mm.then_inc(coef_psum, 1)
            pe.wait_ge(const_ready, 2)
            pe.wait_ge(coefT_ready, 2)

            def rows(a, t):
                if isinstance(t, int):
                    return a[:, TG * t:TG * t + TG]
                return a[:, bass.ds(TG * t, TG)]

            def down(t, e):
                n = NC * t + e
                pe.wait_ge(inter_ready, n + 1)
                if e == 0:
                    after(pe, y_ready, t)
                for j in range(TG):
                    mm = mm_(psY[:, j], inter[:, e % 2, j * P:(j + 1) * P], dw[:, e],
                             start=(e == 0 and j == 0), stop=(e == NC - 1 and j == TG - 1), skip_group_check=True)
                mm.then_inc(down_done, 1)

            def slots(t):
                for e in range(NC):
                    n = NC * t + e
                    after(pe, prod_ready, n - 1 if e else n)
                    mm_(psG[e % 2][:], gw[:, e], rows(xT, t), start=True, stop=True)
                    mm_(psU[e % 2][:], uw[:, e], rows(xT, t), start=True, stop=True).then_inc(gu_psum, 1)
                    if e < EC:
                        after(pe, inter_ready, n - 1)
                        mm_(psC[e % 2][:], spread[:, e].rearrange("k a f -> k (a f)"), rows(coefT, t),
                            start=True, stop=True).then_inc(c_psum, 1)
                    if e:
                        down(t, e - 1)
                pe.wait_ge(inter_ready, NC * t + NC)
                down(t, NC - 1)

            slots(0)
            with nc.tensor.Fori(1, NT) as t:
                slots(t)


_INS = ['x', 'ctx_1024', 'fside_BxSx4_0', 'L0_xattn_Wq', 'L0_xattn_bq', 'L0_xattn_Wk', 'L0_xattn_bk',
        'L0_xattn_Wv', 'L0_xattn_bv', 'L0_xattn_Wo', 'L0_xattn_bo', 'L0_xattn_Wg', 'L0_xattn_bg',
        'L0_ffn_w1', 'L0_ffn_b1', 'L0_ffn_w2', 'L0_ffn_b2', 'L1_xattn_igate_kernel', 'L1_xattn_igate_bias',
        'L1_xattn_fgate_kernel', 'L1_xattn_fgate_bias', 'L1_ffn_router_w', 'L1_ffn_gate_w', 'L1_ffn_up_w',
        'L1_ffn_down_w', 'L1_ffn_shared_gate_w', 'L1_ffn_shared_up_w', 'L1_ffn_shared_down_w']
STAGE = 4


def kernel(**inputs):
    import numpy as _np
    import concourse.bacc as _bacc
    from concourse import mybir as _mybir
    from concourse.bass_utils import run_bass_kernel_spmd as _run

    nc = _bacc.Bacc("TRN2", target_bir_lowering=False, num_devices=1)
    arrays, tensors = {}, {}
    for name in _INS:
        a = _np.ascontiguousarray(inputs[name])
        arrays[f"in_{name}_dram"] = a
        tensors[name] = nc.dram_tensor(f"in_{name}_dram", a.shape, _mybir.dt.from_np(a.dtype),
                                       kind="ExternalInput").ap()
    out = nc.dram_tensor("out_0_dram", (B, P, P), F32, kind="ExternalOutput").ap()
    build(nc, tensors, out, STAGE)
    r = _run(nc, [arrays], core_ids=[0])
    return r.results[0]["out_0_dram"]
```

```python
from contextlib import ExitStack
import math

import concourse.bass as bass
from concourse import mybir

F32 = mybir.dt.float32
BF16 = mybir.dt.bfloat16
F16 = mybir.dt.float16
ALU = mybir.AluOpType
ACT = mybir.ActivationFunctionType
AX = mybir.AxisListType
RMAX = bass.bass_isa.ReduceOp.max

P = 128
B = 16
H0 = 16
DK = 64
HD = H0 * DK
CH = HD // P
HG = 4
UN = H0 // HG
NG = 8
GN = P // NG
F1 = 512
FC = F1 // P
H1 = 8
HW1 = P // H1
E1 = 16
FX = 64
EC = E1 * FX // P
LN_EPS = 1e-5
Q_EPS = 1e-8
ROUND = 1.5 * 2.0 ** 23
TURN = 6.2831845
COS_SHIFT = math.exp(math.pi / 2 / 100.0)
MASKED = -1e30
CYCLES = 100.0 / (4.0 * math.pi)
W_UP = 64.0
G_UP = 4096.0
EXP_LN = "natural_log_exp_and_others"
NSPLIT = 3
SROW = [0, 32, 64]
KB = SROW[-1] + 1
KQ = SROW[-1] + 2 * CH


def after(eng, sem, value):
    if isinstance(value, int) and value <= 0:
        return
    eng.wait_ge(sem, value)


class Order:

    def __init__(self, eng, sem):
        self.eng, self.sem, self.n = eng, sem, 0

    def add(self, ins):
        self.n += 1
        ins.then_inc(self.sem, 1)

    def sync(self):
        self.eng.wait_ge(self.sem, self.n)

    def then(self, ins):
        self.add(ins)
        self.sync()


def over_batches(eng, slots):
    for b in range(2):
        slots(b, b)
    with eng.Fori(2, B - 2, 2) as i:
        for par in range(2):
            slots(i + par, par)
    for b in range(B - 2, B):
        slots(b, b % 2)


def known(b, value):
    return isinstance(b, int) and b == value


def build(nc, T, out, stage):
    ctx = ExitStack()
    with ctx:
        def sb(name, shape, dt=F32, where=ctx):
            return where.enter_context(nc.sbuf_tensor(name, shape, dt))

        x_sb = sb("x_sb", [P, B, P])
        ctx_sb = sb("ctx_sb", [P, B, P])
        ctxT2 = sb("ctxT2", [P, 2, B, P], F16)
        ident = sb("ident", [P, P])
        identb = sb("identb", [P, P], BF16)
        bnst = sb("bnst", [P, B, 6])
        mv = sb("mv", [P, B, 2])
        rstd = sb("rstd", [P, B])
        for_attention = ExitStack()
        with for_attention:
            attention_phases(nc, T, sb, for_attention, x_sb, ctx_sb, ctxT2, ident, identb, bnst, mv, rstd)
        if stage >= 2:
            with ExitStack() as scope:
                ffn_phase(nc, T, sb, scope, x_sb, ident, identb, bnst, mv, rstd)
        if stage >= 3:
            with ExitStack() as scope:
                mlstm_phase(nc, T, sb, scope, x_sb, ctx_sb, ctxT2, ident, identb, bnst, mv, rstd)
        if stage >= 4:
            with ExitStack() as scope:
                moe_phase(nc, T, sb, scope, x_sb, ident, identb, bnst, mv, rstd, out)
        else:
            s_out = ctx.enter_context(nc.semaphore("s_out"))
            with nc.Block() as block:
                @block.sync
                def _(sp):
                    sp.dma_start(out.rearrange("b s d -> s b d"), x_sb[:]).then_inc(s_out, 16)
                    sp.wait_ge(s_out, 16)


def attention_phases(nc, T, sb, scope, x_sb, ctx_sb, ctxT2, ident, identb, bnst, mv, rstd):
    buf = dict(
        xT2=sb("xT2", [P, 2, B, P], F16, scope),
        wT2=sb("wT2", [P, 3, 2, CH, P], F16, scope),
        woT=sb("woT", [P, CH, P], F32, scope),
        kron2=sb("kron2", [P, 2, H0, GN], F16, scope),
        bqk3=sb("bqk3", [KQ, P], BF16, scope),
        bias_pick=sb("bias_pick", [KQ, 2 * CH, P], BF16, scope),
        bo3=sb("bo3", [KB, P], BF16, scope),
        bg3=sb("bg3", [KB, H0], BF16, scope),
        ones3=sb("ones3", [KB, P], BF16, scope),
        beta=sb("beta", [P, B + 1, P], F32, scope),
        alpha=sb("alpha", [P, B + 1, NG], F32, scope),
        gamma2=sb("gamma2", [P, B + 1, NG], F32, scope),
        least2=sb("least2", [P, 1], F32, scope),
        arg=sb("arg", [P, 2, NG, P], F32, scope),
        turns=sb("turns", [P, 2, NG, P], F32, scope),
        whole=sb("whole", [P, 2, NG, P], F32, scope),
        wave=sb("wave", [P, 2, NG, P], F32, scope),
        emb2=sb("emb2", [P, 2, 2, NG, P], F16, scope),
        vx2=sb("vx2", [P, 2, 2, H0, DK + 1], F16, scope),
    )
    with ExitStack() as prep:
        prepare_phase(nc, T, sb, prep, x_sb, ctx_sb, ctxT2, ident, identb, bnst, mv, rstd, **buf)
    with ExitStack() as loop:
        attention_loop(nc, sb, loop, x_sb, ctxT2, identb, ident, bnst, **buf)


def prepare_phase(nc, T, sb, scope, x_sb, ctx_sb, ctxT2, ident, identb, bnst, mv, rstd,
                  xT2, wT2, woT, kron2, bqk3, bias_pick, bo3, bg3, ones3, beta, alpha, gamma2, least2,
                  arg, turns, whole, wave, emb2, vx2):
    def sem(name):
        return scope.enter_context(nc.semaphore(name))

    raw = sb("raw", [P, 4, CH, P], F32, scope)
    xn = sb("xn", [P, B, P], F32, scope)
    box = sb("box", [P, B, 4], F32, scope)
    fbeta = sb("fbeta", [P, B, 4], F32, scope)
    falpha = sb("falpha", [P, B, 4], F32, scope)
    fgamma = sb("fgamma", [P, B, 4], F32, scope)
    repeat = sb("repeat", [P, NG, P], F32, scope)
    kinds = sb("kinds", [P, B, P], F32, scope)
    kind4 = sb("kind4", [P, 4], F32, scope)
    delta16 = sb("delta16", [P, GN], F32, scope)
    picked = sb("picked", [P, NG, B, 4], F32, scope)
    shift = sb("shift", [P, 1], F32, scope)
    wgp = sb("wgp", [P, H0], F32, scope)
    kron = sb("kron", [P, H0, GN], F32, scope)
    chunk1 = sb("chunk1", [KQ, 2 * CH], F32, scope)
    qkrow = sb("qkrow", [KQ, P], F32, scope)
    qkpart = sb("qkpart", [KQ, P], BF16, scope)
    bv = sb("bv", [CH, P], F32, scope)
    bvT = sb("bvT", [P, CH], F32, scope)
    orow = sb("orow", [KB, P], F32, scope)
    opart = sb("opart", [KB, P], BF16, scope)
    grow = sb("grow", [KB, H0], F32, scope)
    gpart = sb("gpart", [KB, H0], BF16, scope)

    psT = scope.enter_context(nc.psum_tensor("psT", [P, 3, 4, P], F32))
    psB = scope.enter_context(nc.psum_tensor("psB", [P, B, P], F32))
    psA = scope.enter_context(nc.psum_tensor("psA", [P, NG, B, 4], F32))

    x_in, ctx_in, wo_in, box_in, wg_in, bias_in = (
        sem(n) for n in ("x_in", "ctx_in", "wo_in", "box_in", "wg_in", "bias_in"))
    w_in = [sem(f"w{k}_in") for k in range(3)]
    pool_order, dve_order, act_order = sem("pool_order"), sem("dve_order"), sem("act_order")
    ident_ready, chunk_ready, square_ready = sem("ident_ready"), sem("chunk_ready"), sem("square_ready")
    var_ready, std_ready, xn_ready = sem("var_ready"), sem("std_ready"), sem("xn_ready")
    boxes_ready, beta_psum, beta_ready, picked_psum, picked_read = (
        sem(n) for n in ("boxes_ready", "beta_psum", "beta_ready", "picked_psum", "picked_read"))
    tr_psum, hi_ready, lo_ready = sem("tr_psum"), sem("hi_ready"), sem("lo_ready")
    dist_ready, arg_ready, log_ready, whole_ready, frac_ready, wave_ready, emb_hi, bvT_psum, bvT_ready, bo_psum = (
        sem(n) for n in ("dist_ready", "arg_ready", "log_ready", "whole_ready", "frac_ready", "wave_ready",
                         "emb_hi", "bvT_psum", "bvT_ready", "bo_psum"))

    NTR = 4 + 4 + 6 + 2

    def halves(n):
        if n < 4:
            return ctxT2[:, 0, 4 * n:4 * n + 4], ctxT2[:, 1, 4 * n:4 * n + 4], 1.0
        if n < 8:
            return xT2[:, 0, 4 * n - 16:4 * n - 12], xT2[:, 1, 4 * n - 16:4 * n - 12], 1.0
        k, half = divmod(n - 8, 2)
        return wT2[:, k, 0, 4 * half:4 * half + 4], wT2[:, k, 1, 4 * half:4 * half + 4], W_UP

    def flat(a):
        return a.rearrange("p g m -> p (g m)")

    with nc.Block() as block:
        @block.sync
        def _(sp):
            sp.dma_start(box[:], T["fside_BxSx4_0"].rearrange("b s c -> s b c")).then_inc(box_in, 16)
            sp.dma_start(ctx_sb[:], T["ctx_1024"].rearrange("b s d -> s b d")).then_inc(ctx_in, 16)
            for k, name in enumerate(("L0_xattn_Wq", "L0_xattn_Wk", "L0_xattn_Wv")):
                sp.dma_start(raw[:, k], T[name].rearrange("(c p) d -> p c d", p=P)).then_inc(w_in[k], 16)

        @block.scalar
        def _(act):
            act.dma_start(x_sb[:], T["x"].rearrange("b s d -> s b d")).then_inc(x_in, 16)
            act.dma_start(raw[:, 3], T["L0_xattn_Wo"].rearrange("p (c d) -> p c d", d=P)).then_inc(wo_in, 16)
            for t in range(4):
                act.wait_ge(beta_psum, t + 1)
                nc.scalar.copy(beta[:, 4 * t:4 * t + 4], psB[:, 4 * t:4 * t + 4]).then_inc(beta_ready, 1)
            def evacuate(n):
                act.wait_ge(tr_psum, n + 1)
                hi, _, up = halves(n)
                nc.scalar.activation(hi, psT[:, n % 3], ACT.Copy, scale=up).then_inc(hi_ready, 1)

            evacuate(0)
            act.wait_ge(dist_ready, 1)
            nc.scalar.activation(arg[:], arg[:], ACT.Square).then_inc(square_ready, 1)
            act.wait_ge(var_ready, 1)
            nc.scalar.activation(rstd[:], rstd[:], ACT.Sqrt).then_inc(std_ready, 1)
            evacuate(1)
            act.wait_ge(arg_ready, 1)
            nc.scalar.activation(arg[:], arg[:], ACT.Ln).then_inc(log_ready, 1)
            act.wait_ge(log_ready, 1)
            nc.scalar.activation(turns[:], arg[:], ACT.Copy, scale=CYCLES).then_inc(log_ready, 1)
            for n in range(2, 5):
                evacuate(n)
            act.wait_ge(frac_ready, 1)
            nc.scalar.activation(wave[:], whole[:], ACT.Sin, scale=-TURN).then_inc(wave_ready, 1)
            act.wait_ge(wave_ready, 1)
            nc.scalar.copy(emb2[:, 0, 0], wave[:, 0]).then_inc(emb_hi, 1)
            for n in range(5, 14):
                evacuate(n)
            for n in range(14, NTR):
                act.wait_ge(tr_psum, n + 1)
                nc.scalar.activation(woT[:, 4 * n - 56:4 * n - 52], psT[:, n % 3], ACT.Copy,
                                     scale=1.0 / W_UP).then_inc(hi_ready, 1)
            nc.scalar.preload_act_table(ACT.Exp)

        @block.gpsimd
        def _(pool):
            order = Order(pool, pool_order)
            order.add(nc.gpsimd.memset(ident[:], 0.0))
            order.add(nc.gpsimd.memset(identb[:], 0.0))
            order.add(nc.gpsimd.memset(falpha[:], 0.0))
            order.add(nc.gpsimd.memset(qkrow[:], 0.0))
            order.sync()
            nc.gpsimd.affine_select(out=ident[:], in_=ident[:], compare_op=ALU.not_equal, fill=1.0,
                                    base=0, pattern=[[-1, P]], channel_multiplier=1).then_inc(ident_ready, 1)
            nc.gpsimd.affine_select(out=identb[:], in_=identb[:], compare_op=ALU.not_equal, fill=1.0,
                                    base=0, pattern=[[-1, P]], channel_multiplier=1).then_inc(ident_ready, 1)
            for row in SROW:
                for k, name in enumerate(("L0_xattn_bq", "L0_xattn_bk")):
                    pool.dma_start(qkrow[row + CH * k:row + CH * k + CH], T[name].rearrange("(c p) -> c p", p=P)
                                   ).then_inc(bias_in, 16)
            pool.dma_start(bv[:], T["L0_xattn_bv"].rearrange("(c p) -> c p", p=P)).then_inc(bias_in, 16)
            for dest, name in ((orow, "L0_xattn_bo"), (grow, "L0_xattn_bg")):
                pool.dma_start(dest[:], T[name].rearrange("(o n) -> o n", o=1)
                               .to_broadcast([KB, T[name].shape[0]])).then_inc(bias_in, 16)
            with nc.allow_non_contiguous_dma(reason="2048 words of Wg, once"):
                for kind in range(8):
                    pool.dma_start(wgp[16 * kind:16 * kind + 16, :],
                                   T["L0_xattn_Wg"].rearrange("h k -> k h")[kind:kind + 1, :]
                                   .to_broadcast([16, H0])).then_inc(wg_in, 16)
            g = nc.gpsimd
            order.add(g.memset(vx2[:, :, 0, :, DK:], 1.0))
            order.add(g.memset(vx2[:, :, 1, :, DK:], 0.0))
            order.add(g.memset(ones3[:], 0.0))
            order.add(g.memset(bg3[:], 0.0))
            order.sync()
            for row in SROW:
                order.then(g.memset(ones3[row:row + 1, :], 1.0))
            pool.wait_ge(bias_in, 16 * 9)
            pool.wait_ge(chunk_ready, 1)
            order.add(g.tensor_copy(bias_pick[:], chunk1[:].unsqueeze(2).to_broadcast([KQ, 2 * CH, P])))

            def three_parts(rows, part, dest):
                for k, row in enumerate(SROW):
                    order.then(g.tensor_copy(part[:], rows[:]))
                    dest(row)
                    if k < NSPLIT - 1:
                        order.then(g.tensor_tensor(rows[:], rows[:], part[:], ALU.subtract))

            def to_qk(row):
                order.then(g.tensor_copy(bqk3[row:min(row + 32, KQ), :], qkpart[row:min(row + 32, KQ), :]))

            def to_g(row):
                order.then(g.tensor_copy(bg3[row:row + 1], gpart[row:row + 1, :]))

            order.add(g.tensor_scalar(qkrow[:], qkrow[:], W_UP, None, ALU.mult))
            order.add(g.tensor_scalar(grow[:], grow[:], G_UP, None, ALU.mult))
            order.sync()
            three_parts(qkrow, qkpart, to_qk)
            three_parts(grow, gpart, to_g)

        @block.vector
        def _(dve):
            order = Order(dve, dve_order)
            v = nc.vector
            dve.wait_ge(ident_ready, 2)
            order.add(v.tensor_reduce(kind4[:], ident[:].rearrange("p (a t n) -> p t a n", a=2, t=4),
                                      AX.XY, ALU.add))
            order.add(v.tensor_reduce(delta16[:], ident[:].rearrange("p (d n) -> p n d", n=GN),
                                      AX.X, ALU.add))
            order.add(v.tensor_reduce(shift[:], ident[:, P // 2:], AX.X, ALU.add))
            order.add(v.tensor_copy(repeat[:].rearrange("p g (k n) -> p g k n", n=GN),
                                    ident[:].rearrange("p (g n) -> p g n", n=GN).unsqueeze(2)
                                    .to_broadcast([P, NG, NG, GN])))
            v.tensor_reduce(chunk1[:], ident[0:KQ, 0:SROW[2] + SROW[1]]
                            .rearrange("p (a c) -> p c a", a=NSPLIT)[:, 0:2 * CH],
                            AX.X, ALU.add).then_inc(chunk_ready, 1)
            dve.wait_ge(box_in, 16)
            order.add(v.tensor_tensor(fbeta[:, :, 0:2], box[:, :, 0:2], box[:, :, 2:4], ALU.add))
            order.add(v.tensor_tensor(fgamma[:, :, 2:4], box[:, :, 2:4], box[:, :, 0:2], ALU.subtract))
            order.sync()
            order.add(v.tensor_scalar(fbeta[:, :, 0:2], fbeta[:, :, 0:2], 0.5, None, ALU.mult))
            order.add(v.tensor_scalar(fgamma[:, :, 2:4], fgamma[:, :, 2:4], 1.0, None, ALU.add))
            order.add(v.tensor_scalar(shift[:], shift[:], COS_SHIFT - 1.0, 1.0, ALU.mult, ALU.add))
            order.add(v.tensor_tensor(least2[:], kind4[:, 0:1], kind4[:, 1:2], ALU.add))
            order.sync()
            order.add(v.reciprocal(fgamma[:, :, 0:2], fgamma[:, :, 2:4]))
            order.add(v.tensor_copy(falpha[:, :, 0:2], fbeta[:, :, 0:2]))
            order.add(v.tensor_scalar(least2[:], least2[:], 1e-3, 1e-18, ALU.mult, ALU.add))
            order.sync()
            order.add(v.tensor_copy(fbeta[:, :, 2:4], fgamma[:, :, 0:2]))
            order.add(v.tensor_tensor(least2[:], least2[:], shift[:], ALU.mult))
            order.sync()
            order.add(v.tensor_tensor(least2[:], least2[:], least2[:], ALU.mult))
            for half in range(2):
                order.add(v.tensor_copy(kinds[:, :, 64 * half:64 * half + 64]
                                        .rearrange("p b (t n) -> p b t n", n=GN),
                                        fbeta[:].unsqueeze(3).to_broadcast([P, B, 4, GN])))
            order.sync()
            v.engine_nop().then_inc(boxes_ready, 1)
            for k, dest in enumerate((alpha, gamma2)):
                dve.wait_ge(picked_psum, k + 1)
                order.then(v.tensor_tensor(picked[:].rearrange("p g b t -> p (g b) t"),
                                           psA[:].rearrange("p g b t -> p (g b) t"),
                                           kind4[:].unsqueeze(1).to_broadcast([P, NG * B, 4]), ALU.mult))
                order.then(v.tensor_reduce(dest[:, 0:B].rearrange("p b g -> p g b"), picked[:], AX.X, ALU.add))
                v.engine_nop().then_inc(picked_read, 1)
            order.then(v.tensor_scalar(gamma2[:, 0:B], gamma2[:, 0:B], shift[:, 0:1], None, ALU.mult))
            order.then(v.tensor_tensor(gamma2[:, 0:B], gamma2[:, 0:B], gamma2[:, 0:B], ALU.mult))
            dve.wait_ge(beta_ready, 1)
            for b in range(2):
                order.add(v.tensor_tensor(arg[:, b], beta[:, b].unsqueeze(1).to_broadcast([P, NG, P]),
                                          alpha[:, b].unsqueeze(2).to_broadcast([P, NG, P]), ALU.subtract))
            order.sync()
            v.engine_nop().then_inc(dist_ready, 1)
            dve.wait_ge(x_in, 16)
            for b in range(B):
                order.add(v.bn_stats(bnst[:, b], x_sb[:, b]))
            order.sync()
            for b in range(B):
                order.add(v.bn_aggr(mv[:, b], bnst[:, b]))
            order.sync()
            v.tensor_scalar(rstd[:], mv[:, :, 1], LN_EPS, None, ALU.add).then_inc(var_ready, 1)
            dve.wait_ge(square_ready, 1)
            for b in range(2):
                order.add(v.tensor_tensor(arg[:, b], arg[:, b], gamma2[:, b].unsqueeze(2)
                                          .to_broadcast([P, NG, P]), ALU.mult))
            order.sync()
            v.tensor_scalar(arg[:], arg[:], least2[:, 0:1], None, ALU.max).then_inc(arg_ready, 1)

            def low_half(n):
                dve.wait_ge(hi_ready, n + 1)
                hi, lo, up = halves(n)
                v.scalar_tensor_tensor(out=lo, in0=psT[:, n % 3], scalar=up, in1=hi, op0=ALU.mult,
                                       op1=ALU.subtract).then_inc(lo_ready, 1)

            low_half(0)
            dve.wait_ge(std_ready, 1)
            order.then(v.reciprocal(rstd[:], rstd[:]))
            for b in range(B):
                v.tensor_scalar(xn[:, b], x_sb[:, b], mv[:, b, 0:1], rstd[:, b:b + 1],
                                ALU.subtract, ALU.mult).then_inc(xn_ready, 1)
            low_half(1)
            dve.wait_ge(log_ready, 1)
            order.then(v.tensor_scalar(whole[:], arg[:], CYCLES, ROUND, ALU.mult, ALU.add))
            dve.wait_ge(log_ready, 2)
            v.scalar_tensor_tensor(out=flat(whole[:].rearrange("p b g m -> p (b g) m")),
                                   in0=flat(whole[:].rearrange("p b g m -> p (b g) m")), scalar=ROUND,
                                   in1=flat(turns[:].rearrange("p b g m -> p (b g) m")), op0=ALU.subtract,
                                   op1=ALU.subtract).then_inc(frac_ready, 1)
            for n in range(2, 5):
                low_half(n)
            dve.wait_ge(wg_in, 16 * 8)
            order.then(v.scalar_tensor_tensor(out=kron[:], in0=wgp[:].unsqueeze(2).to_broadcast([P, H0, GN]),
                                              scalar=G_UP, in1=delta16[:].unsqueeze(1).to_broadcast([P, H0, GN]),
                                              op0=ALU.mult, op1=ALU.mult))
            order.then(v.tensor_copy(kron2[:, 0], kron[:]))
            order.add(v.tensor_tensor(kron2[:, 1], kron[:], kron2[:, 0], ALU.subtract))
            dve.wait_ge(bvT_psum, 1)
            v.tensor_copy(bvT[:], psA[:].rearrange("p g b t -> p (g b t)")[:, 0:CH]).then_inc(bvT_ready, 1)
            dve.wait_ge(emb_hi, 1)
            order.add(v.tensor_tensor(emb2[:, 0, 1], wave[:, 0], emb2[:, 0, 0], ALU.subtract))
            for n in range(5, 14):
                low_half(n)
            order.add(v.memset(bo3[:], 0.0))
            dve.wait_ge(bo_psum, 1)
            order.then(v.scalar_tensor_tensor(out=orow[:], in0=psA[0:KB].rearrange("p g b t -> p (g b t)")
                                              [:, P:2 * P], scalar=W_UP, in1=orow[:], op0=ALU.mult, op1=ALU.add))
            for k, row in enumerate(SROW):
                order.then(v.tensor_copy(opart[:], orow[:]))
                order.add(v.tensor_copy(bo3[row:row + 1, :], opart[row:row + 1, :]))
                if k < NSPLIT - 1:
                    order.then(v.tensor_tensor(orow[:], orow[:], opart[:], ALU.subtract))

        @block.tensor
        def _(pe):
            pe.wait_ge(ident_ready, 2)
            pe.wait_ge(boxes_ready, 1)
            def betas(t):
                for b in range(4 * t, 4 * t + 4):
                    mm = nc.tensor.matmul(psB[:, b], kinds[:, b], ident[:], start=True, stop=True)
                mm.then_inc(beta_psum, 1)

            for k, src in enumerate((falpha, fgamma)):
                if k:
                    pe.wait_ge(picked_read, k)
                for g in range(NG):
                    mm = nc.tensor.matmul(psA[:, g], repeat[:, g], src[:], start=(g == 0), stop=(g == NG - 1),
                                          skip_group_check=True)
                mm.then_inc(picked_psum, 1)
                for t in ((0,), (1, 2, 3))[k]:
                    betas(t)

            def turn(n, blocks):
                if n >= 3:
                    pe.wait_ge(lo_ready, n - 2)
                for j, block_in in enumerate(blocks):
                    mm = nc.tensor.transpose(psT[:, n % 3, j], block_in, ident[:])
                mm.then_inc(tr_psum, 1)

            pe.wait_ge(ctx_in, 16)
            for n in range(4):
                turn(n, [ctx_sb[:, 4 * n + j] for j in range(4)])
            pe.wait_ge(bias_in, 16 * 9)
            pe.wait_ge(picked_read, 2)
            nc.tensor.transpose(psA[:].rearrange("p g b t -> p (g b t)")[:, 0:CH], bv[:],
                                ident[0:CH, 0:CH]).then_inc(bvT_psum, 1)
            for n in range(4):
                pe.wait_ge(xn_ready, 4 * n + 4)
                turn(4 + n, [xn[:, 4 * n + j] for j in range(4)])
            for n in range(6):
                if n % 2 == 0:
                    pe.wait_ge(w_in[n // 2], 16)
                turn(8 + n, [raw[:, n // 2, 4 * (n % 2) + j] for j in range(4)])
            pe.wait_ge(wo_in, 16)
            for n in range(2):
                turn(14 + n, [raw[:, 3, 4 * n + j] for j in range(4)])
            pe.wait_ge(bvT_ready, 1)
            pe.wait_ge(hi_ready, NTR)
            for c in range(CH):
                mm = nc.tensor.matmul(psA[0:KB].rearrange("p g b t -> p (g b t)")[:, P:2 * P],
                                      bvT[:, c:c + 1].to_broadcast([P, KB]), woT[:, c], start=(c == 0),
                                      stop=(c == CH - 1))
            mm.then_inc(bo_psum, 1)


def attention_loop(nc, sb, scope, x_sb, ctxT2, identb, ident, bnst,
                   xT2, wT2, woT, kron2, bqk3, bias_pick, bo3, bg3, ones3, beta, alpha, gamma2, least2,
                   arg, turns, whole, wave, emb2, vx2):
    def sem(name):
        return scope.enter_context(nc.semaphore(name))

    qT = sb("qT", [P, 2, CH, P], F32, scope)
    kT = sb("kT", [P, 2, CH, P], F32, scope)
    negmax = sb("negmax", [P, 2, HG], BF16, scope)
    prob = sb("prob", [P, 2, HG, P], F32, scope)
    gprob = sb("gprob", [P, 2, HG, P], F32, scope)
    gprob2 = sb("gprob2", [P, 2, 2, HG, P], F16, scope)
    rsum = sb("rsum", [P, 2, HG], F32, scope)
    att = sb("att", [P, 2, H0, DK], F32, scope)
    attT = sb("attT", [P, CH, P], F32, scope)

    def bank(name):
        return scope.enter_context(nc.psum_tensor(name, [P, HG, P], F32))

    psM, psG, psV = bank("psM"), bank("psG"), bank("psV")
    psS = [bank("psS0"), bank("psS1")]
    aux = [bank("aux0"), bank("aux1"), bank("aux2")]

    pool_gate = sem("pool_gate")
    qp_psum, q_ready, kp_psum, k_ready, vp_psum, vhi_ready, v_ready = (
        sem(n) for n in ("qp_psum", "q_ready", "kp_psum", "k_ready", "vp_psum", "vhi_ready", "v_ready"))
    max_psum, negmax_ready, score_psum, prob_ready, geo_psum, gprob_ready, gphi_ready, gplo_ready = (
        sem(n) for n in ("max_psum", "negmax_ready", "score_psum", "prob_ready", "geo_psum", "gprob_ready",
                         "gphi_ready", "gplo_ready"))
    pv_psum, rsum_ready, att_ready, attT_psum, attT_ready, op_psum, x1_ready, stat_ready = (
        sem(n) for n in ("pv_psum", "rsum_ready", "att_ready", "attT_psum", "attT_ready", "op_psum",
                         "x1_ready", "stat_ready"))
    dist_ready, square_ready, gamma_done, clip_ready, log_ready, turns_ready, whole_ready, frac_ready = (
        sem(n) for n in ("geo_dist_ready", "geo_square_ready", "geo_gamma_done", "geo_clip_ready",
                         "geo_log_ready", "geo_turns_ready", "geo_whole_ready", "geo_frac_ready"))
    wave_ready, emb_hi = sem("geo_wave_ready"), sem("geo_emb_hi")
    emb_lo_even, emb_lo_odd = sem("geo_emb_lo_even"), sem("geo_emb_lo_odd")

    def heads(u):
        first = 2 * HG * (u % 2) + u // 2
        return [first + 2 * j for j in range(HG)]

    def unit(a, u):
        return a[:, heads(u)[0]:heads(u)[-1] + 1:2]

    def made(b):
        return not (isinstance(b, int) and b >= B)

    def flat(a):
        return a.rearrange("p g m -> p (g m)")

    def pair_flat(a):
        return a.rearrange("p b g m -> p (b g m)")

    with nc.Block() as block:
        @block.gpsimd
        def _(pool):
            def gated():
                pool.sem_inc(pool_gate, 1)

            def square(g, par):
                pool.wait_ge(dist_ready, g - 1)
                gated()
                nc.gpsimd.tensor_tensor(arg[:, par], arg[:, par], arg[:, par], ALU.mult).then_inc(square_ready, 1)

            def low_emb(g, par):
                pool.wait_ge(emb_hi, g)
                gated()
                nc.gpsimd.tensor_tensor(emb2[:, par, 1], wave[:, par], emb2[:, par, 0],
                                        ALU.subtract).then_inc(emb_lo_odd, 2)

            def low_gprob(b, u):
                pool.wait_ge(gphi_ready, UN * b + u + 1)
                gated()
                nc.gpsimd.tensor_tensor(gprob2[:, u % 2, 1], gprob[:, u % 2], gprob2[:, u % 2, 0],
                                        ALU.subtract).then_inc(gplo_ready, 1)

            def slots(b, par):
                for u in range(UN):
                    if u == 0 and par == 0:
                        low_emb(b + 1, 1)
                    low_gprob(b, u)
                    if par == 0 and u in (0, 1) and made(b + 2):
                        square(b + 2 + u, u)

            over_batches(nc.gpsimd, slots)

        @block.tensor
        def _(pe):
            mm_ = nc.tensor.matmul

            def upper(a):
                return a.bitcast(BF16).rearrange("p (n two) -> p n two", two=2)[:, :, 1]

            def rows_of(h):
                return slice(DK * (h % 2), DK * (h % 2) + DK)

            def transposed_proj(k, src, b, half, into, done):
                mm_(aux[into][:], bqk3[:], bias_pick[:, CH * k + 4 * half:CH * k + 4 * half + 4], start=True,
                    stop=False, skip_group_check=True)
                for j in range(4):
                    c = 4 * half + j
                    for w_part, x_part in ((0, 0), (0, 1), (1, 0)):
                        mm = mm_(aux[into][:, j], wT2[:, k, w_part, c], src[:, x_part, b], start=False,
                                 stop=(j == 3 and w_part == 1), skip_group_check=True)
                mm.then_inc(done, 1)

            def q_proj(b, half, into):
                transposed_proj(0, xT2, b, half, into, qp_psum)

            def k_proj(b, half, into):
                transposed_proj(1, ctxT2, b, half, into, kp_psum)

            def v_proj(b, half, into):
                for n, (x_part, w_part) in enumerate(((0, 0), (0, 1), (1, 0))):
                    mm = mm_(aux[into][:], ctxT2[:, x_part, b], wT2[:, 2, w_part, 4 * half:4 * half + 4],
                             start=(n == 0), stop=(n == 2))
                mm.then_inc(vp_psum, 1)

            def maxima(par, u):
                for j, h in enumerate(heads(u)):
                    mm = mm_(psM[:, j], upper(qT[rows_of(h), par, h // 2]), upper(kT[rows_of(h), par, h // 2]),
                             start=True, stop=True)
                mm.then_inc(max_psum, 1)

            def scores(par, u):
                for j, h in enumerate(heads(u)):
                    mm_(psS[u % 2][:, j], kT[rows_of(h), par, h // 2], qT[rows_of(h), par, h // 2],
                        start=(j == 0), stop=False, skip_group_check=True)
                for j in range(HG):
                    mm = mm_(psS[u % 2][:, j], negmax[:, u % 2, j:j + 1].to_broadcast([P, P]), identb[:],
                             start=False, stop=(j == HG - 1), skip_group_check=True)
                mm.then_inc(score_psum, 1)

            def geometry(par, u):
                mm_(psG[:], ones3[:], unit(bg3, u).unsqueeze(2).to_broadcast([KB, HG, P]), start=True, stop=False, skip_group_check=True)
                for g in range(NG):
                    for e_part, w_part in ((0, 0), (0, 1), (1, 0)):
                        mm = mm_(psG[:, :, GN * g:GN * g + GN], emb2[:, par, e_part, g],
                                 unit(kron2[:, w_part], u), start=False,
                                 stop=(g == NG - 1 and e_part == 1), skip_group_check=True)
                mm.then_inc(geo_psum, 1)

            def pv(par, u):
                v = psV[:].rearrange("p a m -> p (a m)")
                for j, h in enumerate(heads(u)):
                    for p_part, v_part in ((0, 0), (0, 1), (1, 0)):
                        mm = mm_(v[:, j * (DK + 1):(j + 1) * (DK + 1)], gprob2[:, u % 2, p_part, j],
                                 vx2[:, par, v_part, h], start=(j == 0 and p_part + v_part == 0),
                                 stop=(j == HG - 1 and p_part == 1), skip_group_check=True)
                mm.then_inc(pv_psum, 1)

            def att_turn(par, half, into):
                for j in range(4):
                    c = 4 * half + j
                    mm = nc.tensor.transpose(aux[into][:, j], att[:, par, 2 * c:2 * c + 2], ident[:])
                mm.then_inc(attT_psum, 1)

            def out_proj(into):
                mm_(aux[into][:, 0], ones3[:], bo3[:], start=True, stop=False)
                for c in range(CH):
                    mm = mm_(aux[into][:, 0], attT[:, c], woT[:, c], start=False, stop=(c == CH - 1))
                mm.then_inc(op_psum, 1)

            def wait_pv(b, u):
                pe.wait_ge(v_ready, 2 * b + min(u, 1) + 1)
                pe.wait_ge(gplo_ready, UN * b + u + 1)
                after(pe, att_ready, UN * b + u)

            q_proj(0, 0, 2)
            q_proj(0, 1, 0)
            k_proj(0, 0, 1)
            pe.wait_ge(q_ready, 1)
            k_proj(0, 1, 2)
            pe.wait_ge(q_ready, 2)
            pe.wait_ge(k_ready, 2)
            maxima(0, 0)

            def slots(b, par):
                first, last = known(b, 0), known(b, B - 1)
                nxt = 1 - par
                for u in range(UN):
                    pe.wait_ge(negmax_ready, UN * b + u + 1)
                    after(pe, prob_ready, UN * b + u - 1)
                    if u == 0:
                        pe.wait_ge(k_ready, 2 * b + 2)
                        pe.wait_ge(q_ready, 2 * b + 2)
                    scores(par, u)
                    if u < UN - 1:
                        maxima(par, u + 1)
                    if u == 0:
                        after(pe, emb_lo_odd if par else emb_lo_even, b + 1 if par else b)
                    after(pe, gprob_ready, UN * b + u)
                    geometry(par, u)
                    if u > 0:
                        wait_pv(b, u - 1)
                        pv(par, u - 1)
                    elif not first:
                        wait_pv(b - 1, UN - 1)
                        pv(nxt, UN - 1)
                    if u == 0:
                        after(pe, x1_ready, b - 1)
                        v_proj(b, 0, 0)
                        pe.wait_ge(k_ready, 2 * b + 1)
                        v_proj(b, 1, 1)
                    if u == 1:
                        if not first:
                            pe.wait_ge(att_ready, UN * b)
                            pe.wait_ge(v_ready, 2 * b + 1)
                            att_turn(nxt, 0, 0)
                            pe.wait_ge(v_ready, 2 * b + 2)
                            att_turn(nxt, 1, 1)
                        if not last:
                            pe.wait_ge(k_ready, 2 * b + 2)
                            q_proj(b + 1, 0, 2)
                    if u == 2 and not last:
                        pe.wait_ge(v_ready, 2 * b + 2)
                        after(pe, attT_ready, 2 * b)
                        q_proj(b + 1, 1, 0)
                        k_proj(b + 1, 0, 1)
                        pe.wait_ge(q_ready, 2 * (b + 1) + 1)
                        k_proj(b + 1, 1, 2)
                    if u == 3 and not last:
                        pe.wait_ge(q_ready, 2 * (b + 1) + 2)
                        pe.wait_ge(k_ready, 2 * (b + 1) + 2)
                        maxima(nxt, 0)
                    if u == 3 and not first:
                        after(pe, attT_ready, 2 * b)
                        if not last:
                            pe.wait_ge(q_ready, 2 * (b + 1) + 2)
                        out_proj(0)

            over_batches(nc.tensor, slots)
            wait_pv(B - 1, UN - 1)
            pv((B - 1) % 2, UN - 1)
            pe.wait_ge(att_ready, UN * B)
            pe.wait_ge(x1_ready, B - 1)
            for half in range(2):
                att_turn((B - 1) % 2, half, half)
            pe.wait_ge(attT_ready, 2 * B)
            out_proj(0)

        @block.scalar
        def _(act):
            def q_out(b, par, half, frm):
                act.wait_ge(qp_psum, 2 * b + half + 1)
                nc.scalar.copy(qT[:, par, 4 * half:4 * half + 4], aux[frm][:]).then_inc(q_ready, 1)

            def v_hi(b, par, half):
                act.wait_ge(vp_psum, 2 * b + half + 1)
                after(act, pv_psum, UN * (b - 1))
                nc.scalar.copy(vx2[:, par, 0, 8 * half:8 * half + 8, 0:DK],
                               aux[half][:].rearrange("p a m -> p (a m)").rearrange("p (h e) -> p h e", e=DK)
                               ).then_inc(vhi_ready, 1)

            def attT_out(b, half):
                act.wait_ge(attT_psum, 2 * b + half + 1)
                after(act, op_psum, b)
                nc.scalar.copy(attT[:, 4 * half:4 * half + 4], aux[half][:]).then_inc(attT_ready, 1)

            def gprob_hi(b, u):
                act.wait_ge(gprob_ready, UN * b + u + 1)
                after(act, pv_psum, UN * b + u - 1)
                nc.scalar.copy(gprob2[:, u % 2, 0], gprob[:, u % 2]).then_inc(gphi_ready, 1)

            def logs(g, par):
                act.wait_ge(clip_ready, g - 1)
                nc.scalar.activation(arg[:, par], arg[:, par], ACT.Ln).then_inc(log_ready, 1)

            def log_cycles(g, par):
                act.wait_ge(log_ready, g - 1)
                after(act, frac_ready, g - 3)
                nc.scalar.activation(turns[:, par], arg[:, par], ACT.Copy, scale=CYCLES).then_inc(turns_ready, 1)

            def waves(g, par):
                act.wait_ge(frac_ready, g - 1)
                after(act, emb_lo_odd if par else emb_lo_even, g - 1 if par else g - 2)
                nc.scalar.activation(wave[:, par], whole[:, par], ACT.Sin, scale=-TURN).then_inc(wave_ready, 1)

            def high_emb(g, par):
                after(act, wave_ready, g - 1)
                after(act, geo_psum, UN * (g - 1))
                nc.scalar.copy(emb2[:, par, 0], wave[:, par]).then_inc(emb_hi, 1)

            nc.scalar.preload_act_table(ACT.Exp)
            q_out(0, 0, 0, 2)
            q_out(0, 0, 1, 0)

            def slots(b, par):
                first, last = known(b, 0), known(b, B - 1)
                for u in range(UN):
                    act.wait_ge(score_psum, UN * b + u + 1)
                    after(act, gprob_ready, UN * b + u - 1)
                    nc.scalar.activation(prob[:, u % 2], psS[u % 2][:], ACT.Exp,
                                         scale=DK ** -0.5 / W_UP ** 2).then_inc(prob_ready, 1)
                    if u == 0 and par == 0:
                        high_emb(b + 1, 1)
                    if u == 2 and not last:
                        q_out(b + 1, 1 - par, 1, 0)
                    if u == 3 and par == 0 and made(b + 2):
                        logs(b + 2, 0)
                        gprob_hi(b, u)
                        logs(b + 3, 1)
                        nc.scalar.preload_act_table(ACT.Exp)
                    elif u == 2 and par == 1 and made(b + 1):
                        waves(b + 1, 0)
                        gprob_hi(b, u)
                        waves(b + 2, 1)
                        nc.scalar.preload_act_table(ACT.Exp)
                    elif u == 3 and par == 1 and made(b + 1):
                        high_emb(b + 1, 0)
                        gprob_hi(b, u)
                    else:
                        gprob_hi(b, u)
                    if u == 0:
                        v_hi(b, par, 0)
                        v_hi(b, par, 1)
                    if u == 1:
                        if not first:
                            attT_out(b - 1, 0)
                            attT_out(b - 1, 1)
                        if not last:
                            after(act, score_psum, UN * b)
                            q_out(b + 1, 1 - par, 0, 2)
                    if par == 1 and u < 2 and made(b + 1):
                        log_cycles(b + 1 + u, u)

            over_batches(nc.scalar, slots)
            attT_out(B - 1, 0)
            attT_out(B - 1, 1)

        @block.vector
        def _(dve):
            v = nc.vector

            def neg_max(b, u):
                dve.wait_ge(max_psum, UN * b + u + 1)
                after(dve, score_psum, UN * b + u - 1)
                v.tensor_reduce(negmax[:, u % 2], psM[:], AX.X, ALU.max, negate=True).then_inc(negmax_ready, 1)

            def weigh(b, u):
                dve.wait_ge(prob_ready, UN * b + u + 1)
                dve.wait_ge(geo_psum, UN * b + u + 1)
                after(dve, gplo_ready, UN * b + u - 1)
                v.scalar_tensor_tensor(out=flat(gprob[:, u % 2]), in0=flat(psG[:]), scalar=1e-6 * G_UP,
                                       in1=flat(prob[:, u % 2]), op0=ALU.max,
                                       op1=ALU.mult).then_inc(gprob_ready, 1)

            def normalise(b, par, u):
                dve.wait_ge(pv_psum, UN * b + u + 1)
                got = psV[:].rearrange("p a m -> p (a m)")[:, 0:HG * (DK + 1)].rearrange("p (h e) -> p h e", h=HG)
                v.reciprocal(rsum[:, u % 2], got[:, :, DK]).then_inc(rsum_ready, 1)
                dve.wait_ge(rsum_ready, UN * b + u + 1)
                after(dve, attT_psum, 2 * b - 2)
                v.tensor_tensor(unit(att[:, par], u), got[:, :, 0:DK],
                                rsum[:, u % 2].unsqueeze(2).to_broadcast([P, HG, DK]),
                                ALU.mult).then_inc(att_ready, 1)

            def k_out(b, par, half, frm):
                dve.wait_ge(kp_psum, 2 * b + half + 1)
                v.tensor_copy(kT[:, par, 4 * half:4 * half + 4], aux[frm][:]).then_inc(k_ready, 1)

            def v_lo(b, par, half):
                dve.wait_ge(vhi_ready, 2 * b + half + 1)
                v.tensor_tensor(vx2[:, par, 1, 8 * half:8 * half + 8, 0:DK],
                                aux[half][:].rearrange("p a m -> p (a m)").rearrange("p (h e) -> p h e", e=DK),
                                vx2[:, par, 0, 8 * half:8 * half + 8, 0:DK], ALU.subtract).then_inc(v_ready, 1)

            def residual(b):
                dve.wait_ge(op_psum, b + 1)
                v.tensor_tensor(x_sb[:, b], x_sb[:, b], aux[0][:, 0], ALU.add).then_inc(x1_ready, 1)
                dve.wait_ge(x1_ready, b + 1)
                v.bn_stats(bnst[:, b], x_sb[:, b]).then_inc(stat_ready, 1)

            def distance(g, par):
                after(dve, turns_ready, g - 3)
                v.tensor_tensor(arg[:, par], beta[:, g].unsqueeze(1).to_broadcast([P, NG, P]),
                                alpha[:, g].unsqueeze(2).to_broadcast([P, NG, P]),
                                ALU.subtract).then_inc(dist_ready, 1)

            def clip(g, par):
                dve.wait_ge(square_ready, g - 1)
                v.tensor_tensor(arg[:, par], arg[:, par], gamma2[:, g].unsqueeze(2).to_broadcast([P, NG, P]),
                                ALU.mult).then_inc(gamma_done, 1)
                dve.wait_ge(gamma_done, g - 1)
                v.tensor_scalar(flat(arg[:, par]), flat(arg[:, par]), least2[:, 0:1], None,
                                ALU.max).then_inc(clip_ready, 1)

            def low_emb(g, par):
                dve.wait_ge(emb_hi, g)
                v.tensor_tensor(emb2[:, par, 1], wave[:, par], emb2[:, par, 0],
                                ALU.subtract).then_inc(emb_lo_even, 2)

            def fraction(g, par):
                dve.wait_ge(log_ready, g - 1)
                after(dve, wave_ready, g - 3)
                v.tensor_scalar(flat(whole[:, par]), flat(arg[:, par]), CYCLES, ROUND, ALU.mult,
                                ALU.add).then_inc(whole_ready, 1)
                dve.wait_ge(whole_ready, g - 1)
                dve.wait_ge(turns_ready, g - 1)
                v.scalar_tensor_tensor(out=flat(whole[:, par]), in0=flat(whole[:, par]), scalar=ROUND,
                                       in1=flat(turns[:, par]), op0=ALU.subtract,
                                       op1=ALU.subtract).then_inc(frac_ready, 1)

            k_out(0, 0, 0, 1)
            k_out(0, 0, 1, 2)
            neg_max(0, 0)

            def slots(b, par):
                first, last = known(b, 0), known(b, B - 1)
                for u in range(UN):
                    if u < UN - 1:
                        neg_max(b, u + 1)
                    weigh(b, u)
                    if u == 3 and not last:
                        neg_max(b + 1, 0)
                    if u > 0:
                        normalise(b, par, u - 1)
                    elif not first:
                        normalise(b - 1, 1 - par, UN - 1)
                    if u == 0:
                        v_lo(b, par, 0)
                        v_lo(b, par, 1)
                    if u == 2 and not last:
                        k_out(b + 1, 1 - par, 0, 1)
                        k_out(b + 1, 1 - par, 1, 2)
                    if u == 3 and not first:
                        residual(b - 1)
                    if par == 0 and made(b + 2):
                        if u < 2:
                            distance(b + 2 + u, u)
                        if u in (1, 2):
                            clip(b + 1 + u, u - 1)
                    if par == 1 and u == 3 and made(b + 1):
                        low_emb(b + 1, 0)
                    if par == 1 and u < 2 and made(b + 1):
                        fraction(b + 1 + u, u)

            over_batches(nc.vector, slots)
            normalise(B - 1, (B - 1) % 2, UN - 1)
            residual(B - 1)


def layernorm_all(v, act_sem_pair, order, dve, x_sb, bnst, mv, rstd, eps=LN_EPS):
    asked, given = act_sem_pair
    for b in range(B):
        order.add(v.bn_aggr(mv[:, b], bnst[:, b]))
    order.sync()
    v.tensor_scalar(rstd[:], mv[:, :, 1], eps, None, ALU.add).then_inc(asked, 1)
    dve.wait_ge(given, 1)
    order.then(v.reciprocal(rstd[:], rstd[:]))


def ffn_phase(nc, T, sb, scope, x_sb, ident, identb, bnst, mv, rstd):
    TG = 4
    NT = B // TG

    def sem(name):
        return scope.enter_context(nc.semaphore(name))

    w1 = sb("w1", [P, FC, P], F32, scope)
    w2 = sb("w2", [P, FC, P], F32, scope)
    q1 = sb("q1", [P, FC, P], BF16, scope)
    q2 = sb("q2", [P, FC, P], BF16, scope)
    q1T = sb("q1T", [P, FC, P], BF16, scope)
    q2T = sb("q2T", [P, FC, P], BF16, scope)
    b1 = sb("b1", [P, FC], F32, scope)
    b2 = sb("b2", [P, 1], F32, scope)
    ws = sb("ws", [P, FC + 1], F32, scope)
    wr = sb("wr", [P, FC + 1], F32, scope)
    sc1 = sb("sc1", [P, FC], F32, scope)
    rc1 = sb("rc1", [P, FC], F32, scope)
    sc2 = sb("sc2", [P, 2], F32, scope)
    xn = sb("xn2", [P, B, P], F32, scope)
    xq = sb("xq", [P, B, P], BF16, scope)
    xf = sb("xf", [P, 2, TG * P], F32, scope)
    hid = sb("hid", [P, NT, FC, TG * P], F32, scope)
    hq = sb("hq", [P, NT, FC, TG * P], BF16, scope)
    hmax = sb("hmax", [P, NT * FC], F32, scope)
    top = sb("top", [P, 2], F32, scope)
    topall = sb("topall", [P, 2], F32, scope)
    inv = sb("inv", [P, 2], F32, scope)
    step = sb("step", [P, 2], F32, scope)
    row2 = sb("row2", [P, 2, P], F32, scope)

    psT = [scope.enter_context(nc.psum_tensor(f"psFT{i}", [P, TG, P], F32)) for i in range(2)]
    psW = scope.enter_context(nc.psum_tensor("psFW", [P, FC, 2 * P], BF16))
    psH = [scope.enter_context(nc.psum_tensor(f"psFH{i}", [P, TG * P], F32)) for i in range(2)]
    psY = [scope.enter_context(nc.psum_tensor(f"psFY{i}", [P, TG, P], F32)) for i in range(2)]
    psR = scope.enter_context(nc.psum_tensor("psFR", [P, 2, P], F32))

    w_in, dve_order, var_ready, std_ready, xn_ready = (
        sem(n) for n in ("ffn_w_in", "ffn_dve_order", "ffn_var_ready", "ffn_std_ready", "ffn_xn_ready"))
    top_ready, topall_ready, inv_ready, q_ready, qT_psum, qT_ready = (
        sem(n) for n in ("ffn_top_ready", "ffn_topall_ready", "ffn_inv_ready", "ffn_q_ready", "ffn_qT_psum",
                         "ffn_qT_ready"))
    xT_psum, xf_ready, xq_ready, h_psum, hid_ready, sc1_ready = (
        sem(n) for n in ("ffn_xT_psum", "ffn_xf_ready", "ffn_xq_ready", "ffn_h_psum", "ffn_hid_ready",
                         "ffn_sc1_ready"))
    hr_ready, hq_ready, y_psum, sc2_ready, row_psum, y_done = (
        sem(n) for n in ("ffn_hr_ready", "ffn_hq_ready", "ffn_y_psum", "ffn_sc2_ready", "ffn_row_psum",
                         "ffn_y_done"))

    with nc.Block() as block:
        @block.sync
        def _(sp):
            sp.dma_start(w1[:], T["L0_ffn_w1"].rearrange("(c p) d -> p c d", p=P)).then_inc(w_in, 16)
            sp.dma_start(w2[:], T["L0_ffn_w2"].rearrange("p (c d) -> p c d", d=P)).then_inc(w_in, 16)
            with nc.allow_non_contiguous_dma(reason="640 words of biases, once"):
                sp.dma_start(b1[:], T["L0_ffn_b1"].rearrange("(c p) -> p c", p=P)).then_inc(w_in, 16)
                sp.dma_start(b2[:], T["L0_ffn_b2"].rearrange("(p o) -> p o", o=1)).then_inc(w_in, 16)

        @block.gpsimd
        def _(pool):
            for k in range(2):
                pool.wait_ge(top_ready, k + 1)
                nc.gpsimd.partition_all_reduce(topall[:, k:k + 1], top[:, k:k + 1], P, RMAX).then_inc(topall_ready, 1)

        @block.scalar
        def _(act):
            act.wait_ge(var_ready, 1)
            nc.scalar.activation(rstd[:], rstd[:], ACT.Sqrt).then_inc(std_ready, 1)
            act.wait_ge(qT_psum, 1)
            nc.scalar.copy(q1T[:], psW[:, :, 0:P]).then_inc(qT_ready, 1)
            act.wait_ge(qT_psum, 2)
            nc.scalar.copy(q2T[:], psW[:, :, 0:P]).then_inc(qT_ready, 1)
            act.wait_ge(inv_ready, 1)
            for t in range(NT):
                act.wait_ge(xT_psum, t + 1)
                if t >= 2:
                    act.wait_ge(xq_ready, t - 1)
                nc.scalar.activation(xf[:, t % 2], psT[t % 2][:].rearrange("p b d -> p (b d)"), ACT.Relu,
                                     scale=inv[:, 0:1]).then_inc(xf_ready, 1)
            act.wait_ge(sc1_ready, 1)
            for t in range(NT):
                for c in range(FC):
                    n = FC * t + c
                    act.wait_ge(h_psum, n + 1)
                    nc.scalar.activation(hid[:, t, c], psH[n % 2][:], ACT.Relu, bias=b1[:, c:c + 1],
                                         scale=sc1[:, c:c + 1]).then_inc(hid_ready, 1)

        @block.vector
        def _(dve):
            v = nc.vector
            order = Order(dve, dve_order)
            layernorm_all(v, (var_ready, std_ready), order, dve, x_sb, bnst, mv, rstd)
            for b in range(B):
                v.tensor_scalar(xn[:, b], x_sb[:, b], mv[:, b, 0:1], rstd[:, b:b + 1],
                                ALU.subtract, ALU.mult).then_inc(xn_ready, 1)
            dve.wait_ge(xn_ready, B)
            v.tensor_reduce(top[:, 0:1], xn[:], AX.XY, ALU.max).then_inc(top_ready, 1)

            dve.wait_ge(w_in, 16 * 4)
            order.add(v.tensor_reduce(ws[:, 0:FC], w1[:], AX.X, ALU.max, apply_absolute_value=True))
            order.add(v.tensor_reduce(ws[:, FC:], w2[:], AX.XY, ALU.max, apply_absolute_value=True))
            order.sync()
            order.then(v.tensor_scalar(ws[:], ws[:], Q_EPS, 1.0 / 127.0, ALU.max, ALU.mult))
            order.then(v.reciprocal(wr[:], ws[:]))
            for c in range(FC):
                order.add(v.tensor_scalar(w1[:, c], w1[:, c], wr[:, c:c + 1], ROUND, ALU.mult, ALU.add))
            order.add(v.tensor_scalar(w2[:], w2[:], wr[:, FC:], ROUND, ALU.mult, ALU.add))
            order.sync()
            for w in (w1, w2):
                order.add(v.tensor_scalar(w[:], w[:], ROUND, -128.0, ALU.subtract, ALU.max))
            order.sync()
            for w, q in ((w1, q1), (w2, q2)):
                v.tensor_scalar(q[:], w[:], 127.0, None, ALU.min).then_inc(q_ready, 1)

            def scales(k):
                dve.wait_ge(topall_ready, k + 1)
                order.then(v.tensor_scalar(step[:, k:k + 1], topall[:, k:k + 1], Q_EPS, 1.0 / 255.0,
                                           ALU.max, ALU.mult))
                order.then(v.reciprocal(inv[:, k:k + 1], step[:, k:k + 1]))
                v.engine_nop().then_inc(inv_ready, 1)

            def quant_bias(bias, sc, rc):
                order.then(v.reciprocal(rc, sc))
                order.then(v.tensor_tensor(bias, bias, rc, ALU.mult))
                order.then(v.tensor_scalar(bias, bias, ROUND, None, ALU.add))
                order.then(v.tensor_scalar(bias, bias, ROUND, None, ALU.subtract))
                order.then(v.tensor_tensor(bias, bias, sc, ALU.mult))

            scales(0)
            order.then(v.tensor_scalar(sc1[:], ws[:, 0:FC], step[:, 0:1], None, ALU.mult))
            quant_bias(b1[:], sc1[:], rc1[:])
            v.engine_nop().then_inc(sc1_ready, 1)
            for t in range(NT):
                dve.wait_ge(xf_ready, t + 1)
                order.then(v.tensor_scalar(xf[:, t % 2], xf[:, t % 2], 255.0, ROUND, ALU.min, ALU.add))
                v.tensor_scalar(xq[:, TG * t:TG * t + TG].rearrange("p b d -> p (b d)"), xf[:, t % 2], ROUND,
                                None, ALU.subtract).then_inc(xq_ready, 1)
            for n in range(NT * FC):
                dve.wait_ge(hid_ready, n + 1)
                order.add(v.tensor_reduce(hmax[:, n:n + 1], hid[:, n // FC, n % FC], AX.X, ALU.max))
            order.sync()
            v.tensor_reduce(top[:, 1:2], hmax[:], AX.X, ALU.max).then_inc(top_ready, 1)
            scales(1)
            order.then(v.tensor_scalar(sc2[:, 0:1], ws[:, FC:], step[:, 1:2], None, ALU.mult))
            order.then(v.tensor_copy(sc2[:, 1:2], b2[:]))
            quant_bias(sc2[:, 1:2], sc2[:, 0:1], rc1[:, 0:1])
            v.engine_nop().then_inc(sc2_ready, 1)
            for t in range(NT):
                for c in range(FC):
                    v.tensor_scalar(hid[:, t, c], hid[:, t, c], inv[:, 1:2], ROUND, ALU.mult,
                                    ALU.add).then_inc(hr_ready, 1)
                dve.wait_ge(hr_ready, FC * (t + 1))
                v.tensor_scalar(hq[:, t], hid[:, t], ROUND, 255.0, ALU.subtract, ALU.min).then_inc(hq_ready, 1)
            dve.wait_ge(row_psum, 1)
            order.then(v.tensor_copy(row2[:], psR[:]))
            for t in range(NT):
                xs = x_sb[:, TG * t:TG * t + TG]
                dve.wait_ge(y_psum, t + 1)
                order.add(v.tensor_tensor(xn[:, TG * t:TG * t + TG], psY[t % 2][:],
                                          row2[:, 0].unsqueeze(1).to_broadcast([P, TG, P]), ALU.mult))
                order.add(v.tensor_tensor(xs, xs, row2[:, 1].unsqueeze(1).to_broadcast([P, TG, P]), ALU.add))
                order.sync()
                v.tensor_tensor(xs, xs, xn[:, TG * t:TG * t + TG], ALU.add).then_inc(y_done, 1)
                dve.wait_ge(y_done, t + 1)
                for b in range(TG * t, TG * t + TG):
                    order.add(v.bn_stats(bnst[:, b], x_sb[:, b]))

        @block.tensor
        def _(pe):
            mm_ = nc.tensor.matmul
            for k, q in enumerate((q1, q2)):
                pe.wait_ge(q_ready, k + 1)
                if k:
                    pe.wait_ge(qT_ready, k)
                for c in range(FC):
                    mm = nc.tensor.transpose(psW[:, c, 0:P], q[:, c], identb[:])
                mm.then_inc(qT_psum, 1)
            for t in range(NT):
                pe.wait_ge(xn_ready, TG * (t + 1))
                if t >= 2:
                    pe.wait_ge(xf_ready, t - 1)
                for j in range(TG):
                    mm = nc.tensor.transpose(psT[t % 2][:, j], xn[:, TG * t + j], ident[:])
                mm.then_inc(xT_psum, 1)
            pe.wait_ge(qT_ready, 2)
            for t in range(NT):
                pe.wait_ge(xq_ready, t + 1)
                for c in range(FC):
                    n = FC * t + c
                    if n >= 2:
                        pe.wait_ge(hid_ready, n - 1)
                    mm_(psH[n % 2][:], q1T[:, c], xq[:, TG * t:TG * t + TG], start=True,
                        stop=True).then_inc(h_psum, 1)
            pe.wait_ge(sc2_ready, 1)
            for k in range(2):
                mm = mm_(psR[:, k], sc2[:, k:k + 1].to_broadcast([P, P]), ident[:], start=True, stop=True)
            mm.then_inc(row_psum, 1)
            for t in range(NT):
                pe.wait_ge(hq_ready, t + 1)
                if t >= 2:
                    pe.wait_ge(y_done, t - 1)
                for j in range(TG):
                    for c in range(FC):
                        mm = mm_(psY[t % 2][:, j], hq[:, t, c, j * P:(j + 1) * P], q2T[:, c],
                                 start=(c == 0), stop=(c == FC - 1))
                mm.then_inc(y_psum, 1)


def mlstm_phase(nc, T, sb, scope, x_sb, ctx_sb, ctxT2, ident, identb, bnst, mv, rstd):
    G = 2
    GH = H1 // G
    VW = HW1 + 1
    PARTS = ((0, 0), (0, 1), (1, 0))

    def sem(name):
        return scope.enter_context(nc.semaphore(name))

    xn = sb("xn3", [P, B, P], F32, scope)
    qT2 = sb("qT2", [P, 2, B, P], F16, scope)
    gk = sb("gk", [P, 3, 2, H1], F32, scope)
    gk2 = sb("gk2", [P, 2, 3, 2 * H1], F16, scope)
    gb = sb("gb", [P, 2, H1], F32, scope)
    gates = sb("gates", [P, 2, B, H1], F32, scope)
    low = sb("low", [P, P], F32, scope)
    soft = sb("soft", [P, P], F32, scope)
    zeros = sb("zeros", [P, P], F32, scope)
    ones = sb("ones", [P, P], F32, scope)
    csum = sb("csum", [P, P], F32, scope)
    gain = sb("gain", [P, P], F32, scope)
    peak = sb("peak", [P, P], F32, scope)
    guard = sb("guard", [P, P], F32, scope)
    peak3 = sb("peak3", [P, NSPLIT, P], BF16, scope)
    gainT = sb("gainT", [P, B, H1], F32, scope)
    eguard = sb("eguard", [P, B, H1], F32, scope)
    negid = sb("negid", [P, P], BF16, scope)
    future = sb("future", [P, P], BF16, scope)
    headm = sb("headm", [P, H1], F32, scope)
    bias_now = sb("bias_now", [P, 2, H1], F32, scope)
    qm2 = sb("qm2", [P, 2, 2, H1, P], F16, scope)
    v2 = sb("v2", [P, 2, B, H1, VW], F16, scope)
    decay = sb("decay", [P, G, GH, P], F32, scope)
    cmat = sb("cmat", [P, 2, H1, P], F32, scope)
    cmat2 = sb("cmat2", [P, 2, 2, H1, P], F16, scope)
    num = sb("num", [P, B, H1, VW], F32, scope)
    square = sb("square", [P, 2, H1, HW1], F32, scope)
    msq = sb("msq", [P, B, H1], F32, scope)
    factor = sb("factor", [P, B, H1], F32, scope)
    tmp = sb("tmp3", [P, B, H1], F32, scope)

    with ExitStack() as prep, nc.Block() as block:
        psT = [prep.enter_context(nc.psum_tensor(f"psMT{i}", [P, 4, P], F32)) for i in range(2)]
        psI = prep.enter_context(nc.psum_tensor("psMI", [P, B, 2, H1], F32))
        psF = prep.enter_context(nc.psum_tensor("psMF", [P, 2, P], F32))
        psE = prep.enter_context(nc.psum_tensor("psME", [P, 2, P], F32))
        w_in, dve_order, pool_order, var_ready, std_ready, xn_ready = (
            sem(n) for n in ("ml_w_in", "ml_dve_order", "ml_pool_order", "ml_var_ready", "ml_std_ready",
                             "ml_xn_ready"))
        qT_psum, qhi_ready, qlo_ready, gk_ready, gate_psum, gates_ready, gatesT_psum = (
            sem(n) for n in ("ml_qT_psum", "ml_qhi_ready", "ml_qlo_ready", "ml_gk_ready", "ml_gate_psum",
                             "ml_gates_ready", "ml_gatesT_psum"))
        abs_ready, soft_ready, gain_ready, guard_ready, gainT_psum, guard_psum, eg_ready, vhi_ready = (
            sem(n) for n in ("ml_abs_ready", "ml_soft_ready", "ml_gain_ready", "ml_guard_ready",
                             "ml_gainT_psum", "ml_guard_psum", "ml_eg_ready", "ml_vhi_ready"))

        @block.sync
        def _(sp):
            for k, name in enumerate(("L1_xattn_igate", "L1_xattn_fgate")):
                with nc.allow_non_contiguous_dma(reason="small gate weights, once"):
                    sp.dma_start(gk[:, :, k], T[name + "_kernel"].rearrange("(s p) h -> p s h", p=P)).then_inc(w_in, 16)
                sp.dma_start(gb[:, k], T[name + "_bias"].rearrange("(o h) -> o h", o=1)
                             .to_broadcast([P, H1])).then_inc(w_in, 16)

        @block.gpsimd
        def _(pool):
            order = Order(pool, pool_order)
            g = nc.gpsimd
            order.add(g.memset(future[:], MASKED))
            order.add(g.memset(headm[:], HW1 ** -0.5))
            order.add(g.memset(negid[:], 0.0))
            order.add(g.memset(v2[:, 0, :, :, HW1:], 1.0))
            order.add(g.memset(v2[:, 1, :, :, HW1:], 0.0))
            order.sync()
            order.add(g.affine_select(out=negid[:], in_=negid[:], compare_op=ALU.not_equal, fill=-1.0,
                                      base=0, pattern=[[-1, P]], channel_multiplier=1))
            order.add(g.affine_select(out=future[:], in_=future[:], compare_op=ALU.is_gt, fill=0.0,
                                      base=0, pattern=[[-1, P]], channel_multiplier=1))
            order.then(g.affine_select(out=headm[:], in_=headm[:], compare_op=ALU.is_ge, fill=0.0,
                                       base=0, pattern=[[-HW1, H1]], channel_multiplier=1))
            order.add(g.affine_select(out=headm[:], in_=headm[:], compare_op=ALU.is_ge, fill=0.0,
                                      base=HW1 - 1, pattern=[[HW1, H1]], channel_multiplier=-1))
            pool.wait_ge(vhi_ready, 1)
            order.add(g.tensor_tensor(v2[:, 1, :, :, 0:HW1], ctx_sb[:].rearrange("p b (h e) -> p b h e", h=H1),
                                      v2[:, 0, :, :, 0:HW1], ALU.subtract))

        @block.scalar
        def _(act):
            nc.scalar.copy(v2[:, 0, :, :, 0:HW1],
                           ctx_sb[:].rearrange("p b (h e) -> p b h e", h=H1)).then_inc(vhi_ready, 1)
            act.wait_ge(var_ready, 1)
            nc.scalar.activation(rstd[:], rstd[:], ACT.Sqrt).then_inc(std_ready, 1)
            nc.scalar.preload_act_table(ACT.Exp)
            for t in range(4):
                act.wait_ge(qT_psum, t + 1)
                nc.scalar.copy(qT2[:, 0, 4 * t:4 * t + 4], psT[t % 2][:]).then_inc(qhi_ready, 1)
            act.wait_ge(abs_ready, 1)
            nc.scalar.activation(soft[:], soft[:], ACT.Exp, scale=-1.0).then_inc(soft_ready, 1)
            act.wait_ge(soft_ready, 1)
            nc.scalar.activation(soft[:], soft[:], ACT.Ln, bias=1.0).then_inc(soft_ready, 1)
            nc.scalar.preload_act_table(ACT.Exp)
            act.wait_ge(guard_psum, 1)
            nc.scalar.activation(eguard[:].rearrange("p b h -> p (b h)"), psE[:, 1], ACT.Exp,
                                 scale=-1.0).then_inc(eg_ready, 1)

        @block.vector
        def _(dve):
            v = nc.vector
            order = Order(dve, dve_order)
            layernorm_all(v, (var_ready, std_ready), order, dve, x_sb, bnst, mv, rstd)
            for b in range(B):
                v.tensor_scalar(xn[:, b], x_sb[:, b], mv[:, b, 0:1], rstd[:, b:b + 1],
                                ALU.subtract, ALU.mult).then_inc(xn_ready, 1)
            order.add(v.memset(zeros[:], 0.0))
            order.add(v.memset(ones[:], 1.0))
            dve.wait_ge(w_in, 16 * 4)
            flat_gk = gk[:].rearrange("p s k h -> p s (k h)")
            order.then(v.tensor_scalar(gk2[:, 0], flat_gk, W_UP, None, ALU.mult))
            v.scalar_tensor_tensor(out=gk2[:, 1], in0=flat_gk, scalar=W_UP, in1=gk2[:, 0], op0=ALU.mult,
                                   op1=ALU.subtract).then_inc(gk_ready, 1)
            for t in range(4):
                dve.wait_ge(qhi_ready, t + 1)
                v.tensor_tensor(qT2[:, 1, 4 * t:4 * t + 4], psT[t % 2][:], qT2[:, 0, 4 * t:4 * t + 4],
                                ALU.subtract).then_inc(qlo_ready, 1)
            dve.wait_ge(gate_psum, 1)
            for k in range(2):
                v.scalar_tensor_tensor(out=gates[:, k], in0=psI[:, :, k], scalar=1.0 / W_UP,
                                       in1=gb[:, k].unsqueeze(1).to_broadcast([P, B, H1]), op0=ALU.mult,
                                       op1=ALU.add).then_inc(gates_ready, 1)
            dve.wait_ge(gatesT_psum, 1)
            order.then(v.tensor_scalar(low[:], psF[:, 1], 0.0, None, ALU.min))
            v.scalar_tensor_tensor(out=soft[:], in0=low[:], scalar=-2.0, in1=psF[:, 1], op0=ALU.mult,
                                   op1=ALU.add).then_inc(abs_ready, 1)
            dve.wait_ge(soft_ready, 2)
            order.then(v.tensor_tensor(low[:], low[:], soft[:], ALU.subtract))
            order.then(v.tensor_tensor_scan(csum[:], ones[:], low[:], 0.0, ALU.mult, ALU.add))
            v.tensor_tensor(gain[:], psF[:, 0], csum[:], ALU.subtract).then_inc(gain_ready, 1)
            dve.wait_ge(gain_ready, 1)
            order.then(v.tensor_tensor_scan(peak[:], zeros[:], gain[:], MASKED, ALU.add, ALU.max))
            v.tensor_tensor(guard[:], csum[:], peak[:], ALU.add).then_inc(guard_ready, 1)
            dve.wait_ge(guard_ready, 1)
            for part in range(NSPLIT):
                order.then(v.tensor_copy(peak3[:, part], peak[:]))
                if part < NSPLIT - 1:
                    order.then(v.tensor_tensor(peak[:], peak[:], peak3[:, part], ALU.subtract))
            dve.wait_ge(gainT_psum, 1)
            dve.wait_ge(eg_ready, 1)
            order.then(v.tensor_copy(gainT[:].rearrange("p b h -> p (b h)"), psE[:, 0]))

        @block.tensor
        def _(pe):
            mm_ = nc.tensor.matmul
            for t in range(4):
                pe.wait_ge(xn_ready, 4 * t + 4)
                if t >= 2:
                    pe.wait_ge(qlo_ready, t - 1)
                for j in range(4):
                    mm = nc.tensor.transpose(psT[t % 2][:, j], xn[:, 4 * t + j], ident[:])
                mm.then_inc(qT_psum, 1)
            pe.wait_ge(gk_ready, 1)
            pe.wait_ge(qlo_ready, 4)
            for b in range(B):
                for s, src in enumerate((ctxT2, ctxT2, qT2)):
                    for x_part, w_part in PARTS:
                        mm = mm_(psI[:, b].rearrange("p k h -> p (k h)"), src[:, x_part, b],
                                 gk2[:, w_part, (1, 2, 0)[s]], start=(b == 0 and s == 0 and x_part + w_part == 0),
                                 stop=(b == B - 1 and s == 2 and x_part == 1), skip_group_check=True)
            mm.then_inc(gate_psum, 1)
            pe.wait_ge(gates_ready, 2)
            for k in range(2):
                mm = nc.tensor.transpose(psF[:, k], gates[:, k].rearrange("p b h -> p (b h)"), ident[:])
            mm.then_inc(gatesT_psum, 1)
            pe.wait_ge(gain_ready, 1)
            nc.tensor.transpose(psE[:, 0], gain[:], ident[:]).then_inc(gainT_psum, 1)
            pe.wait_ge(guard_ready, 1)
            nc.tensor.transpose(psE[:, 1], guard[:], ident[:]).then_inc(guard_psum, 1)

    with ExitStack() as loop, nc.Block() as block:
        psS = [loop.enter_context(nc.psum_tensor(f"psMS{i}", [P, GH, P], F32)) for i in range(G)]
        psA = [loop.enter_context(nc.psum_tensor(f"psMA{i}", [P, GH, P], F32)) for i in range(G)]
        psN = loop.enter_context(nc.psum_tensor("psMN", [P, H1, VW], F32))
        gate_, staged, bias_ready, s_psum, a_psum, d_ready, c_ready, chi_ready, clo_ready, n_psum, n_ready = (
            sem(n) for n in ("ml_pool_gate", "ml_staged", "ml_bias_ready", "ml_s_psum", "ml_a_psum", "ml_d_ready",
                             "ml_c_ready", "ml_chi_ready", "ml_clo_ready", "ml_n_psum", "ml_n_ready"))
        sq_ready, ms_ready, f_order, var_asked, std_given, x_ready = (
            sem(n) for n in ("ml_sq_ready", "ml_ms_ready", "ml_f_order", "ml_var_asked", "ml_std_given",
                             "ml_x_ready"))

        @block.gpsimd
        def _(pool):
            def stage(b, par):
                after(pool, s_psum, 2 * b - 2)
                pool.sem_inc(gate_, 1)
                for part in range(2):
                    nc.gpsimd.tensor_tensor(qm2[:, par, part], qT2[:, part, b].unsqueeze(1).to_broadcast([P, H1, P]),
                                            headm[:].unsqueeze(2).to_broadcast([P, H1, P]),
                                            ALU.mult).then_inc(staged, 1)
            over_batches(nc.gpsimd, stage)

        @block.tensor
        def _(pe):
            mm_ = nc.tensor.matmul

            def values(b, par):
                pe.wait_ge(clo_ready, 2 * b + 2)
                after(pe, n_ready, b)
                for h in range(H1):
                    for c_part, v_part in PARTS:
                        mm = mm_(psN[:, h], cmat2[:, par, c_part, h], v2[:, v_part, b, h],
                                 start=(h == 0 and c_part + v_part == 0), stop=(h == H1 - 1 and c_part == 1),
                                 skip_group_check=True)
                mm.then_inc(n_psum, 1)

            def slots(b, par):
                for g in range(G):
                    after(pe, d_ready, 2 * b + g - 1)
                    mm_(psA[g][:], identb[:], future[:].unsqueeze(1).to_broadcast([P, GH, P]), start=True,
                        stop=False, skip_group_check=True)
                    for j in range(GH):
                        row = H1 * b + GH * g + j
                        pick_row = negid[:, row:row + 1] if isinstance(b, int) else negid[:, bass.ds(row, 1)]
                        for part in range(NSPLIT):
                            mm = mm_(psA[g][:, j], pick_row.to_broadcast([P, P]), peak3[:, part], start=False,
                                     stop=(j == GH - 1 and part == NSPLIT - 1), skip_group_check=True)
                    mm.then_inc(a_psum, 1)
                pe.wait_ge(staged, 2 * b + 2)
                for g in range(G):
                    after(pe, c_ready, 2 * b + g - 1)
                    for k_part, q_part in PARTS:
                        mm = mm_(psS[g][:], ctxT2[:, k_part, b], qm2[:, par, q_part, GH * g:GH * g + GH],
                                 start=(k_part + q_part == 0), stop=(k_part == 1))
                    mm.then_inc(s_psum, 1)
                if not known(b, 0):
                    values(b - 1, 1 - par)

            over_batches(nc.tensor, slots)
            values(B - 1, (B - 1) % 2)

        @block.scalar
        def _(act):
            def high(b, par, g):
                act.wait_ge(c_ready, 2 * b + g + 1)
                after(act, n_psum, b - 1)
                nc.scalar.copy(cmat2[:, par, 0, GH * g:GH * g + GH],
                               cmat[:, par, GH * g:GH * g + GH]).then_inc(chi_ready, 1)

            def sums(b):
                act.wait_ge(n_psum, b + 1)
                nc.scalar.copy(num[:, b], psN[:]).then_inc(n_ready, 1)

            def slots(b, par):
                act.wait_ge(bias_ready, b + 1)
                for g in range(G):
                    act.wait_ge(a_psum, 2 * b + g + 1)
                    after(act, c_ready, 2 * b + g - 1)
                    for j in range(GH):
                        h = GH * g + j
                        act_ = nc.scalar.activation(decay[:, g, j], psA[g][:, j], ACT.Exp,
                                                    bias=bias_now[:, par, h:h + 1])
                    act_.then_inc(d_ready, 1)
                for g in range(G):
                    high(b, par, g)
                if not known(b, 0):
                    sums(b - 1)

            over_batches(nc.scalar, slots)
            sums(B - 1)
            act.wait_ge(var_asked, 1)
            nc.scalar.activation(tmp[:], tmp[:], ACT.Sqrt).then_inc(std_given, 1)

        @block.vector
        def _(dve):
            v = nc.vector

            def bias(b, par):
                after(dve, d_ready, 2 * b - 2)
                v.tensor_copy(bias_now[:, par], gainT[:, b]).then_inc(bias_ready, 1)

            def squares(b, par):
                dve.wait_ge(n_ready, b + 1)
                v.tensor_tensor(square[:, par], num[:, b, :, 0:HW1], num[:, b, :, 0:HW1],
                                ALU.mult).then_inc(sq_ready, 1)
                dve.wait_ge(sq_ready, b + 1)
                v.tensor_reduce(msq[:, b], square[:, par], AX.X, ALU.add).then_inc(ms_ready, 1)

            bias(0, 0)

            def slots(b, par):
                if not known(b, B - 1):
                    bias(b + 1, 1 - par)
                for g in range(G):
                    dve.wait_ge(d_ready, 2 * b + g + 1)
                    dve.wait_ge(s_psum, 2 * b + g + 1)
                    v.tensor_tensor(cmat[:, par, GH * g:GH * g + GH], psS[g][:], decay[:, g],
                                    ALU.mult).then_inc(c_ready, 1)
                for g in range(G):
                    dve.wait_ge(chi_ready, 2 * b + g + 1)
                    v.tensor_tensor(cmat2[:, par, 1, GH * g:GH * g + GH], cmat[:, par, GH * g:GH * g + GH],
                                    cmat2[:, par, 0, GH * g:GH * g + GH], ALU.subtract).then_inc(clo_ready, 1)
                if not known(b, 0):
                    squares(b - 1, 1 - par)

            over_batches(nc.vector, slots)
            squares(B - 1, (B - 1) % 2)
            dve.wait_ge(ms_ready, B)
            order = Order(dve, f_order)
            total = num[:, :, :, HW1]
            order.then(v.scalar_tensor_tensor(out=factor[:], in0=total, scalar=-1.0, in1=total,
                                              op0=ALU.mult, op1=ALU.max))
            order.then(v.tensor_tensor(factor[:], factor[:], eguard[:], ALU.max))
            order.then(v.tensor_scalar(factor[:], factor[:], 1e-6, None, ALU.add))
            order.then(v.reciprocal(factor[:], factor[:]))
            order.then(v.tensor_tensor(tmp[:], factor[:], factor[:], ALU.mult))
            order.then(v.tensor_tensor(tmp[:], tmp[:], msq[:], ALU.mult))
            v.tensor_scalar(tmp[:], tmp[:], 1.0 / HW1, 1e-6, ALU.mult, ALU.add).then_inc(var_asked, 1)
            dve.wait_ge(std_given, 1)
            order.then(v.reciprocal(tmp[:], tmp[:]))
            order.then(v.tensor_tensor(factor[:], factor[:], tmp[:], ALU.mult))
            for t in range(4):
                bs = slice(4 * t, 4 * t + 4)
                xs = x_sb[:, bs].rearrange("p b (h e) -> p b h e", h=H1)
                hs = xn[:, bs].rearrange("p b (h e) -> p b h e", h=H1)
                order.then(v.tensor_tensor(hs, num[:, bs, :, 0:HW1],
                                           factor[:, bs].unsqueeze(3).to_broadcast([P, 4, H1, HW1]), ALU.mult))
                v.tensor_tensor(x_sb[:, bs], x_sb[:, bs], xn[:, bs], ALU.add).then_inc(x_ready, 1)
                dve.wait_ge(x_ready, t + 1)
                for b in range(4 * t, 4 * t + 4):
                    order.add(v.bn_stats(bnst[:, b], x_sb[:, b]))


def moe_phase(nc, T, sb, scope, x_sb, ident, identb, bnst, mv, rstd, out):
    TG = 4
    NT = B // TG
    NC = EC + 1
    K3 = NSPLIT * E1

    def sem(name):
        return scope.enter_context(nc.semaphore(name))

    gw = sb("gw", [P, NC, P], F32, scope)
    uw = sb("uw", [P, NC, P], F32, scope)
    dw = sb("dw", [P, NC, P], F32, scope)
    rw = sb("rw", [P, E1], F32, scope)
    xn = sb("xn4", [P, B, P], F32, scope)
    xT = sb("xT4", [P, B, P], F32, scope)
    order_i = sb("order_i", [P, E1], mybir.dt.int32, scope)
    desc = sb("desc", [P, E1], F32, scope)
    prob = sb("prob4", [P, B, E1], F32, scope)
    best = sb("best", [P, B], F32, scope)
    key = sb("key", [P, B, E1], F32, scope)
    pick = sb("pick", [P, 2, B, E1], F32, scope)
    rest = sb("rest", [P, B, E1], F32, scope)
    coef3 = sb("coef3", [P, B, NSPLIT, E1], BF16, scope)
    coefT = sb("coefT", [P, B, P], BF16, scope)
    spread = sb("spread", [P, EC, 2, FX], BF16, scope)
    act_g = sb("act_g", [P, 2, TG * P], F32, scope)
    prod = sb("prod", [P, 2, TG * P], F32, scope)
    inter = sb("inter", [P, 2, TG * P], F32, scope)

    psG = [scope.enter_context(nc.psum_tensor(f"psEG{i}", [P, TG * P], F32)) for i in range(2)]
    psU = [scope.enter_context(nc.psum_tensor(f"psEU{i}", [P, TG * P], F32)) for i in range(2)]
    psC = [scope.enter_context(nc.psum_tensor(f"psEC{i}", [P, TG * P], F32)) for i in range(2)]
    psY = scope.enter_context(nc.psum_tensor("psEY", [P, TG, P], F32))
    psR = scope.enter_context(nc.psum_tensor("psER", [P, B, E1], F32))

    w_in, pool_order, dve_order, var_ready, std_ready, xn_ready = (
        sem(n) for n in ("moe_w_in", "moe_pool_order", "moe_dve_order", "moe_var_ready", "moe_std_ready",
                         "moe_xn_ready"))
    const_ready, xT_psum, xT_ready, r_psum, shifted, exp_ready, coef_ready, coef_psum, coefT_ready = (
        sem(n) for n in ("moe_const_ready", "moe_xT_psum", "moe_xT_ready", "moe_r_psum", "moe_shifted",
                         "moe_exp_ready", "moe_coef_ready", "moe_coef_psum", "moe_coefT_ready"))
    gu_psum, g_ready, prod_ready, c_psum, inter_ready, down_done, y_ready, stored = (
        sem(n) for n in ("moe_gu_psum", "moe_g_ready", "moe_prod_ready", "moe_c_psum", "moe_inter_ready",
                         "moe_down_done", "moe_y_ready", "moe_stored"))
    NW = 7

    def turned(t):
        return psG[t % 2][:].rearrange("p (b d) -> p b d", b=TG)

    def coef_bank(b):
        bank = psC[b // 8][:].bitcast(BF16)
        return bank[0:K3, (b % 8) * P:(b % 8 + 1) * P]

    with nc.Block() as block:
        @block.sync
        def _(sp):
            sp.dma_start(rw[:], T["L1_ffn_router_w"]).then_inc(w_in, 16)
            for name, dest in (("gate", gw), ("up", uw)):
                sp.dma_start(dest[:, 0:EC].rearrange("p c (two f) -> p (c two) f", two=2),
                             T[f"L1_ffn_{name}_w"].rearrange("e p f -> p e f")).then_inc(w_in, 16)
                sp.dma_start(dest[:, EC], T[f"L1_ffn_shared_{name}_w"]).then_inc(w_in, 16)
            sp.dma_start(dw[:, 0:EC], T["L1_ffn_down_w"].rearrange("e f d -> (e f) d")
                         .rearrange("(c p) d -> p c d", p=P)).then_inc(w_in, 16)
            sp.dma_start(dw[:, EC], T["L1_ffn_shared_down_w"]).then_inc(w_in, 16)
            for t in range(NT):
                sp.wait_ge(y_ready, t + 1)
                sp.dma_start(out[TG * t:TG * t + TG].rearrange("b s d -> s b d"),
                             x_sb[:, TG * t:TG * t + TG]).then_inc(stored, 16)
            sp.wait_ge(stored, 16 * NT)

        @block.gpsimd
        def _(pool):
            order = Order(pool, pool_order)
            order.add(nc.gpsimd.iota(order_i[:], pattern=[[-1, E1]], base=E1, channel_multiplier=0))
            order.add(nc.gpsimd.memset(spread[:], 0.0))
            order.add(nc.gpsimd.memset(coefT[:], 0.0))
            order.sync()
            nc.gpsimd.tensor_copy(desc[:], order_i[:]).then_inc(const_ready, 1)
            for part in range(NSPLIT):
                order.then(nc.gpsimd.affine_select(out=spread[:], in_=spread[:], compare_op=ALU.not_equal,
                                                   fill=1.0, base=-E1 * part,
                                                   pattern=[[-2, EC], [-1, 2], [0, FX]], channel_multiplier=1))
            pool.sem_inc(const_ready, 1)

        @block.scalar
        def _(act):
            act.wait_ge(var_ready, 1)
            nc.scalar.activation(rstd[:], rstd[:], ACT.Sqrt).then_inc(std_ready, 1)
            for t in range(NT):
                act.wait_ge(xT_psum, t + 1)
                nc.scalar.copy(xT[:, TG * t:TG * t + TG], turned(t)).then_inc(xT_ready, 1)
            act.wait_ge(shifted, 1)
            nc.scalar.activation(prob[:], prob[:], ACT.Exp).then_inc(exp_ready, 1)
            act.wait_ge(coef_psum, 1)
            act.wait_ge(const_ready, 2)
            for k in range(2):
                nc.scalar.copy(coefT[0:K3, 8 * k:8 * k + 8].rearrange("k b s -> k (b s)"),
                               psC[k][:].bitcast(BF16)[0:K3]).then_inc(coefT_ready, 1)

            def slots(t):
                for e in range(NC):
                    n = NC * t + e
                    act.wait_ge(gu_psum, n + 1)
                    after(act, prod_ready, n - 1 if e else n)
                    nc.scalar.activation(act_g[:, e % 2], psG[e % 2][:], ACT.Silu).then_inc(g_ready, 1)

            slots(0)
            with nc.scalar.Fori(1, NT) as t:
                slots(t)

        @block.vector
        def _(dve):
            v = nc.vector
            order = Order(dve, dve_order)
            layernorm_all(v, (var_ready, std_ready), order, dve, x_sb, bnst, mv, rstd)
            for b in range(B):
                v.tensor_scalar(xn[:, b], x_sb[:, b], mv[:, b, 0:1], rstd[:, b:b + 1],
                                ALU.subtract, ALU.mult).then_inc(xn_ready, 1)
            wide = [P, B, E1]

            def over(col):
                return col[:].unsqueeze(2).to_broadcast(wide)

            dve.wait_ge(r_psum, 1)
            order.then(v.tensor_reduce(best[:], psR[:], AX.X, ALU.max))
            v.tensor_tensor(prob[:], psR[:], over(best), ALU.subtract).then_inc(shifted, 1)
            dve.wait_ge(exp_ready, 1)
            order.then(v.tensor_reduce(best[:], prob[:], AX.X, ALU.add))
            order.then(v.reciprocal(best[:], best[:]))
            order.then(v.tensor_tensor(prob[:], prob[:], over(best), ALU.mult))
            dve.wait_ge(const_ready, 2)
            left = prob
            for k in range(2):
                order.then(v.tensor_reduce(best[:], left[:], AX.X, ALU.max))
                order.then(v.tensor_tensor(key[:], left[:], over(best), ALU.is_equal))
                order.then(v.tensor_tensor(key[:], key[:], desc[:].unsqueeze(1).to_broadcast(wide), ALU.mult))
                order.then(v.tensor_reduce(best[:], key[:], AX.X, ALU.max))
                order.then(v.tensor_tensor(pick[:, k], key[:], over(best), ALU.is_equal))
                if k == 0:
                    order.then(v.scalar_tensor_tensor(out=rest[:].rearrange("p b e -> p (b e)"),
                                                      in0=pick[:, 0].rearrange("p b e -> p (b e)"), scalar=-2.0,
                                                      in1=prob[:].rearrange("p b e -> p (b e)"),
                                                      op0=ALU.mult, op1=ALU.add))
                    left = rest
            order.then(v.tensor_tensor(pick[:, 0], pick[:, 0], pick[:, 1], ALU.add))
            order.then(v.tensor_tensor(prob[:], prob[:], pick[:, 0], ALU.mult))
            for part in range(NSPLIT):
                order.then(v.tensor_copy(coef3[:, :, part], prob[:]))
                if part < NSPLIT - 1:
                    order.then(v.tensor_tensor(prob[:], prob[:], coef3[:, :, part], ALU.subtract))
            v.engine_nop().then_inc(coef_ready, 1)

            def slots(t):
                for e in range(NC):
                    n = NC * t + e
                    free = n - 1 if e else n
                    dve.wait_ge(g_ready, n + 1)
                    if e < EC:
                        v.tensor_tensor(prod[:, e % 2], act_g[:, e % 2], psU[e % 2][:],
                                        ALU.mult).then_inc(prod_ready, 1)
                        dve.wait_ge(prod_ready, n + 1)
                        dve.wait_ge(c_psum, EC * t + e + 1)
                        after(dve, down_done, free)
                        v.tensor_tensor(inter[:, e % 2], prod[:, e % 2], psC[e % 2][:],
                                        ALU.mult).then_inc(inter_ready, 1)
                    else:
                        after(dve, down_done, free)
                        v.tensor_tensor(inter[:, e % 2], act_g[:, e % 2], psU[e % 2][:],
                                        ALU.mult).then_inc(prod_ready, 1)
                        dve.wait_ge(prod_ready, n + 1)
                        dve.sem_inc(inter_ready, 1)
                dve.wait_ge(down_done, NC * t + NC)
                if isinstance(t, int):
                    xs = x_sb[:, TG * t:TG * t + TG]
                else:
                    xs = x_sb[:, bass.ds(TG * t, TG)]
                v.tensor_tensor(xs, xs, psY[:], ALU.add).then_inc(y_ready, 1)

            slots(0)
            with v.Fori(1, NT) as t:
                slots(t)

        @block.tensor
        def _(pe):
            mm_ = nc.tensor.matmul
            for t in range(NT):
                pe.wait_ge(xn_ready, TG * (t + 1))
                if t >= 2:
                    pe.wait_ge(xT_ready, t - 1)
                for j in range(TG):
                    mm = nc.tensor.transpose(turned(t)[:, j], xn[:, TG * t + j], ident[:])
                mm.then_inc(xT_psum, 1)
            pe.wait_ge(w_in, 16 * NW)
            pe.wait_ge(xT_ready, NT)
            for b in range(B):
                mm = mm_(psR[:, b], xT[:, b], rw[:], start=True, stop=True)
            mm.then_inc(r_psum, 1)
            pe.wait_ge(coef_ready, 1)
            for b in range(B):
                mm = nc.tensor.transpose(coef_bank(b), coef3[:, b].rearrange("p k e -> p (k e)"), identb[:])
            mm.then_inc(coef_psum, 1)
            pe.wait_ge(const_ready, 2)
            pe.wait_ge(coefT_ready, 2)

            def rows(a, t):
                if isinstance(t, int):
                    return a[:, TG * t:TG * t + TG]
                return a[:, bass.ds(TG * t, TG)]

            def down(t, e):
                n = NC * t + e
                pe.wait_ge(inter_ready, n + 1)
                if e == 0:
                    after(pe, y_ready, t)
                for j in range(TG):
                    mm = mm_(psY[:, j], inter[:, e % 2, j * P:(j + 1) * P], dw[:, e],
                             start=(e == 0 and j == 0), stop=(e == NC - 1 and j == TG - 1), skip_group_check=True)
                mm.then_inc(down_done, 1)

            def slots(t):
                for e in range(NC):
                    n = NC * t + e
                    after(pe, prod_ready, n - 1 if e else n)
                    mm_(psG[e % 2][:], gw[:, e], rows(xT, t), start=True, stop=True)
                    mm_(psU[e % 2][:], uw[:, e], rows(xT, t), start=True, stop=True).then_inc(gu_psum, 1)
                    if e < EC:
                        after(pe, inter_ready, n - 1)
                        mm_(psC[e % 2][:], spread[:, e].rearrange("k a f -> k (a f)"), rows(coefT, t),
                            start=True, stop=True).then_inc(c_psum, 1)
                    if e:
                        down(t, e - 1)
                pe.wait_ge(inter_ready, NC * t + NC)
                down(t, NC - 1)

            slots(0)
            with nc.tensor.Fori(1, NT) as t:
                slots(t)


_INS = ['x', 'ctx_1024', 'fside_BxSx4_0', 'L0_xattn_Wq', 'L0_xattn_bq', 'L0_xattn_Wk', 'L0_xattn_bk',
        'L0_xattn_Wv', 'L0_xattn_bv', 'L0_xattn_Wo', 'L0_xattn_bo', 'L0_xattn_Wg', 'L0_xattn_bg',
        'L0_ffn_w1', 'L0_ffn_b1', 'L0_ffn_w2', 'L0_ffn_b2', 'L1_xattn_igate_kernel', 'L1_xattn_igate_bias',
        'L1_xattn_fgate_kernel', 'L1_xattn_fgate_bias', 'L1_ffn_router_w', 'L1_ffn_gate_w', 'L1_ffn_up_w',
        'L1_ffn_down_w', 'L1_ffn_shared_gate_w', 'L1_ffn_shared_up_w', 'L1_ffn_shared_down_w']
STAGE = 4


def kernel(**inputs):
    import numpy as _np
    import concourse.bacc as _bacc
    from concourse import mybir as _mybir
    from concourse.bass_utils import run_bass_kernel_spmd as _run

    nc = _bacc.Bacc("TRN2", target_bir_lowering=False, num_devices=1)
    arrays, tensors = {}, {}
    for name in _INS:
        a = _np.ascontiguousarray(inputs[name])
        arrays[f"in_{name}_dram"] = a
        tensors[name] = nc.dram_tensor(f"in_{name}_dram", a.shape, _mybir.dt.from_np(a.dtype),
                                       kind="ExternalInput").ap()
    out = nc.dram_tensor("out_0_dram", (B, P, P), F32, kind="ExternalOutput").ap()
    build(nc, tensors, out, STAGE)
    r = _run(nc, [arrays], core_ids=[0])
    return r.results[0]["out_0_dram"]
```

```python
from contextlib import ExitStack
import math

import concourse.bass as bass
from concourse import mybir

F32 = mybir.dt.float32
BF16 = mybir.dt.bfloat16
F16 = mybir.dt.float16
ALU = mybir.AluOpType
ACT = mybir.ActivationFunctionType
AX = mybir.AxisListType
RMAX = bass.bass_isa.ReduceOp.max

P = 128
B = 16
H0 = 16
DK = 64
HD = H0 * DK
CH = HD // P
HG = 4
UN = H0 // HG
NG = 8
GN = P // NG
F1 = 512
FC = F1 // P
H1 = 8
HW1 = P // H1
E1 = 16
FX = 64
EC = E1 * FX // P
NC = EC + 1
LN_EPS = 1e-5
Q_EPS = 1e-8
ROUND = 1.5 * 2.0 ** 23
TURN = 6.2831845
COS_SHIFT = math.exp(math.pi / 2 / 100.0)
MASKED = -1e30
CYCLES = 100.0 / (4.0 * math.pi)
W_UP = 64.0
G_UP = 4096.0
EXP_LN = "natural_log_exp_and_others"
NSPLIT = 3
SROW = [0, 32, 64]
KB = SROW[-1] + 1
KQ = SROW[-1] + 2 * CH


def after(eng, sem, value):
    if isinstance(value, int) and value <= 0:
        return
    eng.wait_ge(sem, value)


class Order:

    def __init__(self, sem):
        self.eng, self.sem, self.n = None, sem, 0

    def on(self, eng):
        self.eng = eng
        return self

    def add(self, ins):
        self.n += 1
        ins.then_inc(self.sem, 1)

    def sync(self):
        self.eng.wait_ge(self.sem, self.n)

    def then(self, ins):
        self.add(ins)
        self.sync()


def over_batches(eng, slots, step=4):
    for b in range(2):
        slots(b, b)
    with eng.Fori(0, (B - 4) // step) as i:
        for k in range(step):
            slots(step * i + (2 + k), k % 2)
    for b in range(B - 2, B):
        slots(b, b % 2)


def known(b, value):
    return isinstance(b, int) and b == value


def build(nc, T, out, stage):
    ctx = ExitStack()
    with ctx:
        def sb(name, shape, dt=F32, where=ctx):
            return where.enter_context(nc.sbuf_tensor(name, shape, dt))

        x_sb = sb("x_sb", [P, B, P])
        ctx_sb = sb("ctx_sb", [P, B, P])
        ctxT2 = sb("ctxT2", [P, 2, B, P], F16)
        ident = sb("ident", [P, P])
        identb = sb("identb", [P, P], BF16)
        bnst = sb("bnst", [P, B, 6])
        mv = sb("mv", [P, B, 2])
        rstd = sb("rstd", [P, B])
        steps = dict(dve=Order(ctx.enter_context(nc.semaphore("dve_order"))),
                     pool=Order(ctx.enter_context(nc.semaphore("pool_order"))),
                     asked=ctx.enter_context(nc.semaphore("sqrt_asked")),
                     shift=sb("ln_shift", [P, B]),
                     shift_ready=ctx.enter_context(nc.semaphore("ln_shift_ready")),
                     dve_xn=ctx.enter_context(nc.semaphore("dve_xn")),
                     act_xn=ctx.enter_context(nc.semaphore("act_xn")),
                     given=ctx.enter_context(nc.semaphore("sqrt_given")))
        later = dict(
            w1=sb("w1", [P, FC, P]),
            w2=sb("w2", [P, FC, P]),
            b1=sb("b1", [P, FC]),
            b2=sb("b2", [P, 1]),
            ws=sb("ws", [P, FC + 1]),
            wr=sb("wr", [P, FC + 1]),
            q1=sb("q1", [P, FC, P], BF16),
            q2=sb("q2", [P, FC, P], BF16),
            moe_w=sb("moe_w", [P, 3, NC, P]),
            rw=sb("rw", [P, E1]),
            moe_w2=sb("moe_w2", [P, 3, 2, NC, P], F16),
            rw2=sb("rw2", [P, 2, E1], F16),
            rowmax=sb("rowmax", [P, B, 1]),
            ffn_in=ctx.enter_context(nc.semaphore("ffn_in")),
            moe_in=ctx.enter_context(nc.semaphore("moe_in")),
            moe_hi=ctx.enter_context(nc.semaphore("moe_hi")),
            moe_lo=ctx.enter_context(nc.semaphore("moe_lo")),
            q_ready=ctx.enter_context(nc.semaphore("ffn_q_ready")),
        )
        for_attention = ExitStack()
        with for_attention:
            attention_phases(nc, T, sb, for_attention, x_sb, ctx_sb, ctxT2, ident, identb, bnst, mv, rstd,
                             later, steps)
        if stage >= 2:
            with ExitStack() as scope:
                ffn_phase(nc, sb, scope, x_sb, ident, identb, bnst, mv, rstd, steps, later)
        if stage >= 3:
            with ExitStack() as scope:
                mlstm_phase(nc, T, sb, scope, x_sb, ctx_sb, ctxT2, ident, identb, bnst, mv, rstd, steps, later)
        if stage >= 4:
            with ExitStack() as scope:
                moe_phase(nc, sb, scope, x_sb, ident, identb, bnst, mv, rstd, steps, later, out)
        else:
            s_out = ctx.enter_context(nc.semaphore("s_out"))
            with nc.Block() as block:
                @block.sync
                def _(sp):
                    sp.dma_start(out.rearrange("b s d -> s b d"), x_sb[:]).then_inc(s_out, 16)
                    sp.wait_ge(s_out, 16)


def attention_phases(nc, T, sb, scope, x_sb, ctx_sb, ctxT2, ident, identb, bnst, mv, rstd, later, steps):
    buf = dict(
        xT2=sb("xT2", [P, 2, B, P], F16, scope),
        wT2=sb("wT2", [P, 3, 2, CH, P], F16, scope),
        woT=sb("woT", [P, CH, P], F32, scope),
        kron2=sb("kron2", [P, 2, H0, GN], F16, scope),
        bqk3=sb("bqk3", [KQ, P], BF16, scope),
        bias_pick=sb("bias_pick", [KQ, 2 * CH, P], BF16, scope),
        bo3=sb("bo3", [KB, P], BF16, scope),
        bg3=sb("bg3", [KB, H0], BF16, scope),
        ones3=sb("ones3", [KB, P], BF16, scope),
        beta=sb("beta", [P, B + 1, P], F32, scope),
        alpha=sb("alpha", [P, B + 1, NG], F32, scope),
        gamma2=sb("gamma2", [P, B + 1, NG], F32, scope),
        least2=sb("least2", [P, 1], F32, scope),
        arg=sb("arg", [P, 2, NG, P], F32, scope),
        turns=sb("turns", [P, 2, NG, P], F32, scope),
        whole=sb("whole", [P, 2, NG, P], F32, scope),
        wave=sb("wave", [P, 2, NG, P], F32, scope),
        emb2=sb("emb2", [P, 2, 2, NG, P], F16, scope),
        vx2=sb("vx2", [P, 2, 2, H0, DK + 1], F16, scope),
    )
    with ExitStack() as prep:
        prepare_phase(nc, T, sb, prep, x_sb, ctx_sb, ctxT2, ident, identb, bnst, mv, rstd, steps, **buf)
    with ExitStack() as loop:
        attention_loop(nc, T, sb, loop, x_sb, ctxT2, identb, ident, bnst, mv, later, steps, **buf)


def prepare_phase(nc, T, sb, scope, x_sb, ctx_sb, ctxT2, ident, identb, bnst, mv, rstd, steps,
                  xT2, wT2, woT, kron2, bqk3, bias_pick, bo3, bg3, ones3, beta, alpha, gamma2, least2,
                  arg, turns, whole, wave, emb2, vx2):
    def sem(name):
        return scope.enter_context(nc.semaphore(name))

    raw = sb("raw", [P, 4, CH, P], F32, scope)
    xn = sb("xn", [P, B, P], F32, scope)
    box = sb("box", [P, B, 4], F32, scope)
    fbeta = sb("fbeta", [P, B, 4], F32, scope)
    falpha = sb("falpha", [P, B, 4], F32, scope)
    fgamma = sb("fgamma", [P, B, 4], F32, scope)
    repeat = sb("repeat", [P, NG, P], F32, scope)
    kinds = sb("kinds", [P, B, P], F32, scope)
    kind4 = sb("kind4", [P, 4], F32, scope)
    delta16 = sb("delta16", [P, GN], F32, scope)
    picked = sb("picked", [P, NG, B, 4], F32, scope)
    shift = sb("shift", [P, 1], F32, scope)
    wgp = sb("wgp", [P, H0], F32, scope)
    kron = sb("kron", [P, H0, GN], F32, scope)
    chunk1 = sb("chunk1", [KQ, 2 * CH], F32, scope)
    qkrow = sb("qkrow", [KQ, P], F32, scope)
    qkpart = sb("qkpart", [KQ, P], BF16, scope)
    bv = sb("bv", [CH, P], F32, scope)
    bvT = sb("bvT", [P, CH], F32, scope)
    orow = sb("orow", [KB, P], F32, scope)
    opart = sb("opart", [KB, P], BF16, scope)
    grow = sb("grow", [KB, H0], F32, scope)
    gpart = sb("gpart", [KB, H0], BF16, scope)

    psT = scope.enter_context(nc.psum_tensor("psT", [P, 3, 4, P], F32))
    psB = scope.enter_context(nc.psum_tensor("psB", [P, B, P], F32))
    psA = scope.enter_context(nc.psum_tensor("psA", [P, NG, B, 4], F32))

    x_in, ctx_in, wo_in, box_in, wg_in, bias_in = (
        sem(n) for n in ("x_in", "ctx_in", "wo_in", "box_in", "wg_in", "bias_in"))
    w_in = [sem(f"w{k}_in") for k in range(3)]
    ident_ready, chunk_ready, square_ready = sem("ident_ready"), sem("chunk_ready"), sem("square_ready")
    xn_ready = sem("xn_ready")
    boxes_ready, beta_psum, beta_ready, picked_psum, picked_read = (
        sem(n) for n in ("boxes_ready", "beta_psum", "beta_ready", "picked_psum", "picked_read"))
    tr_psum, hi_ready, lo_ready = sem("tr_psum"), sem("hi_ready"), sem("lo_ready")
    dist_ready, arg_ready, log_ready, frac_ready, wave_ready, emb_hi, bvT_psum, bvT_ready, bo_psum = (
        sem(n) for n in ("dist_ready", "arg_ready", "log_ready", "frac_ready", "wave_ready",
                         "emb_hi", "bvT_psum", "bvT_ready", "bo_psum"))

    NTR = 4 + 4 + 6 + 2

    def halves(n):
        if n < 4:
            return ctxT2[:, 0, 4 * n:4 * n + 4], ctxT2[:, 1, 4 * n:4 * n + 4], 1.0
        if n < 8:
            return xT2[:, 0, 4 * n - 16:4 * n - 12], xT2[:, 1, 4 * n - 16:4 * n - 12], 1.0
        k, half = divmod(n - 8, 2)
        return wT2[:, k, 0, 4 * half:4 * half + 4], wT2[:, k, 1, 4 * half:4 * half + 4], W_UP

    def flat(a):
        return a.rearrange("p g m -> p (g m)")

    with nc.Block() as block:
        @block.sync
        def _(sp):
            sp.dma_start(box[:], T["fside_BxSx4_0"].rearrange("b s c -> s b c")).then_inc(box_in, 16)
            sp.dma_start(ctx_sb[:], T["ctx_1024"].rearrange("b s d -> s b d")).then_inc(ctx_in, 16)
            for k, name in enumerate(("L0_xattn_Wq", "L0_xattn_Wk", "L0_xattn_Wv")):
                sp.dma_start(raw[:, k], T[name].rearrange("(c p) d -> p c d", p=P)).then_inc(w_in[k], 16)

        @block.scalar
        def _(act):
            act.dma_start(x_sb[:], T["x"].rearrange("b s d -> s b d")).then_inc(x_in, 16)
            act.dma_start(raw[:, 3], T["L0_xattn_Wo"].rearrange("p (c d) -> p c d", d=P)).then_inc(wo_in, 16)
            for t in range(4):
                act.wait_ge(beta_psum, t + 1)
                nc.scalar.copy(beta[:, 4 * t:4 * t + 4], psB[:, 4 * t:4 * t + 4]).then_inc(beta_ready, 1)
            def evacuate(n):
                act.wait_ge(tr_psum, n + 1)
                hi, _, up = halves(n)
                nc.scalar.activation(hi, psT[:, n % 3], ACT.Copy, scale=up).then_inc(hi_ready, 1)

            evacuate(0)
            act.wait_ge(dist_ready, 1)
            nc.scalar.activation(arg[:], arg[:], ACT.Square).then_inc(square_ready, 1)
            act.wait_ge(steps["asked"], 1)
            nc.scalar.activation(rstd[:], rstd[:], ACT.Sqrt).then_inc(steps["given"], 1)
            evacuate(1)
            act.wait_ge(arg_ready, 1)
            nc.scalar.activation(arg[:], arg[:], ACT.Ln).then_inc(log_ready, 1)
            act.wait_ge(log_ready, 1)
            nc.scalar.activation(turns[:], arg[:], ACT.Copy, scale=CYCLES).then_inc(log_ready, 1)
            for n in range(2, 5):
                evacuate(n)
            act.wait_ge(frac_ready, 1)
            nc.scalar.activation(wave[:], whole[:], ACT.Sin, scale=-TURN).then_inc(wave_ready, 1)
            act.wait_ge(wave_ready, 1)
            nc.scalar.copy(emb2[:, 0, 0], wave[:, 0]).then_inc(emb_hi, 1)
            for n in range(5, 14):
                evacuate(n)
            for n in range(14, NTR):
                act.wait_ge(tr_psum, n + 1)
                nc.scalar.activation(woT[:, 4 * n - 56:4 * n - 52], psT[:, n % 3], ACT.Copy,
                                     scale=1.0 / W_UP).then_inc(hi_ready, 1)
            nc.scalar.preload_act_table(ACT.Exp)

        @block.gpsimd
        def _(pool):
            order = steps["pool"].on(pool)
            order.add(nc.gpsimd.memset(ident[:], 0.0))
            order.add(nc.gpsimd.memset(identb[:], 0.0))
            order.add(nc.gpsimd.memset(falpha[:], 0.0))
            order.add(nc.gpsimd.memset(qkrow[:], 0.0))
            order.sync()
            nc.gpsimd.affine_select(out=ident[:], in_=ident[:], compare_op=ALU.not_equal, fill=1.0,
                                    base=0, pattern=[[-1, P]], channel_multiplier=1).then_inc(ident_ready, 1)
            nc.gpsimd.affine_select(out=identb[:], in_=identb[:], compare_op=ALU.not_equal, fill=1.0,
                                    base=0, pattern=[[-1, P]], channel_multiplier=1).then_inc(ident_ready, 1)
            for row in SROW:
                for k, name in enumerate(("L0_xattn_bq", "L0_xattn_bk")):
                    pool.dma_start(qkrow[row + CH * k:row + CH * k + CH], T[name].rearrange("(c p) -> c p", p=P)
                                   ).then_inc(bias_in, 16)
            pool.dma_start(bv[:], T["L0_xattn_bv"].rearrange("(c p) -> c p", p=P)).then_inc(bias_in, 16)
            for dest, name in ((orow, "L0_xattn_bo"), (grow, "L0_xattn_bg")):
                pool.dma_start(dest[:], T[name].rearrange("(o n) -> o n", o=1)
                               .to_broadcast([KB, T[name].shape[0]])).then_inc(bias_in, 16)
            with nc.allow_non_contiguous_dma(reason="2048 words of Wg, once"):
                for kind in range(8):
                    pool.dma_start(wgp[16 * kind:16 * kind + 16, :],
                                   T["L0_xattn_Wg"].rearrange("h k -> k h")[kind:kind + 1, :]
                                   .to_broadcast([16, H0])).then_inc(wg_in, 16)
            g = nc.gpsimd
            order.add(g.memset(vx2[:, :, 0, :, DK:], 1.0))
            order.add(g.memset(vx2[:, :, 1, :, DK:], 0.0))
            order.add(g.memset(ones3[:], 0.0))
            order.add(g.memset(bg3[:], 0.0))
            order.sync()
            for row in SROW:
                order.then(g.memset(ones3[row:row + 1, :], 1.0))
            pool.wait_ge(bias_in, 16 * 9)
            pool.wait_ge(chunk_ready, 1)
            order.add(g.tensor_copy(bias_pick[:], chunk1[:].unsqueeze(2).to_broadcast([KQ, 2 * CH, P])))

            def three_parts(rows, part, dest):
                for k, row in enumerate(SROW):
                    order.then(g.tensor_copy(part[:], rows[:]))
                    dest(row)
                    if k < NSPLIT - 1:
                        order.then(g.tensor_tensor(rows[:], rows[:], part[:], ALU.subtract))

            def to_qk(row):
                order.then(g.tensor_copy(bqk3[row:min(row + 32, KQ), :], qkpart[row:min(row + 32, KQ), :]))

            def to_g(row):
                order.then(g.tensor_copy(bg3[row:row + 1], gpart[row:row + 1, :]))

            order.add(g.tensor_scalar(qkrow[:], qkrow[:], W_UP, None, ALU.mult))
            order.add(g.tensor_scalar(grow[:], grow[:], G_UP, None, ALU.mult))
            order.sync()
            three_parts(qkrow, qkpart, to_qk)
            three_parts(grow, gpart, to_g)

        @block.vector
        def _(dve):
            order = steps["dve"].on(dve)
            v = nc.vector
            dve.wait_ge(ident_ready, 2)
            order.add(v.tensor_reduce(kind4[:], ident[:].rearrange("p (a t n) -> p t a n", a=2, t=4),
                                      AX.XY, ALU.add))
            order.add(v.tensor_reduce(delta16[:], ident[:].rearrange("p (d n) -> p n d", n=GN),
                                      AX.X, ALU.add))
            order.add(v.tensor_reduce(shift[:], ident[:, P // 2:], AX.X, ALU.add))
            order.add(v.tensor_copy(repeat[:].rearrange("p g (k n) -> p g k n", n=GN),
                                    ident[:].rearrange("p (g n) -> p g n", n=GN).unsqueeze(2)
                                    .to_broadcast([P, NG, NG, GN])))
            v.tensor_reduce(chunk1[:], ident[0:KQ, 0:SROW[2] + SROW[1]]
                            .rearrange("p (a c) -> p c a", a=NSPLIT)[:, 0:2 * CH],
                            AX.X, ALU.add).then_inc(chunk_ready, 1)
            dve.wait_ge(box_in, 16)
            order.add(v.tensor_tensor(fbeta[:, :, 0:2], box[:, :, 0:2], box[:, :, 2:4], ALU.add))
            order.add(v.tensor_tensor(fgamma[:, :, 2:4], box[:, :, 2:4], box[:, :, 0:2], ALU.subtract))
            order.sync()
            order.add(v.tensor_scalar(fbeta[:, :, 0:2], fbeta[:, :, 0:2], 0.5, None, ALU.mult))
            order.add(v.tensor_scalar(fgamma[:, :, 2:4], fgamma[:, :, 2:4], 1.0, None, ALU.add))
            order.add(v.tensor_scalar(shift[:], shift[:], COS_SHIFT - 1.0, 1.0, ALU.mult, ALU.add))
            order.add(v.tensor_tensor(least2[:], kind4[:, 0:1], kind4[:, 1:2], ALU.add))
            order.sync()
            order.add(v.reciprocal(fgamma[:, :, 0:2], fgamma[:, :, 2:4]))
            order.add(v.tensor_copy(falpha[:, :, 0:2], fbeta[:, :, 0:2]))
            order.add(v.tensor_scalar(least2[:], least2[:], 1e-3, 1e-18, ALU.mult, ALU.add))
            order.sync()
            order.add(v.tensor_copy(fbeta[:, :, 2:4], fgamma[:, :, 0:2]))
            order.add(v.tensor_tensor(least2[:], least2[:], shift[:], ALU.mult))
            order.sync()
            order.add(v.tensor_tensor(least2[:], least2[:], least2[:], ALU.mult))
            for half in range(2):
                order.add(v.tensor_copy(kinds[:, :, 64 * half:64 * half + 64]
                                        .rearrange("p b (t n) -> p b t n", n=GN),
                                        fbeta[:].unsqueeze(3).to_broadcast([P, B, 4, GN])))
            order.sync()
            v.engine_nop().then_inc(boxes_ready, 1)
            for k, dest in enumerate((alpha, gamma2)):
                dve.wait_ge(picked_psum, k + 1)
                order.then(v.tensor_tensor(picked[:].rearrange("p g b t -> p (g b) t"),
                                           psA[:].rearrange("p g b t -> p (g b) t"),
                                           kind4[:].unsqueeze(1).to_broadcast([P, NG * B, 4]), ALU.mult))
                order.then(v.tensor_reduce(dest[:, 0:B].rearrange("p b g -> p g b"), picked[:], AX.X, ALU.add))
                v.engine_nop().then_inc(picked_read, 1)
            order.then(v.tensor_scalar(gamma2[:, 0:B], gamma2[:, 0:B], shift[:, 0:1], None, ALU.mult))
            order.then(v.tensor_tensor(gamma2[:, 0:B], gamma2[:, 0:B], gamma2[:, 0:B], ALU.mult))
            dve.wait_ge(beta_ready, 1)
            for b in range(2):
                order.add(v.tensor_tensor(arg[:, b], beta[:, b].unsqueeze(1).to_broadcast([P, NG, P]),
                                          alpha[:, b].unsqueeze(2).to_broadcast([P, NG, P]), ALU.subtract))
            order.sync()
            v.engine_nop().then_inc(dist_ready, 1)
            dve.wait_ge(x_in, 16)
            for b in range(B):
                order.add(v.bn_stats(bnst[:, b], x_sb[:, b]))
            order.sync()
            for b in range(B):
                order.add(v.bn_aggr(mv[:, b], bnst[:, b]))
            order.sync()
            v.tensor_scalar(rstd[:], mv[:, :, 1], LN_EPS, None, ALU.add).then_inc(steps["asked"], 1)
            dve.wait_ge(square_ready, 1)
            for b in range(2):
                order.add(v.tensor_tensor(arg[:, b], arg[:, b], gamma2[:, b].unsqueeze(2)
                                          .to_broadcast([P, NG, P]), ALU.mult))
            order.sync()
            v.tensor_scalar(arg[:], arg[:], least2[:, 0:1], None, ALU.max).then_inc(arg_ready, 1)

            def low_half(n):
                dve.wait_ge(hi_ready, n + 1)
                hi, lo, up = halves(n)
                v.scalar_tensor_tensor(out=lo, in0=psT[:, n % 3], scalar=up, in1=hi, op0=ALU.mult,
                                       op1=ALU.subtract).then_inc(lo_ready, 1)

            low_half(0)
            dve.wait_ge(steps["given"], 1)
            order.then(v.reciprocal(rstd[:], rstd[:]))
            for b in range(B):
                v.tensor_scalar(xn[:, b], x_sb[:, b], mv[:, b, 0:1], rstd[:, b:b + 1],
                                ALU.subtract, ALU.mult).then_inc(xn_ready, 1)
            low_half(1)
            dve.wait_ge(log_ready, 1)
            order.then(v.tensor_scalar(whole[:], arg[:], CYCLES, ROUND, ALU.mult, ALU.add))
            dve.wait_ge(log_ready, 2)
            v.scalar_tensor_tensor(out=flat(whole[:].rearrange("p b g m -> p (b g) m")),
                                   in0=flat(whole[:].rearrange("p b g m -> p (b g) m")), scalar=ROUND,
                                   in1=flat(turns[:].rearrange("p b g m -> p (b g) m")), op0=ALU.subtract,
                                   op1=ALU.subtract).then_inc(frac_ready, 1)
            for n in range(2, 5):
                low_half(n)
            dve.wait_ge(wg_in, 16 * 8)
            order.then(v.scalar_tensor_tensor(out=kron[:], in0=wgp[:].unsqueeze(2).to_broadcast([P, H0, GN]),
                                              scalar=G_UP, in1=delta16[:].unsqueeze(1).to_broadcast([P, H0, GN]),
                                              op0=ALU.mult, op1=ALU.mult))
            order.then(v.tensor_copy(kron2[:, 0], kron[:]))
            order.add(v.tensor_tensor(kron2[:, 1], kron[:], kron2[:, 0], ALU.subtract))
            dve.wait_ge(bvT_psum, 1)
            v.tensor_copy(bvT[:], psA[:].rearrange("p g b t -> p (g b t)")[:, 0:CH]).then_inc(bvT_ready, 1)
            dve.wait_ge(emb_hi, 1)
            order.add(v.tensor_tensor(emb2[:, 0, 1], wave[:, 0], emb2[:, 0, 0], ALU.subtract))
            for n in range(5, 14):
                low_half(n)
            order.add(v.memset(bo3[:], 0.0))
            dve.wait_ge(bo_psum, 1)
            order.then(v.scalar_tensor_tensor(out=orow[:], in0=psA[0:KB].rearrange("p g b t -> p (g b t)")
                                              [:, P:2 * P], scalar=W_UP, in1=orow[:], op0=ALU.mult, op1=ALU.add))
            for k, row in enumerate(SROW):
                order.then(v.tensor_copy(opart[:], orow[:]))
                order.add(v.tensor_copy(bo3[row:row + 1, :], opart[row:row + 1, :]))
                if k < NSPLIT - 1:
                    order.then(v.tensor_tensor(orow[:], orow[:], opart[:], ALU.subtract))

        @block.tensor
        def _(pe):
            pe.wait_ge(ident_ready, 2)
            pe.wait_ge(boxes_ready, 1)
            def betas(t):
                for b in range(4 * t, 4 * t + 4):
                    mm = nc.tensor.matmul(psB[:, b], kinds[:, b], ident[:], start=True, stop=True)
                mm.then_inc(beta_psum, 1)

            for k, src in enumerate((falpha, fgamma)):
                if k:
                    pe.wait_ge(picked_read, k)
                for g in range(NG):
                    mm = nc.tensor.matmul(psA[:, g], repeat[:, g], src[:], start=(g == 0), stop=(g == NG - 1),
                                          skip_group_check=True)
                mm.then_inc(picked_psum, 1)
                for t in ((0,), (1, 2, 3))[k]:
                    betas(t)

            def turn(n, blocks):
                if n >= 3:
                    pe.wait_ge(lo_ready, n - 2)
                for j, block_in in enumerate(blocks):
                    mm = nc.tensor.transpose(psT[:, n % 3, j], block_in, ident[:])
                mm.then_inc(tr_psum, 1)

            pe.wait_ge(ctx_in, 16)
            for n in range(4):
                turn(n, [ctx_sb[:, 4 * n + j] for j in range(4)])
            pe.wait_ge(bias_in, 16 * 9)
            pe.wait_ge(picked_read, 2)
            nc.tensor.transpose(psA[:].rearrange("p g b t -> p (g b t)")[:, 0:CH], bv[:],
                                ident[0:CH, 0:CH]).then_inc(bvT_psum, 1)
            for n in range(4):
                pe.wait_ge(xn_ready, 4 * n + 4)
                turn(4 + n, [xn[:, 4 * n + j] for j in range(4)])
            for n in range(6):
                if n % 2 == 0:
                    pe.wait_ge(w_in[n // 2], 16)
                turn(8 + n, [raw[:, n // 2, 4 * (n % 2) + j] for j in range(4)])
            pe.wait_ge(wo_in, 16)
            for n in range(2):
                turn(14 + n, [raw[:, 3, 4 * n + j] for j in range(4)])
            pe.wait_ge(bvT_ready, 1)
            pe.wait_ge(hi_ready, NTR)
            for c in range(CH):
                mm = nc.tensor.matmul(psA[0:KB].rearrange("p g b t -> p (g b t)")[:, P:2 * P],
                                      bvT[:, c:c + 1].to_broadcast([P, KB]), woT[:, c], start=(c == 0),
                                      stop=(c == CH - 1))
            mm.then_inc(bo_psum, 1)


def attention_loop(nc, T, sb, scope, x_sb, ctxT2, identb, ident, bnst, mv, later, steps,
                   xT2, wT2, woT, kron2, bqk3, bias_pick, bo3, bg3, ones3, beta, alpha, gamma2, least2,
                   arg, turns, whole, wave, emb2, vx2):
    def sem(name):
        return scope.enter_context(nc.semaphore(name))

    qT = sb("qT", [P, 2, CH, P], F32, scope)
    kT = sb("kT", [P, 2, CH, P], F32, scope)
    negmax = sb("negmax", [P, 2, HG], BF16, scope)
    prob = sb("prob", [P, 2, HG, P], F32, scope)
    gprob = sb("gprob", [P, 2, HG, P], F32, scope)
    gprob2 = sb("gprob2", [P, 2, 2, HG, P], F16, scope)
    rsum = sb("rsum", [P, 2, HG], F32, scope)
    att = sb("att", [P, 2, H0, DK], F32, scope)
    attT = sb("attT", [P, CH, P], F32, scope)

    def bank(name):
        return scope.enter_context(nc.psum_tensor(name, [P, HG, P], F32))

    psM, psG, psV = bank("psM"), bank("psG"), bank("psV")
    psS = [bank("psS0"), bank("psS1")]
    aux = [bank("aux0"), bank("aux1"), bank("aux2")]

    pool_gate = sem("pool_gate")
    qp_psum, q_ready, kp_psum, k_ready, vp_psum, vhi_ready, v_ready = (
        sem(n) for n in ("qp_psum", "q_ready", "kp_psum", "k_ready", "vp_psum", "vhi_ready", "v_ready"))
    max_psum, negmax_ready, score_psum, prob_ready, geo_psum, gprob_ready, gphi_ready, gplo_ready = (
        sem(n) for n in ("max_psum", "negmax_ready", "score_psum", "prob_ready", "geo_psum", "gprob_ready",
                         "gphi_ready", "gplo_ready"))
    pv_psum, rsum_ready, att_ready, attT_psum, attT_ready, op_psum, x1_ready, stat_ready = (
        sem(n) for n in ("pv_psum", "rsum_ready", "att_ready", "attT_psum", "attT_ready", "op_psum",
                         "x1_ready", "stat_ready"))
    dist_ready, square_ready, gamma_done, clip_ready, log_ready, turns_ready, whole_ready, frac_ready = (
        sem(n) for n in ("geo_dist_ready", "geo_square_ready", "geo_gamma_done", "geo_clip_ready",
                         "geo_log_ready", "geo_turns_ready", "geo_whole_ready", "geo_frac_ready"))
    wave_ready, emb_hi = sem("geo_wave_ready"), sem("geo_emb_hi")
    max_ready = sem("max_ready")
    emb_lo_even, emb_lo_odd = sem("geo_emb_lo_even"), sem("geo_emb_lo_odd")

    def heads(u):
        first = 2 * HG * (u % 2) + u // 2
        return [first + 2 * j for j in range(HG)]

    def unit(a, u):
        return a[:, heads(u)[0]:heads(u)[-1] + 1:2]

    def made(b):
        return not (isinstance(b, int) and b >= B)

    def flat(a):
        return a.rearrange("p g m -> p (g m)")

    def pair_flat(a):
        return a.rearrange("p b g m -> p (b g m)")

    with nc.Block() as block:
        @block.sync
        def _(sp):
            ffn_in, moe_in, moe_w = later["ffn_in"], later["moe_in"], later["moe_w"]
            sp.dma_start(later["w1"][:], T["L0_ffn_w1"].rearrange("(c p) d -> p c d", p=P)).then_inc(ffn_in, 16)
            sp.dma_start(later["w2"][:], T["L0_ffn_w2"].rearrange("p (c d) -> p c d", d=P)).then_inc(ffn_in, 16)
            with nc.allow_non_contiguous_dma(reason="640 words of biases, once"):
                sp.dma_start(later["b1"][:], T["L0_ffn_b1"].rearrange("(c p) -> p c", p=P)).then_inc(ffn_in, 16)
                sp.dma_start(later["b2"][:], T["L0_ffn_b2"].rearrange("(p o) -> p o", o=1)).then_inc(ffn_in, 16)
            sp.dma_start(later["rw"][:], T["L1_ffn_router_w"]).then_inc(moe_in, 16)
            for k, name in enumerate(("gate", "up")):
                sp.dma_start(moe_w[:, k, 0:EC].rearrange("p c (two f) -> p (c two) f", two=2),
                             T[f"L1_ffn_{name}_w"].rearrange("e p f -> p e f")).then_inc(moe_in, 16)
                sp.dma_start(moe_w[:, k, EC], T[f"L1_ffn_shared_{name}_w"]).then_inc(moe_in, 16)
            sp.dma_start(moe_w[:, 2, 0:EC], T["L1_ffn_down_w"].rearrange("e f d -> (e f) d")
                         .rearrange("(c p) d -> p c d", p=P)).then_inc(moe_in, 16)
            sp.dma_start(moe_w[:, 2, EC], T["L1_ffn_shared_down_w"]).then_inc(moe_in, 16)

        @block.gpsimd
        def _(pool):
            def gated():
                pool.sem_inc(pool_gate, 1)

            def square(g, par):
                pool.wait_ge(dist_ready, g - 1)
                gated()
                nc.gpsimd.tensor_tensor(arg[:, par], arg[:, par], arg[:, par], ALU.mult).then_inc(square_ready, 1)

            def low_emb(g, par):
                pool.wait_ge(emb_hi, g)
                gated()
                nc.gpsimd.tensor_tensor(emb2[:, par, 1], wave[:, par], emb2[:, par, 0],
                                        ALU.subtract).then_inc(emb_lo_odd, 2)

            def low_gprob(b, u):
                pool.wait_ge(gphi_ready, UN * b + u + 1)
                gated()
                nc.gpsimd.tensor_tensor(gprob2[:, u % 2, 1], gprob[:, u % 2], gprob2[:, u % 2, 0],
                                        ALU.subtract).then_inc(gplo_ready, 1)

            def slots(b, par):
                for u in range(UN):
                    if u == 0 and par == 0:
                        low_emb(b + 1, 1)
                    low_gprob(b, u)
                    if par == 0 and u in (0, 1) and made(b + 2):
                        square(b + 2 + u, u)

            over_batches(nc.gpsimd, slots)

        @block.tensor
        def _(pe):
            mm_ = nc.tensor.matmul

            def upper(a):
                return a.bitcast(BF16).rearrange("p (n two) -> p n two", two=2)[:, :, 1]

            def rows_of(h):
                return slice(DK * (h % 2), DK * (h % 2) + DK)

            def transposed_proj(k, src, b, half, into, done):
                mm_(aux[into][:], bqk3[:], bias_pick[:, CH * k + 4 * half:CH * k + 4 * half + 4], start=True,
                    stop=False, skip_group_check=True)
                for j in range(4):
                    c = 4 * half + j
                    for w_part, x_part in ((0, 0), (0, 1), (1, 0)):
                        mm = mm_(aux[into][:, j], wT2[:, k, w_part, c], src[:, x_part, b], start=False,
                                 stop=(j == 3 and w_part == 1), skip_group_check=True)
                mm.then_inc(done, 1)

            def q_proj(b, half, into):
                transposed_proj(0, xT2, b, half, into, qp_psum)

            def k_proj(b, half, into):
                transposed_proj(1, ctxT2, b, half, into, kp_psum)

            def v_proj(b, half, into):
                for n, (x_part, w_part) in enumerate(((0, 0), (0, 1), (1, 0))):
                    mm = mm_(aux[into][:], ctxT2[:, x_part, b], wT2[:, 2, w_part, 4 * half:4 * half + 4],
                             start=(n == 0), stop=(n == 2))
                mm.then_inc(vp_psum, 1)

            def maxima(par, u):
                for j, h in enumerate(heads(u)):
                    mm = mm_(psM[:, j], upper(qT[rows_of(h), par, h // 2]), upper(kT[rows_of(h), par, h // 2]),
                             start=True, stop=True)
                mm.then_inc(max_psum, 1)

            def scores(par, u):
                for j, h in enumerate(heads(u)):
                    mm_(psS[u % 2][:, j], kT[rows_of(h), par, h // 2], qT[rows_of(h), par, h // 2],
                        start=(j == 0), stop=False, skip_group_check=True)
                for j in range(HG):
                    mm = mm_(psS[u % 2][:, j], negmax[:, u % 2, j:j + 1].to_broadcast([P, P]), identb[:],
                             start=False, stop=(j == HG - 1), skip_group_check=True)
                mm.then_inc(score_psum, 1)

            def geometry(par, u):
                mm_(psG[:], ones3[:], unit(bg3, u).unsqueeze(2).to_broadcast([KB, HG, P]), start=True, stop=False, skip_group_check=True)
                for g in range(NG):
                    for e_part, w_part in ((0, 0), (0, 1), (1, 0)):
                        mm = mm_(psG[:, :, GN * g:GN * g + GN], emb2[:, par, e_part, g],
                                 unit(kron2[:, w_part], u), start=False,
                                 stop=(g == NG - 1 and e_part == 1), skip_group_check=True)
                mm.then_inc(geo_psum, 1)

            def pv(par, u):
                v = psV[:].rearrange("p a m -> p (a m)")
                for j, h in enumerate(heads(u)):
                    for p_part, v_part in ((0, 0), (0, 1), (1, 0)):
                        mm = mm_(v[:, j * (DK + 1):(j + 1) * (DK + 1)], gprob2[:, u % 2, p_part, j],
                                 vx2[:, par, v_part, h], start=(j == 0 and p_part + v_part == 0),
                                 stop=(j == HG - 1 and p_part == 1), skip_group_check=True)
                mm.then_inc(pv_psum, 1)

            def att_turn(par, half, into):
                for j in range(4):
                    c = 4 * half + j
                    mm = nc.tensor.transpose(aux[into][:, j], att[:, par, 2 * c:2 * c + 2], ident[:])
                mm.then_inc(attT_psum, 1)

            def out_proj(into):
                mm_(aux[into][:, 0], ones3[:], bo3[:], start=True, stop=False)
                for c in range(CH):
                    mm = mm_(aux[into][:, 0], attT[:, c], woT[:, c], start=False, stop=(c == CH - 1))
                mm.then_inc(op_psum, 1)

            def wait_pv(b, u):
                pe.wait_ge(v_ready, 2 * b + min(u, 1) + 1)
                pe.wait_ge(gplo_ready, UN * b + u + 1)
                after(pe, att_ready, UN * b + u)

            q_proj(0, 0, 2)
            q_proj(0, 1, 0)
            k_proj(0, 0, 1)
            pe.wait_ge(q_ready, 1)
            k_proj(0, 1, 2)
            pe.wait_ge(q_ready, 2)
            pe.wait_ge(k_ready, 2)
            maxima(0, 0)

            def slots(b, par):
                first, last = known(b, 0), known(b, B - 1)
                nxt = 1 - par
                for u in range(UN):
                    pe.wait_ge(negmax_ready, UN * b + u + 1)
                    after(pe, prob_ready, UN * b + u - 1)
                    if u == 0:
                        pe.wait_ge(k_ready, 2 * b + 2)
                        pe.wait_ge(q_ready, 2 * b + 2)
                    scores(par, u)
                    if u < UN - 1:
                        maxima(par, u + 1)
                    if u == 0:
                        after(pe, emb_lo_odd if par else emb_lo_even, b + 1 if par else b)
                    after(pe, gprob_ready, UN * b + u)
                    geometry(par, u)
                    if u > 0:
                        wait_pv(b, u - 1)
                        pv(par, u - 1)
                    elif not first:
                        wait_pv(b - 1, UN - 1)
                        pv(nxt, UN - 1)
                    if u == 0:
                        after(pe, x1_ready, b - 1)
                        v_proj(b, 0, 0)
                        pe.wait_ge(k_ready, 2 * b + 1)
                        v_proj(b, 1, 1)
                    if u == 1:
                        if not first:
                            pe.wait_ge(att_ready, UN * b)
                            pe.wait_ge(v_ready, 2 * b + 1)
                            att_turn(nxt, 0, 0)
                            pe.wait_ge(v_ready, 2 * b + 2)
                            att_turn(nxt, 1, 1)
                        if not last:
                            pe.wait_ge(k_ready, 2 * b + 2)
                            q_proj(b + 1, 0, 2)
                    if u == 2 and not last:
                        pe.wait_ge(v_ready, 2 * b + 2)
                        after(pe, attT_ready, 2 * b)
                        q_proj(b + 1, 1, 0)
                        k_proj(b + 1, 0, 1)
                        pe.wait_ge(q_ready, 2 * (b + 1) + 1)
                        k_proj(b + 1, 1, 2)
                    if u == 3 and not last:
                        pe.wait_ge(q_ready, 2 * (b + 1) + 2)
                        pe.wait_ge(k_ready, 2 * (b + 1) + 2)
                        maxima(nxt, 0)
                    if u == 3 and not first:
                        after(pe, attT_ready, 2 * b)
                        if not last:
                            pe.wait_ge(q_ready, 2 * (b + 1) + 2)
                        out_proj(0)

            over_batches(nc.tensor, slots)
            wait_pv(B - 1, UN - 1)
            pv((B - 1) % 2, UN - 1)
            pe.wait_ge(att_ready, UN * B)
            pe.wait_ge(x1_ready, B - 1)
            for half in range(2):
                att_turn((B - 1) % 2, half, half)
            pe.wait_ge(attT_ready, 2 * B)
            out_proj(0)

        @block.scalar
        def _(act):
            def q_out(b, par, half, frm):
                act.wait_ge(qp_psum, 2 * b + half + 1)
                nc.scalar.copy(qT[:, par, 4 * half:4 * half + 4], aux[frm][:]).then_inc(q_ready, 1)

            def v_hi(b, par, half):
                act.wait_ge(vp_psum, 2 * b + half + 1)
                after(act, pv_psum, UN * (b - 1))
                nc.scalar.copy(vx2[:, par, 0, 8 * half:8 * half + 8, 0:DK],
                               aux[half][:].rearrange("p a m -> p (a m)").rearrange("p (h e) -> p h e", e=DK)
                               ).then_inc(vhi_ready, 1)

            def attT_out(b, half):
                act.wait_ge(attT_psum, 2 * b + half + 1)
                after(act, op_psum, b)
                nc.scalar.copy(attT[:, 4 * half:4 * half + 4], aux[half][:]).then_inc(attT_ready, 1)

            def gprob_hi(b, u):
                act.wait_ge(gprob_ready, UN * b + u + 1)
                after(act, pv_psum, UN * b + u - 1)
                nc.scalar.copy(gprob2[:, u % 2, 0], gprob[:, u % 2]).then_inc(gphi_ready, 1)

            def logs(g, par):
                act.wait_ge(clip_ready, g - 1)
                nc.scalar.activation(arg[:, par], arg[:, par], ACT.Ln).then_inc(log_ready, 1)

            def log_cycles(g, par):
                act.wait_ge(log_ready, g - 1)
                after(act, frac_ready, g - 3)
                nc.scalar.activation(turns[:, par], arg[:, par], ACT.Copy, scale=CYCLES).then_inc(turns_ready, 1)

            def waves(g, par):
                act.wait_ge(frac_ready, g - 1)
                after(act, emb_lo_odd if par else emb_lo_even, g - 1 if par else g - 2)
                nc.scalar.activation(wave[:, par], whole[:, par], ACT.Sin, scale=-TURN).then_inc(wave_ready, 1)

            def high_emb(g, par):
                after(act, wave_ready, g - 1)
                after(act, geo_psum, UN * (g - 1))
                nc.scalar.copy(emb2[:, par, 0], wave[:, par]).then_inc(emb_hi, 1)

            nc.scalar.preload_act_table(ACT.Exp)
            q_out(0, 0, 0, 2)
            q_out(0, 0, 1, 0)

            def slots(b, par):
                first, last = known(b, 0), known(b, B - 1)
                for u in range(UN):
                    act.wait_ge(score_psum, UN * b + u + 1)
                    after(act, gprob_ready, UN * b + u - 1)
                    nc.scalar.activation(prob[:, u % 2], psS[u % 2][:], ACT.Exp,
                                         scale=DK ** -0.5 / W_UP ** 2).then_inc(prob_ready, 1)
                    if u == 0 and par == 0:
                        high_emb(b + 1, 1)
                    if u == 2 and not last:
                        q_out(b + 1, 1 - par, 1, 0)
                    if u == 3 and par == 0 and made(b + 2):
                        logs(b + 2, 0)
                        gprob_hi(b, u)
                        logs(b + 3, 1)
                        nc.scalar.preload_act_table(ACT.Exp)
                    elif u == 2 and par == 1 and made(b + 1):
                        waves(b + 1, 0)
                        gprob_hi(b, u)
                        waves(b + 2, 1)
                        nc.scalar.preload_act_table(ACT.Exp)
                    elif u == 3 and par == 1 and made(b + 1):
                        high_emb(b + 1, 0)
                        gprob_hi(b, u)
                    else:
                        gprob_hi(b, u)
                    if u == 0:
                        v_hi(b, par, 0)
                        v_hi(b, par, 1)
                    if u == 1:
                        if not first:
                            attT_out(b - 1, 0)
                            attT_out(b - 1, 1)
                        if not last:
                            after(act, score_psum, UN * b)
                            q_out(b + 1, 1 - par, 0, 2)
                    if par == 1 and u < 2 and made(b + 1):
                        log_cycles(b + 1 + u, u)

            over_batches(nc.scalar, slots)
            nc.scalar.preload_act_table(ACT.Sqrt)
            attT_out(B - 1, 0)
            attT_out(B - 1, 1)

        @block.vector
        def _(dve):
            v = nc.vector

            def neg_max(b, u):
                dve.wait_ge(max_psum, UN * b + u + 1)
                after(dve, score_psum, UN * b + u - 1)
                v.tensor_reduce(negmax[:, u % 2], psM[:], AX.X, ALU.max, negate=True).then_inc(negmax_ready, 1)

            def weigh(b, u):
                dve.wait_ge(prob_ready, UN * b + u + 1)
                dve.wait_ge(geo_psum, UN * b + u + 1)
                after(dve, gplo_ready, UN * b + u - 1)
                v.scalar_tensor_tensor(out=flat(gprob[:, u % 2]), in0=flat(psG[:]), scalar=1e-6 * G_UP,
                                       in1=flat(prob[:, u % 2]), op0=ALU.max,
                                       op1=ALU.mult).then_inc(gprob_ready, 1)

            def normalise(b, par, u):
                dve.wait_ge(pv_psum, UN * b + u + 1)
                got = psV[:].rearrange("p a m -> p (a m)")[:, 0:HG * (DK + 1)].rearrange("p (h e) -> p h e", h=HG)
                v.reciprocal(rsum[:, u % 2], got[:, :, DK]).then_inc(rsum_ready, 1)
                dve.wait_ge(rsum_ready, UN * b + u + 1)
                after(dve, attT_psum, 2 * b - 2)
                v.tensor_tensor(unit(att[:, par], u), got[:, :, 0:DK],
                                rsum[:, u % 2].unsqueeze(2).to_broadcast([P, HG, DK]),
                                ALU.mult).then_inc(att_ready, 1)

            def k_out(b, par, half, frm):
                dve.wait_ge(kp_psum, 2 * b + half + 1)
                v.tensor_copy(kT[:, par, 4 * half:4 * half + 4], aux[frm][:]).then_inc(k_ready, 1)

            def v_lo(b, par, half):
                dve.wait_ge(vhi_ready, 2 * b + half + 1)
                v.tensor_tensor(vx2[:, par, 1, 8 * half:8 * half + 8, 0:DK],
                                aux[half][:].rearrange("p a m -> p (a m)").rearrange("p (h e) -> p h e", e=DK),
                                vx2[:, par, 0, 8 * half:8 * half + 8, 0:DK], ALU.subtract).then_inc(v_ready, 1)

            def residual(b):
                dve.wait_ge(op_psum, b + 1)
                v.tensor_tensor(x_sb[:, b], x_sb[:, b], aux[0][:, 0], ALU.add).then_inc(x1_ready, 1)
                dve.wait_ge(x1_ready, b + 1)
                v.bn_stats(bnst[:, b], x_sb[:, b]).then_inc(stat_ready, 1)
                v.tensor_reduce(later["rowmax"][:, b], x_sb[:, b], AX.X, ALU.max).then_inc(max_ready, 1)

            def distance(g, par):
                after(dve, turns_ready, g - 3)
                v.tensor_tensor(arg[:, par], beta[:, g].unsqueeze(1).to_broadcast([P, NG, P]),
                                alpha[:, g].unsqueeze(2).to_broadcast([P, NG, P]),
                                ALU.subtract).then_inc(dist_ready, 1)

            def clip(g, par):
                dve.wait_ge(square_ready, g - 1)
                v.tensor_tensor(arg[:, par], arg[:, par], gamma2[:, g].unsqueeze(2).to_broadcast([P, NG, P]),
                                ALU.mult).then_inc(gamma_done, 1)
                dve.wait_ge(gamma_done, g - 1)
                v.tensor_scalar(flat(arg[:, par]), flat(arg[:, par]), least2[:, 0:1], None,
                                ALU.max).then_inc(clip_ready, 1)

            def low_emb(g, par):
                dve.wait_ge(emb_hi, g)
                v.tensor_tensor(emb2[:, par, 1], wave[:, par], emb2[:, par, 0],
                                ALU.subtract).then_inc(emb_lo_even, 2)

            def whole_cycles(g, par):
                dve.wait_ge(log_ready, g - 1)
                after(dve, wave_ready, g - 3)
                v.tensor_scalar(flat(whole[:, par]), flat(arg[:, par]), CYCLES, ROUND, ALU.mult,
                                ALU.add).then_inc(whole_ready, 1)

            def fraction(g, par):
                dve.wait_ge(whole_ready, g - 1)
                dve.wait_ge(turns_ready, g - 1)
                v.scalar_tensor_tensor(out=flat(whole[:, par]), in0=flat(whole[:, par]), scalar=ROUND,
                                       in1=flat(turns[:, par]), op0=ALU.subtract,
                                       op1=ALU.subtract).then_inc(frac_ready, 1)

            k_out(0, 0, 0, 1)
            k_out(0, 0, 1, 2)
            neg_max(0, 0)

            def slots(b, par):
                first, last = known(b, 0), known(b, B - 1)
                for u in range(UN):
                    if u < UN - 1:
                        neg_max(b, u + 1)
                    elif not last:
                        neg_max(b + 1, 0)
                    weigh(b, u)
                    if u > 0:
                        normalise(b, par, u - 1)
                    elif not first:
                        normalise(b - 1, 1 - par, UN - 1)
                    if u == 0:
                        v_lo(b, par, 0)
                        v_lo(b, par, 1)
                    if u == 2 and not last:
                        k_out(b + 1, 1 - par, 0, 1)
                        k_out(b + 1, 1 - par, 1, 2)
                    if par == 1 and u == 3 and made(b + 1):
                        low_emb(b + 1, 0)
                    if u == 3 and not first:
                        residual(b - 1)
                    if par == 0 and made(b + 2):
                        if u < 2:
                            distance(b + 2 + u, u)
                        if u in (1, 2):
                            clip(b + 1 + u, u - 1)
                    if par == 1 and u == 0 and made(b + 1):
                        whole_cycles(b + 1, 0)
                    if par == 1 and u == 1 and made(b + 1):
                        fraction(b + 1, 0)
                        whole_cycles(b + 2, 1)
                        fraction(b + 2, 1)
                    if known(b, B - 2) and u < 3:
                        quantise_weights(nc, dve, steps["dve"].on(dve), later, u)

            over_batches(nc.vector, slots)
            normalise(B - 1, (B - 1) % 2, UN - 1)
            dve.wait_ge(stat_ready, B - 1)
            aggregate(v, steps["dve"].on(dve), mv, bnst, range(B - 1))
            residual(B - 1)


def quantise_weights(nc, dve, order, later, stage):
    v = nc.vector
    w1, w2, ws, wr = later["w1"], later["w2"], later["ws"], later["wr"]
    if stage == 0:
        dve.wait_ge(later["ffn_in"], 16 * 4)
        order.add(v.tensor_reduce(ws[:, 0:FC], w1[:], AX.X, ALU.max, apply_absolute_value=True))
        order.add(v.tensor_reduce(ws[:, FC:], w2[:], AX.XY, ALU.max, apply_absolute_value=True))
    if stage == 1:
        order.sync()
        order.then(v.tensor_scalar(ws[:], ws[:], Q_EPS, 1.0 / 127.0, ALU.max, ALU.mult))
        order.then(v.reciprocal(wr[:], ws[:]))
        for c in range(FC):
            order.add(v.tensor_scalar(w1[:, c], w1[:, c], wr[:, c:c + 1], ROUND, ALU.mult, ALU.add))
        order.add(v.tensor_scalar(w2[:], w2[:], wr[:, FC:], ROUND, ALU.mult, ALU.add))
    if stage == 2:
        order.sync()
        for w in (w1, w2):
            order.add(v.tensor_scalar(w[:], w[:], ROUND, -128.0, ALU.subtract, ALU.max))
        order.sync()
        for w, q in ((w1, later["q1"]), (w2, later["q2"])):
            v.tensor_scalar(q[:], w[:], 127.0, None, ALU.min).then_inc(later["q_ready"], 1)


def expert_halves(later):
    found = []
    for k in range(3):
        found.append((later["moe_w"][:, k].rearrange("p c d -> p (c d)"),
                      later["moe_w2"][:, k, 0].rearrange("p c d -> p (c d)"),
                      later["moe_w2"][:, k, 1].rearrange("p c d -> p (c d)")))
    found.append((later["rw"][:], later["rw2"][:, 0], later["rw2"][:, 1]))
    return found


def aggregate(v, order, mv, bnst, rows):
    for b in rows:
        order.add(v.bn_aggr(mv[:, b], bnst[:, b]))


def layernorm_all(v, steps, count, order, dve, first, bnst, mv, rstd, eps=LN_EPS):
    aggregate(v, order, mv, bnst, range(first, B))
    order.sync()
    v.tensor_scalar(rstd[:], mv[:, :, 1], eps, None, ALU.add).then_inc(steps["asked"], 1)
    dve.wait_ge(steps["given"], count)
    order.then(v.reciprocal(rstd[:], rstd[:]))
    v.scalar_tensor_tensor(out=steps["shift"][:], in0=mv[:, :, 0], scalar=-1.0, in1=rstd[:], op0=ALU.mult,
                           op1=ALU.mult).then_inc(steps["shift_ready"], 1)


ACT_XN = 1


def dve_normalises(v, steps, t, xn, x_sb, mv, rstd):
    for b in range(4 * t, 4 * t + 4 - ACT_XN):
        v.tensor_scalar(xn[:, b], x_sb[:, b], mv[:, b, 0:1], rstd[:, b:b + 1],
                        ALU.subtract, ALU.mult).then_inc(steps["dve_xn"], 1)


def act_normalises(nc, act, steps, phase, xn, x_sb, rstd):
    act.wait_ge(steps["shift_ready"], phase)
    for b in range(B):
        if b % 4 >= 4 - ACT_XN:
            nc.scalar.activation(xn[:, b], x_sb[:, b], ACT.Identity, bias=steps["shift"][:, b:b + 1],
                                 scale=rstd[:, b:b + 1]).then_inc(steps["act_xn"], 1)


def wait_normalised(pe, steps, phase, t):
    groups = B // 4 * (phase - 1) + t + 1
    pe.wait_ge(steps["dve_xn"], (4 - ACT_XN) * groups)
    pe.wait_ge(steps["act_xn"], ACT_XN * groups)


def ffn_phase(nc, sb, scope, x_sb, ident, identb, bnst, mv, rstd, steps, later):
    TG = 4
    NT = B // TG
    BY_ACT = (2, 2, 2, FC)

    def sem(name):
        return scope.enter_context(nc.semaphore(name))

    q1, q2, b1, b2, ws, q_ready = (later[k] for k in ("q1", "q2", "b1", "b2", "ws", "q_ready"))
    q1T = sb("q1T", [P, FC, P], BF16, scope)
    q2T = sb("q2T", [P, FC, P], BF16, scope)
    sc1 = sb("sc1", [P, FC], F32, scope)
    rc1 = sb("rc1", [P, FC], F32, scope)
    sc2 = sb("sc2", [P, 2], F32, scope)
    xn = sb("xn2", [P, B, P], F32, scope)
    xq = sb("xq", [P, B, P], BF16, scope)
    xf = sb("xf", [P, 2, TG * P], F32, scope)
    hid = sb("hid", [P, NT, FC, TG * P], F32, scope)
    hq = sb("hq", [P, NT, FC, TG * P], BF16, scope)
    hmax = sb("hmax", [P, NT * FC], F32, scope)
    top = sb("top", [P, 2], F32, scope)
    topall = sb("topall", [P, 2], F32, scope)
    inv = sb("inv", [P, 2], F32, scope)
    step = sb("step", [P, 2], F32, scope)
    row2 = sb("row2", [P, 2, P], F32, scope)
    round_ = sb("round_", [P, 1], F32, scope)

    psT = [scope.enter_context(nc.psum_tensor(f"psFT{i}", [P, TG, P], F32)) for i in range(2)]
    psW = scope.enter_context(nc.psum_tensor("psFW", [P, FC, 2 * P], BF16))
    psH = [scope.enter_context(nc.psum_tensor(f"psFH{i}", [P, TG * P], F32)) for i in range(2)]
    psY = [scope.enter_context(nc.psum_tensor(f"psFY{i}", [P, TG, P], F32)) for i in range(2)]
    psR = scope.enter_context(nc.psum_tensor("psFR", [P, 2, P], F32))

    y_ready = sem("ffn_y_ready")
    top_ready, topall_ready, inv_ready, qT_psum, qT_ready, b2_added = (
        sem(n) for n in ("ffn_top_ready", "ffn_topall_ready", "ffn_inv_ready", "ffn_qT_psum", "ffn_qT_ready",
                         "ffn_b2_added"))
    xT_psum, xf_ready, xq_ready, h_psum, hid_ready, sc1_ready = (
        sem(n) for n in ("ffn_xT_psum", "ffn_xf_ready", "ffn_xq_ready", "ffn_h_psum", "ffn_hid_ready",
                         "ffn_sc1_ready"))
    hr_ready, hq_ready, y_psum, sc2_ready, row_psum, row_ready, y_done = (
        sem(n) for n in ("ffn_hr_ready", "ffn_hq_ready", "ffn_y_psum", "ffn_sc2_ready", "ffn_row_psum",
                         "ffn_row_ready", "ffn_y_done"))

    with nc.Block() as block:
        @block.gpsimd
        def _(pool):
            order = steps["pool"].on(pool)
            order.add(nc.gpsimd.memset(round_[:], ROUND))
            for k in range(2):
                pool.wait_ge(top_ready, k + 1)
                order.sync()
                nc.gpsimd.partition_all_reduce(topall[:, k:k + 1], top[:, k:k + 1], P, RMAX).then_inc(topall_ready, 1)
            pool.wait_ge(row_ready, 1)
            for t in range(NT):
                xs = x_sb[:, TG * t:TG * t + TG]
                nc.gpsimd.tensor_tensor(xs, xs, row2[:, 1].unsqueeze(1).to_broadcast([P, TG, P]),
                                        ALU.add).then_inc(b2_added, 1)
            for t in range(NT):
                xs = x_sb[:, TG * t:TG * t + TG]
                pool.wait_ge(b2_added, t + 1)
                pool.wait_ge(y_ready, t + 1)
                nc.gpsimd.tensor_tensor(xs, xs, xn[:, TG * t:TG * t + TG], ALU.add).then_inc(y_done, 1)

        @block.scalar
        def _(act):
            act.wait_ge(steps["asked"], 2)
            nc.scalar.activation(rstd[:], rstd[:], ACT.Sqrt).then_inc(steps["given"], 1)
            act.wait_ge(qT_psum, 1)
            nc.scalar.copy(q1T[:], psW[:, :, 0:P]).then_inc(qT_ready, 1)
            act_normalises(nc, act, steps, 1, xn, x_sb, rstd)
            act.wait_ge(qT_psum, 2)
            nc.scalar.copy(q2T[:], psW[:, :, 0:P]).then_inc(qT_ready, 1)
            act.wait_ge(inv_ready, 1)
            for t in range(NT):
                act.wait_ge(xT_psum, t + 1)
                if t >= 2:
                    act.wait_ge(xq_ready, t - 1)
                nc.scalar.activation(xf[:, t % 2], psT[t % 2][:].rearrange("p b d -> p (b d)"), ACT.Relu,
                                     scale=inv[:, 0:1]).then_inc(xf_ready, 1)
            act.wait_ge(sc1_ready, 1)
            for t in range(NT):
                for c in range(FC):
                    n = FC * t + c
                    act.wait_ge(h_psum, n + 1)
                    nc.scalar.activation(hid[:, t, c], psH[n % 2][:], ACT.Relu, bias=b1[:, c:c + 1],
                                         scale=sc1[:, c:c + 1]).then_inc(hid_ready, 1)
            act.wait_ge(inv_ready, 2)
            for t in range(NT):
                for c in range(BY_ACT[t]):
                    nc.scalar.activation(hid[:, t, c], hid[:, t, c], ACT.Identity, bias=round_[:, 0:1],
                                         scale=inv[:, 1:2]).then_inc(hr_ready, 1)
            act.wait_ge(later["moe_in"], 16 * 7)
            for raw, hi, _ in expert_halves(later):
                nc.scalar.activation(hi, raw, ACT.Copy, scale=W_UP).then_inc(later["moe_hi"], 1)

        @block.vector
        def _(dve):
            v = nc.vector
            order = steps["dve"].on(dve)
            def scales(k):
                dve.wait_ge(topall_ready, k + 1)
                order.then(v.tensor_scalar(step[:, k:k + 1], topall[:, k:k + 1], Q_EPS, 1.0 / 255.0,
                                           ALU.max, ALU.mult))
                order.then(v.reciprocal(inv[:, k:k + 1], step[:, k:k + 1]))
                v.engine_nop().then_inc(inv_ready, 1)

            layernorm_all(v, steps, 2, order, dve, B - 1, bnst, mv, rstd)
            rowmax = later["rowmax"][:].rearrange("p b o -> p (b o)")
            order.then(v.tensor_tensor(rowmax, rowmax, mv[:, :, 0], ALU.subtract))
            order.then(v.tensor_tensor(rowmax, rowmax, rstd[:], ALU.mult))
            v.tensor_reduce(top[:, 0:1], rowmax, AX.X, ALU.max).then_inc(top_ready, 1)
            for t in range(NT):
                dve_normalises(v, steps, t, xn, x_sb, mv, rstd)
                if t == 0:
                    scales(0)

            def quant_bias(bias, sc, rc):
                order.then(v.reciprocal(rc, sc))
                order.then(v.tensor_tensor(bias, bias, rc, ALU.mult))
                order.then(v.tensor_scalar(bias, bias, ROUND, None, ALU.add))
                order.then(v.tensor_scalar(bias, bias, ROUND, None, ALU.subtract))
                order.then(v.tensor_tensor(bias, bias, sc, ALU.mult))

            for t in range(NT):
                dve.wait_ge(xf_ready, t + 1)
                order.then(v.tensor_scalar(xf[:, t % 2], xf[:, t % 2], 255.0, ROUND, ALU.min, ALU.add))
                v.tensor_scalar(xq[:, TG * t:TG * t + TG].rearrange("p b d -> p (b d)"), xf[:, t % 2], ROUND,
                                None, ALU.subtract).then_inc(xq_ready, 1)
                if t == 0:
                    order.then(v.tensor_scalar(sc1[:], ws[:, 0:FC], step[:, 0:1], None, ALU.mult))
                    quant_bias(b1[:], sc1[:], rc1[:])
                    v.engine_nop().then_inc(sc1_ready, 1)
            for n in range(NT * FC):
                dve.wait_ge(hid_ready, n + 1)
                order.add(v.tensor_reduce(hmax[:, n:n + 1], hid[:, n // FC, n % FC], AX.X, ALU.max))
            order.sync()
            v.tensor_reduce(top[:, 1:2], hmax[:], AX.X, ALU.max).then_inc(top_ready, 1)
            scales(1)

            def rounded(t):
                for c in range(BY_ACT[t], FC):
                    order.add(v.tensor_scalar(hid[:, t, c], hid[:, t, c], inv[:, 1:2], ROUND, ALU.mult, ALU.add))

            def whole(t):
                order.sync()
                dve.wait_ge(hr_ready, sum(BY_ACT[:t + 1]))
                v.tensor_scalar(hq[:, t], hid[:, t], ROUND, 255.0, ALU.subtract, ALU.min).then_inc(hq_ready, 1)

            def scaled(t):
                dve.wait_ge(y_psum, t + 1)
                v.tensor_tensor(xn[:, TG * t:TG * t + TG], psY[t % 2][:],
                                row2[:, 0].unsqueeze(1).to_broadcast([P, TG, P]), ALU.mult).then_inc(y_ready, 1)

            def statistics(t):
                dve.wait_ge(y_done, t + 1)
                for b in range(TG * t, TG * t + TG):
                    order.add(v.bn_stats(bnst[:, b], x_sb[:, b]))

            rounded(0)
            order.then(v.tensor_scalar(sc2[:, 0:1], ws[:, FC:], step[:, 1:2], None, ALU.mult))
            order.then(v.tensor_copy(sc2[:, 1:2], b2[:]))
            quant_bias(sc2[:, 1:2], sc2[:, 0:1], rc1[:, 0:1])
            v.engine_nop().then_inc(sc2_ready, 1)
            whole(0)
            dve.wait_ge(row_psum, 1)
            v.tensor_copy(row2[:], psR[:]).then_inc(row_ready, 1)
            rounded(1)
            whole(1)
            rounded(2)
            whole(2)
            dve.wait_ge(row_ready, 1)
            scaled(0)
            whole(3)
            for t in range(NT):
                if t:
                    scaled(t)
                    statistics(t - 1)
            order.sync()
            aggregate(v, order, mv, bnst, range(B - TG))
            statistics(NT - 1)

        @block.tensor
        def _(pe):
            mm_ = nc.tensor.matmul
            for k, q in enumerate((q1, q2)):
                pe.wait_ge(q_ready, k + 1)
                if k:
                    pe.wait_ge(qT_ready, k)
                for c in range(FC):
                    mm = nc.tensor.transpose(psW[:, c, 0:P], q[:, c], identb[:])
                mm.then_inc(qT_psum, 1)
            for t in range(NT):
                wait_normalised(pe, steps, 1, t)
                if t >= 2:
                    pe.wait_ge(xf_ready, t - 1)
                for j in range(TG):
                    mm = nc.tensor.transpose(psT[t % 2][:, j], xn[:, TG * t + j], ident[:])
                mm.then_inc(xT_psum, 1)
            pe.wait_ge(qT_ready, 2)
            for t in range(NT):
                pe.wait_ge(xq_ready, t + 1)
                for c in range(FC):
                    n = FC * t + c
                    if n >= 2:
                        pe.wait_ge(hid_ready, n - 1)
                    mm_(psH[n % 2][:], q1T[:, c], xq[:, TG * t:TG * t + TG], start=True,
                        stop=True).then_inc(h_psum, 1)
            pe.wait_ge(sc2_ready, 1)
            for k in range(2):
                mm = mm_(psR[:, k], sc2[:, k:k + 1].to_broadcast([P, P]), ident[:], start=True, stop=True)
            mm.then_inc(row_psum, 1)
            for t in range(NT):
                pe.wait_ge(hq_ready, t + 1)
                if t >= 2:
                    pe.wait_ge(y_ready, t - 1)
                for j in range(TG):
                    for c in range(FC):
                        mm = mm_(psY[t % 2][:, j], hq[:, t, c, j * P:(j + 1) * P], q2T[:, c],
                                 start=(c == 0), stop=(c == FC - 1))
                mm.then_inc(y_psum, 1)


def mlstm_phase(nc, T, sb, scope, x_sb, ctx_sb, ctxT2, ident, identb, bnst, mv, rstd, steps, later):
    G = 2
    GH = H1 // G
    VW = HW1 + 1
    POOL_H = 7
    PARTS = ((0, 0), (0, 1), (1, 0))

    def sem(name):
        return scope.enter_context(nc.semaphore(name))

    xn = sb("xn3", [P, B, P], F32, scope)
    qT2 = sb("qT2", [P, 2, B, P], F16, scope)
    gk = sb("gk", [P, 3, 2, H1], F32, scope)
    gk2 = sb("gk2", [P, 2, 3, 2 * H1], F16, scope)
    gb = sb("gb", [P, 2, H1], F32, scope)
    gates = sb("gates", [P, 2, B, H1], F32, scope)
    low = sb("low", [P, P], F32, scope)
    soft = sb("soft", [P, P], F32, scope)
    zeros = sb("zeros", [P, P], F32, scope)
    ones = sb("ones", [P, P], F32, scope)
    csum = sb("csum", [P, P], F32, scope)
    gain = sb("gain", [P, P], F32, scope)
    peak = sb("peak", [P, P], F32, scope)
    guard = sb("guard", [P, P], F32, scope)
    peak3 = sb("peak3", [P, NSPLIT, P], BF16, scope)
    gainT = sb("gainT", [P, B, H1], F32, scope)
    eguard = sb("eguard", [P, B, H1], F32, scope)
    peakR = sb("peakR", [NSPLIT, B, H1, P], BF16, scope)
    minus = sb("minus", [NSPLIT, P], BF16, scope)
    future = sb("future", [P, P], BF16, scope)
    headm = sb("headm", [P, H1], F32, scope)
    bias_now = sb("bias_now", [P, 2, H1], F32, scope)
    qm2 = sb("qm2", [P, 2, 2, H1, P], F16, scope)
    v2 = sb("v2", [P, 2, B, H1, VW], F16, scope)
    decay = sb("decay", [P, G, GH, P], F32, scope)
    cmat = sb("cmat", [P, 2, H1, P], F32, scope)
    cmat2 = sb("cmat2", [P, 2, 2, H1, P], F16, scope)
    num = sb("num", [P, B, H1, VW], F32, scope)
    square = sb("square", [P, 2, H1, HW1], F32, scope)
    msq = sb("msq", [P, B, H1], F32, scope)
    factor = sb("factor", [P, B, H1], F32, scope)
    tmp = sb("tmp3", [P, B, H1], F32, scope)

    with ExitStack() as prep, nc.Block() as block:
        psT = [prep.enter_context(nc.psum_tensor(f"psMT{i}", [P, 4, P], F32)) for i in range(2)]
        psI = prep.enter_context(nc.psum_tensor("psMI", [P, B, 2, H1], F32))
        psF = prep.enter_context(nc.psum_tensor("psMF", [P, 2, P], F32))
        psE = prep.enter_context(nc.psum_tensor("psME", [P, 2, P], F32))
        w_in, parts_ready = sem("ml_w_in"), sem("ml_parts_ready")
        qT_psum, qhi_ready, qlo_ready, gk_ready, gate_psum, gates_ready, gatesT_psum = (
            sem(n) for n in ("ml_qT_psum", "ml_qhi_ready", "ml_qlo_ready", "ml_gk_ready", "ml_gate_psum",
                             "ml_gates_ready", "ml_gatesT_psum"))
        abs_ready, soft_ready, gain_ready, guard_ready, gainT_psum, guard_psum, eg_ready, vhi_ready = (
            sem(n) for n in ("ml_abs_ready", "ml_soft_ready", "ml_gain_ready", "ml_guard_ready",
                             "ml_gainT_psum", "ml_guard_psum", "ml_eg_ready", "ml_vhi_ready"))

        @block.sync
        def _(sp):
            for k, name in enumerate(("L1_xattn_igate", "L1_xattn_fgate")):
                with nc.allow_non_contiguous_dma(reason="small gate weights, once"):
                    sp.dma_start(gk[:, :, k], T[name + "_kernel"].rearrange("(s p) h -> p s h", p=P)).then_inc(w_in, 16)
                sp.dma_start(gb[:, k], T[name + "_bias"].rearrange("(o h) -> o h", o=1)
                             .to_broadcast([P, H1])).then_inc(w_in, 16)
            for part in range(NSPLIT):
                sp.wait_ge(parts_ready, part + 1)
                sp.dma_start(peakR[part:part + 1].rearrange("o b h q -> o (b h) q"),
                             peak3[:, part]).then_inc(w_in, 16)

        @block.gpsimd
        def _(pool):
            order = steps["pool"].on(pool)
            g = nc.gpsimd
            order.add(g.memset(future[:], MASKED))
            order.add(g.memset(headm[:], HW1 ** -0.5))
            order.add(g.memset(minus[:], -1.0))
            order.add(g.memset(v2[:, 0, :, :, HW1:], 1.0))
            order.add(g.memset(v2[:, 1, :, :, HW1:], 0.0))
            order.sync()
            order.add(g.affine_select(out=future[:], in_=future[:], compare_op=ALU.is_gt, fill=0.0,
                                      base=0, pattern=[[-1, P]], channel_multiplier=1))
            order.then(g.affine_select(out=headm[:], in_=headm[:], compare_op=ALU.is_ge, fill=0.0,
                                       base=0, pattern=[[-HW1, H1]], channel_multiplier=1))
            order.add(g.affine_select(out=headm[:], in_=headm[:], compare_op=ALU.is_ge, fill=0.0,
                                      base=HW1 - 1, pattern=[[HW1, H1]], channel_multiplier=-1))
            pool.wait_ge(vhi_ready, 1)
            order.add(g.tensor_tensor(v2[:, 1, :, :, 0:HW1], ctx_sb[:].rearrange("p b (h e) -> p b h e", h=H1),
                                      v2[:, 0, :, :, 0:HW1], ALU.subtract))

        @block.scalar
        def _(act):
            act.wait_ge(steps["asked"], 3)
            nc.scalar.activation(rstd[:], rstd[:], ACT.Sqrt).then_inc(steps["given"], 1)
            nc.scalar.preload_act_table(ACT.Exp)
            act_normalises(nc, act, steps, 2, xn, x_sb, rstd)
            for t in range(4):
                act.wait_ge(qT_psum, t + 1)
                nc.scalar.copy(qT2[:, 0, 4 * t:4 * t + 4], psT[t % 2][:]).then_inc(qhi_ready, 1)
            nc.scalar.copy(v2[:, 0, :, :, 0:HW1],
                           ctx_sb[:].rearrange("p b (h e) -> p b h e", h=H1)).then_inc(vhi_ready, 1)
            act.wait_ge(abs_ready, 1)
            nc.scalar.activation(soft[:], soft[:], ACT.Exp, scale=-1.0).then_inc(soft_ready, 1)
            act.wait_ge(soft_ready, 1)
            nc.scalar.activation(soft[:], soft[:], ACT.Ln, bias=1.0).then_inc(soft_ready, 1)
            nc.scalar.preload_act_table(ACT.Exp)
            act.wait_ge(guard_psum, 1)
            nc.scalar.activation(eguard[:].rearrange("p b h -> p (b h)"), psE[:, 1], ACT.Exp,
                                 scale=-1.0).then_inc(eg_ready, 1)

        @block.vector
        def _(dve):
            v = nc.vector
            order = steps["dve"].on(dve)
            layernorm_all(v, steps, 3, order, dve, B - 4, bnst, mv, rstd)
            for t in range(4):
                dve_normalises(v, steps, t, xn, x_sb, mv, rstd)
            order.add(v.memset(zeros[:], 0.0))
            order.add(v.memset(ones[:], 1.0))
            dve.wait_ge(w_in, 16 * 4)
            flat_gk = gk[:].rearrange("p s k h -> p s (k h)")
            order.then(v.tensor_scalar(gk2[:, 0], flat_gk, W_UP, None, ALU.mult))
            v.scalar_tensor_tensor(out=gk2[:, 1], in0=flat_gk, scalar=W_UP, in1=gk2[:, 0], op0=ALU.mult,
                                   op1=ALU.subtract).then_inc(gk_ready, 1)
            for t in range(4):
                dve.wait_ge(qhi_ready, t + 1)
                v.tensor_tensor(qT2[:, 1, 4 * t:4 * t + 4], psT[t % 2][:], qT2[:, 0, 4 * t:4 * t + 4],
                                ALU.subtract).then_inc(qlo_ready, 1)
            for n, (raw, hi, lo) in enumerate(expert_halves(later)):
                dve.wait_ge(later["moe_hi"], n + 1)
                v.scalar_tensor_tensor(out=lo, in0=raw, scalar=W_UP, in1=hi, op0=ALU.mult,
                                       op1=ALU.subtract).then_inc(later["moe_lo"], 1)
            dve.wait_ge(gate_psum, 1)
            for k in range(2):
                v.scalar_tensor_tensor(out=gates[:, k], in0=psI[:, :, k], scalar=1.0 / W_UP,
                                       in1=gb[:, k].unsqueeze(1).to_broadcast([P, B, H1]), op0=ALU.mult,
                                       op1=ALU.add).then_inc(gates_ready, 1)
            dve.wait_ge(gatesT_psum, 1)
            order.then(v.tensor_scalar(low[:], psF[:, 1], 0.0, None, ALU.min))
            v.scalar_tensor_tensor(out=soft[:], in0=low[:], scalar=-2.0, in1=psF[:, 1], op0=ALU.mult,
                                   op1=ALU.add).then_inc(abs_ready, 1)
            dve.wait_ge(soft_ready, 2)
            order.then(v.tensor_tensor(low[:], low[:], soft[:], ALU.subtract))
            order.then(v.tensor_tensor_scan(csum[:], ones[:], low[:], 0.0, ALU.mult, ALU.add))
            v.tensor_tensor(gain[:], psF[:, 0], csum[:], ALU.subtract).then_inc(gain_ready, 1)
            dve.wait_ge(gain_ready, 1)
            order.then(v.tensor_tensor_scan(peak[:], zeros[:], gain[:], MASKED, ALU.add, ALU.max))
            v.tensor_tensor(guard[:], csum[:], peak[:], ALU.add).then_inc(guard_ready, 1)
            dve.wait_ge(guard_ready, 1)
            for part in range(NSPLIT):
                v.tensor_copy(peak3[:, part], peak[:]).then_inc(parts_ready, 1)
                dve.wait_ge(parts_ready, part + 1)
                if part < NSPLIT - 1:
                    order.then(v.tensor_tensor(peak[:], peak[:], peak3[:, part], ALU.subtract))
            dve.wait_ge(gainT_psum, 1)
            dve.wait_ge(eg_ready, 1)
            order.then(v.tensor_copy(gainT[:].rearrange("p b h -> p (b h)"), psE[:, 0]))

        @block.tensor
        def _(pe):
            mm_ = nc.tensor.matmul
            for t in range(4):
                wait_normalised(pe, steps, 2, t)
                if t >= 2:
                    pe.wait_ge(qlo_ready, t - 1)
                for j in range(4):
                    mm = nc.tensor.transpose(psT[t % 2][:, j], xn[:, 4 * t + j], ident[:])
                mm.then_inc(qT_psum, 1)
            pe.wait_ge(gk_ready, 1)
            pe.wait_ge(qlo_ready, 4)
            for b in range(B):
                for s, src in enumerate((ctxT2, ctxT2, qT2)):
                    for x_part, w_part in PARTS:
                        mm = mm_(psI[:, b].rearrange("p k h -> p (k h)"), src[:, x_part, b],
                                 gk2[:, w_part, (1, 2, 0)[s]], start=(b == 0 and s == 0 and x_part + w_part == 0),
                                 stop=(b == B - 1 and s == 2 and x_part == 1), skip_group_check=True)
            mm.then_inc(gate_psum, 1)
            pe.wait_ge(gates_ready, 2)
            for k in range(2):
                mm = nc.tensor.transpose(psF[:, k], gates[:, k].rearrange("p b h -> p (b h)"), ident[:])
            mm.then_inc(gatesT_psum, 1)
            pe.wait_ge(gain_ready, 1)
            nc.tensor.transpose(psE[:, 0], gain[:], ident[:]).then_inc(gainT_psum, 1)
            pe.wait_ge(guard_ready, 1)
            nc.tensor.transpose(psE[:, 1], guard[:], ident[:]).then_inc(guard_psum, 1)

    with ExitStack() as loop, nc.Block() as block:
        psS = [loop.enter_context(nc.psum_tensor(f"psMS{i}", [P, GH, P], F32)) for i in range(G)]
        psA = [loop.enter_context(nc.psum_tensor(f"psMA{i}", [P, GH, P], F32)) for i in range(G)]
        psN = loop.enter_context(nc.psum_tensor("psMN", [P, H1, VW], F32))
        gate_, staged, bias_ready, s_psum, a_psum, d_ready, c_ready, chi_ready, clo_ready, n_psum, n_ready = (
            sem(n) for n in ("ml_pool_gate", "ml_staged", "ml_bias_ready", "ml_s_psum", "ml_a_psum", "ml_d_ready",
                             "ml_c_ready", "ml_chi_ready", "ml_clo_ready", "ml_n_psum", "ml_n_ready"))
        sq_ready, ms_ready, x_ready = (sem(n) for n in ("ml_sq_ready", "ml_ms_ready", "ml_x_ready"))
        y_ready, last_staged = sem("ml_y_ready"), sem("ml_last_staged")

        @block.gpsimd
        def _(pool):
            def stage(b, par):
                after(pool, s_psum, 2 * b - 2)
                pool.sem_inc(gate_, 1)
                for part in range(2):
                    nc.gpsimd.tensor_tensor(qm2[:, par, part, 0:POOL_H],
                                            qT2[:, part, b].unsqueeze(1).to_broadcast([P, POOL_H, P]),
                                            headm[:, 0:POOL_H].unsqueeze(2).to_broadcast([P, POOL_H, P]),
                                            ALU.mult).then_inc(staged, 1)
            over_batches(nc.gpsimd, stage)
            for t in range(4):
                bs = slice(4 * t, 4 * t + 4)
                pool.wait_ge(y_ready, t + 1)
                nc.gpsimd.tensor_tensor(x_sb[:, bs], x_sb[:, bs], xn[:, bs], ALU.add).then_inc(x_ready, 1)

        @block.tensor
        def _(pe):
            mm_ = nc.tensor.matmul

            def values(b, par):
                pe.wait_ge(clo_ready, 2 * b + 2)
                after(pe, n_ready, b)
                for h in range(H1):
                    for c_part, v_part in PARTS:
                        mm = mm_(psN[:, h], cmat2[:, par, c_part, h], v2[:, v_part, b, h],
                                 start=(h == 0 and c_part + v_part == 0), stop=(h == H1 - 1 and c_part == 1),
                                 skip_group_check=True)
                mm.then_inc(n_psum, 1)

            def slots(b, par):
                for g in range(G):
                    after(pe, d_ready, 2 * b + g - 1)
                    mm_(psA[g][:], identb[:], future[:].unsqueeze(1).to_broadcast([P, GH, P]), start=True,
                        stop=False, skip_group_check=True)
                    if known(b, 0):
                        pe.wait_ge(w_in, 16 * (4 + NSPLIT))
                    mm = mm_(psA[g][:], minus[:], peakR[:, b, GH * g:GH * g + GH], start=False, stop=True,
                             skip_group_check=True)
                    mm.then_inc(a_psum, 1)
                pe.wait_ge(staged, 2 * b + 2)
                pe.wait_ge(last_staged, b + 1)
                for g in range(G):
                    after(pe, c_ready, 2 * b + g - 1)
                    for k_part, q_part in PARTS:
                        mm = mm_(psS[g][:], ctxT2[:, k_part, b], qm2[:, par, q_part, GH * g:GH * g + GH],
                                 start=(k_part + q_part == 0), stop=(k_part == 1))
                    mm.then_inc(s_psum, 1)
                if not known(b, 0):
                    values(b - 1, 1 - par)

            over_batches(nc.tensor, slots)
            values(B - 1, (B - 1) % 2)

        @block.scalar
        def _(act):
            def high(b, par, g):
                act.wait_ge(c_ready, 2 * b + g + 1)
                after(act, n_psum, b - 1)
                nc.scalar.copy(cmat2[:, par, 0, GH * g:GH * g + GH],
                               cmat[:, par, GH * g:GH * g + GH]).then_inc(chi_ready, 1)

            def sums(b):
                act.wait_ge(n_psum, b + 1)
                nc.scalar.copy(num[:, b], psN[:]).then_inc(n_ready, 1)

            def slots(b, par):
                act.wait_ge(bias_ready, b + 1)
                for g in range(G):
                    act.wait_ge(a_psum, 2 * b + g + 1)
                    after(act, c_ready, 2 * b + g - 1)
                    for j in range(GH):
                        h = GH * g + j
                        act_ = nc.scalar.activation(decay[:, g, j], psA[g][:, j], ACT.Exp,
                                                    bias=bias_now[:, par, h:h + 1])
                    act_.then_inc(d_ready, 1)
                for g in range(G):
                    high(b, par, g)
                if not known(b, 0):
                    sums(b - 1)

            over_batches(nc.scalar, slots)
            sums(B - 1)
            act.wait_ge(steps["asked"], 4)
            nc.scalar.activation(tmp[:], tmp[:], ACT.Sqrt).then_inc(steps["given"], 1)

        @block.vector
        def _(dve):
            v = nc.vector

            def bias(b, par):
                after(dve, d_ready, 2 * b - 2)
                v.tensor_copy(bias_now[:, par], gainT[:, b]).then_inc(bias_ready, 1)

            def squares(b, par):
                dve.wait_ge(n_ready, b + 1)
                v.tensor_tensor(square[:, par], num[:, b, :, 0:HW1], num[:, b, :, 0:HW1],
                                ALU.mult).then_inc(sq_ready, 1)

            def mean_squares(b, par):
                dve.wait_ge(sq_ready, b + 1)
                v.tensor_reduce(msq[:, b], square[:, par], AX.X, ALU.add).then_inc(ms_ready, 1)

            def stage(b, par):
                after(dve, s_psum, 2 * b - 2)
                for h in range(POOL_H, H1):
                    ins = v.tensor_scalar(qm2[:, par, :, h], qT2[:, :, b], headm[:, h:h + 1], None, ALU.mult)
                ins.then_inc(last_staged, 1)

            bias(0, 0)
            stage(0, 0)

            def slots(b, par):
                if not known(b, B - 1):
                    bias(b + 1, 1 - par)
                    stage(b + 1, 1 - par)
                if not known(b, 0) and not known(b, 1):
                    mean_squares(b - 2, par)
                for g in range(G):
                    dve.wait_ge(d_ready, 2 * b + g + 1)
                    dve.wait_ge(s_psum, 2 * b + g + 1)
                    v.tensor_tensor(cmat[:, par, GH * g:GH * g + GH], psS[g][:], decay[:, g],
                                    ALU.mult).then_inc(c_ready, 1)
                for g in range(G):
                    dve.wait_ge(chi_ready, 2 * b + g + 1)
                    v.tensor_tensor(cmat2[:, par, 1, GH * g:GH * g + GH], cmat[:, par, GH * g:GH * g + GH],
                                    cmat2[:, par, 0, GH * g:GH * g + GH], ALU.subtract).then_inc(clo_ready, 1)
                if not known(b, 0):
                    squares(b - 1, 1 - par)

            over_batches(nc.vector, slots)
            mean_squares(B - 2, B % 2)
            squares(B - 1, (B - 1) % 2)
            mean_squares(B - 1, (B - 1) % 2)
            dve.wait_ge(ms_ready, B)
            order = steps["dve"].on(dve)
            total = num[:, :, :, HW1]
            order.then(v.scalar_tensor_tensor(out=factor[:], in0=total, scalar=-1.0, in1=total,
                                              op0=ALU.mult, op1=ALU.max))
            order.then(v.tensor_tensor(factor[:], factor[:], eguard[:], ALU.max))
            order.then(v.tensor_scalar(factor[:], factor[:], 1e-6, None, ALU.add))
            order.then(v.reciprocal(factor[:], factor[:]))
            order.then(v.tensor_tensor(tmp[:], factor[:], factor[:], ALU.mult))
            order.then(v.tensor_tensor(tmp[:], tmp[:], msq[:], ALU.mult))
            v.tensor_scalar(tmp[:], tmp[:], 1.0 / HW1, 1e-6, ALU.mult, ALU.add).then_inc(steps["asked"], 1)
            dve.wait_ge(steps["given"], 4)
            order.then(v.reciprocal(tmp[:], tmp[:]))
            order.then(v.tensor_tensor(factor[:], factor[:], tmp[:], ALU.mult))
            def statistics(t):
                dve.wait_ge(x_ready, t + 1)
                for b in range(4 * t, 4 * t + 4):
                    order.add(v.bn_stats(bnst[:, b], x_sb[:, b]))

            for t in range(4):
                bs = slice(4 * t, 4 * t + 4)
                v.tensor_tensor(xn[:, bs].rearrange("p b (h e) -> p b h e", h=H1), num[:, bs, :, 0:HW1],
                                factor[:, bs].unsqueeze(3).to_broadcast([P, 4, H1, HW1]),
                                ALU.mult).then_inc(y_ready, 1)
                if t:
                    statistics(t - 1)
            order.sync()
            aggregate(v, order, mv, bnst, range(B - 4))
            statistics(3)


def moe_phase(nc, sb, scope, x_sb, ident, identb, bnst, mv, rstd, steps, later, out):
    TG = 4
    NT = B // TG
    K3 = NSPLIT * E1
    RING = 4
    BANKS = 2
    LAG = 2
    PARTS = ((0, 0), (0, 1), (1, 0))

    def sem(name):
        return scope.enter_context(nc.semaphore(name))

    w2 = later["moe_w2"]
    rw2 = later["rw2"]
    xn = sb("xn4", [P, B, P], F32, scope)
    xT2 = sb("xTe2", [P, 2, B, P], F16, scope)
    order_i = sb("order_i", [P, E1], mybir.dt.int32, scope)
    desc = sb("desc", [P, E1], F32, scope)
    prob = sb("prob4", [P, B, E1], F32, scope)
    best = sb("best", [P, B], F32, scope)
    key = sb("key", [P, B, E1], F32, scope)
    pick = sb("pick", [P, 2, B, E1], F32, scope)
    rest = sb("rest", [P, B, E1], F32, scope)
    coef3 = sb("coef3", [P, B, NSPLIT, E1], BF16, scope)
    coefT = sb("coefT", [P, B, P], BF16, scope)
    spread = sb("spread", [P, EC, 2, FX], BF16, scope)
    act_g = sb("act_g", [P, RING, TG * P], F32, scope)
    prod = sb("prod", [P, RING, TG * P], F32, scope)
    inter = sb("inter", [P, RING, TG * P], F32, scope)
    inter2 = sb("inter2", [P, RING, 2, TG * P], F16, scope)

    psG = [scope.enter_context(nc.psum_tensor(f"psEG{i}", [P, TG * P], F32)) for i in range(BANKS)]
    psU = [scope.enter_context(nc.psum_tensor(f"psEU{i}", [P, TG * P], F32)) for i in range(BANKS)]
    psC = [scope.enter_context(nc.psum_tensor(f"psEC{i}", [P, TG * P], F32)) for i in range(BANKS)]
    psY = scope.enter_context(nc.psum_tensor("psEY", [P, TG, P], F32))
    psS = scope.enter_context(nc.psum_tensor("psES", [P, TG, P], F32))
    shared_y = (psS, psY)
    psR = psC[0][:, 0:B * E1].rearrange("p (b e) -> p b e", b=B)

    const_ready, xT_psum, xhi_ready, xlo_ready, r_psum, shifted, exp_ready = (
        sem(n) for n in ("moe_const_ready", "moe_xT_psum", "moe_xhi_ready", "moe_xlo_ready", "moe_r_psum",
                         "moe_shifted", "moe_exp_ready"))
    coef_ready, coef_psum, coefT_ready = sem("moe_coef_ready"), sem("moe_coef_psum"), sem("moe_coefT_ready")
    sh_read, sh_inter, sh_lo, y_copied = (sem(n) for n in ("moe_sh_read", "moe_sh_inter", "moe_sh_lo",
                                                           "moe_y_copied"))
    gu_psum, g_ready, prod_ready, c_psum, inter_ready, hi_ready, lo_ready, down_done, y_ready, stored = (
        sem(n) for n in ("moe_gu_psum", "moe_g_ready", "moe_prod_ready", "moe_c_psum", "moe_inter_ready",
                         "moe_hi_ready", "moe_lo_ready", "moe_down_done", "moe_y_ready", "moe_stored"))

    def turned(t):
        return psG[t % 2][:].rearrange("p (b d) -> p b d", b=TG)

    def coef_bank(b):
        bank = psC[b // 8][:].bitcast(BF16)
        return bank[0:K3, (b % 8) * P:(b % 8 + 1) * P]

    def rows(a, t):
        return a[:, TG * t:TG * t + TG] if isinstance(t, int) else a[:, bass.ds(TG * t, TG)]

    def flat(a):
        return a.rearrange("p b d -> p (b d)")

    def groups(eng, slots):
        slots(0)
        with eng.Fori(1, NT) as t:
            slots(t)

    def first(t):
        return isinstance(t, int)

    with nc.Block() as block:
        @block.sync
        def _(sp):
            for t in range(NT):
                sp.wait_ge(y_ready, NT + t + 1)
                sp.dma_start(out[TG * t:TG * t + TG].rearrange("b s d -> s b d"),
                             x_sb[:, TG * t:TG * t + TG]).then_inc(stored, 16)
            sp.wait_ge(stored, 16 * NT)

        @block.gpsimd
        def _(pool):
            order = steps["pool"].on(pool)
            order.add(nc.gpsimd.iota(order_i[:], pattern=[[-1, E1]], base=E1, channel_multiplier=0))
            order.add(nc.gpsimd.memset(spread[:], 0.0))
            order.add(nc.gpsimd.memset(coefT[:], 0.0))
            order.sync()
            nc.gpsimd.tensor_copy(desc[:], order_i[:]).then_inc(const_ready, 1)
            for part in range(NSPLIT):
                order.then(nc.gpsimd.affine_select(out=spread[:], in_=spread[:], compare_op=ALU.not_equal,
                                                   fill=1.0, base=-E1 * part,
                                                   pattern=[[-2, EC], [-1, 2], [0, FX]], channel_multiplier=1))
            pool.sem_inc(const_ready, 1)

            def multiply(t):
                pool.wait_ge(sh_read, t + 1)
                nc.gpsimd.tensor_tensor(inter[:, t], act_g[:, t], prod[:, t], ALU.mult).then_inc(sh_inter, 1)

            def low(t):
                pool.wait_ge(hi_ready, t + 1)
                nc.gpsimd.tensor_tensor(inter2[:, t, 1], inter[:, t], inter2[:, t, 0],
                                        ALU.subtract).then_inc(sh_lo, 1)

            def residual(t, copied):
                pool.wait_ge(y_copied, copied)
                nc.gpsimd.tensor_tensor(rows(x_sb, t), rows(x_sb, t), rows(xn, t), ALU.add).then_inc(y_ready, 1)

            multiply(0)
            for t in range(1, NT):
                multiply(t)
                low(t - 1)
            low(NT - 1)
            for t in range(NT):
                residual(t, t + 1)
            for t in range(NT - 1):
                pool.wait_ge(y_ready, NT + t)
                residual(t, NT + t + 1)

        @block.scalar
        def _(act):
            act.wait_ge(steps["asked"], 5)
            nc.scalar.activation(rstd[:], rstd[:], ACT.Sqrt).then_inc(steps["given"], 1)
            nc.scalar.preload_act_table(ACT.Exp)
            act_normalises(nc, act, steps, 3, xn, x_sb, rstd)
            for t in range(NT):
                act.wait_ge(xT_psum, t + 1)
                nc.scalar.copy(xT2[:, 0, TG * t:TG * t + TG], turned(t)).then_inc(xhi_ready, 1)
            act.wait_ge(shifted, 1)
            nc.scalar.activation(prob[:], rest[:], ACT.Exp, scale=1.0 / W_UP).then_inc(exp_ready, 1)
            nc.scalar.preload_act_table(ACT.Silu)

            def shared(t):
                act.wait_ge(gu_psum, t + 1)
                nc.scalar.activation(act_g[:, t], psG[t % BANKS][:], ACT.Silu, scale=1.0 / W_UP)
                nc.scalar.copy(prod[:, t], psU[t % BANKS][:]).then_inc(sh_read, 1)

            def shared_high(t):
                act.wait_ge(sh_inter, t + 1)
                nc.scalar.copy(inter2[:, t, 0], inter[:, t]).then_inc(hi_ready, 1)

            def copy_y(bank, t):
                nc.scalar.activation(rows(xn, t), bank[:], ACT.Copy, scale=W_UP ** -2).then_inc(y_copied, 1)

            def shared_y_out(t):
                act.wait_ge(down_done, t + 1)
                copy_y(shared_y[t % 2], t)

            def coefT_out(k):
                act.wait_ge(coef_psum, k + 1)
                nc.scalar.copy(flat(coefT[0:K3, 8 * k:8 * k + 8]),
                               psC[k][:].bitcast(BF16)[0:K3]).then_inc(coefT_ready, 1)

            def gate(n, e):
                act.wait_ge(gu_psum, NT + n + 1)
                if isinstance(n, int) and n < RING:
                    act.wait_ge(sh_inter, n + 1)
                else:
                    act.wait_ge(prod_ready, n - RING + 1)
                nc.scalar.activation(act_g[:, e % RING], psG[e % BANKS][:], ACT.Silu,
                                     scale=1.0 / W_UP).then_inc(g_ready, 1)

            def high(n, ring):
                act.wait_ge(inter_ready, n + 1)
                act.wait_ge(down_done, NT + n - RING + 1)
                nc.scalar.copy(inter2[:, ring, 0], inter[:, ring]).then_inc(hi_ready, 1)

            shared(0)
            shared(1)
            shared_high(0)
            shared(2)
            shared_high(1)
            shared(3)
            shared_high(2)
            shared_y_out(0)
            gate(0, 0)
            shared_high(3)
            shared_y_out(1)
            act.wait_ge(const_ready, 2)
            coefT_out(0)
            gate(1, 1)
            coefT_out(1)
            shared_y_out(2)
            shared_y_out(3)

            def slots(t):
                for e in range(EC):
                    n = EC * t + e
                    if e == LAG and not first(t):
                        act.wait_ge(down_done, NT + EC * t)
                        act.wait_ge(y_ready, t)
                        copy_y(psY, t - 1)
                    if e >= BANKS or not first(t):
                        gate(n, e)
                    if e or not first(t):
                        high(n - 1, (e - 1) % RING)

            groups(nc.scalar, slots)
            high(EC * NT - 1, (EC - 1) % RING)

        @block.vector
        def _(dve):
            v = nc.vector
            order = steps["dve"].on(dve)
            layernorm_all(v, steps, 5, order, dve, B - TG, bnst, mv, rstd)
            for t in range(NT):
                dve_normalises(v, steps, t, xn, x_sb, mv, rstd)
            for t in range(NT):
                dve.wait_ge(xhi_ready, t + 1)
                v.tensor_tensor(xT2[:, 1, TG * t:TG * t + TG], turned(t), xT2[:, 0, TG * t:TG * t + TG],
                                ALU.subtract).then_inc(xlo_ready, 1)
            wide = [P, B, E1]

            def over(col):
                return col[:].unsqueeze(2).to_broadcast(wide)

            dve.wait_ge(r_psum, 1)
            order.then(v.tensor_reduce(best[:], psR, AX.X, ALU.max))
            order.then(v.tensor_tensor(rest[:], psR, over(best), ALU.subtract))
            dve.sem_inc(shifted, 1)
            dve.wait_ge(const_ready, 2)
            for k in range(2):
                if k:
                    order.then(v.scalar_tensor_tensor(out=key[:].rearrange("p b e -> p (b e)"),
                                                      in0=pick[:, 0].rearrange("p b e -> p (b e)"), scalar=-1e30,
                                                      in1=rest[:].rearrange("p b e -> p (b e)"),
                                                      op0=ALU.mult, op1=ALU.add))
                    order.then(v.tensor_reduce(best[:], key[:], AX.X, ALU.max))
                    order.then(v.tensor_tensor(key[:], key[:], over(best), ALU.is_equal))
                else:
                    order.then(v.tensor_scalar(key[:], rest[:], 0.0, None, ALU.is_equal))
                order.then(v.tensor_tensor(key[:], key[:], desc[:].unsqueeze(1).to_broadcast(wide), ALU.mult))
                order.then(v.tensor_reduce(best[:], key[:], AX.X, ALU.max))
                order.then(v.tensor_tensor(pick[:, k], key[:], over(best), ALU.is_equal))
            dve.wait_ge(exp_ready, 1)
            order.add(v.tensor_reduce(best[:], prob[:], AX.X, ALU.add))
            order.then(v.tensor_tensor(pick[:, 0], pick[:, 0], pick[:, 1], ALU.add))
            order.add(v.tensor_tensor(prob[:], prob[:], pick[:, 0], ALU.mult))
            order.then(v.reciprocal(best[:], best[:]))
            order.then(v.tensor_tensor(prob[:], prob[:], over(best), ALU.mult))
            for part in range(NSPLIT):
                order.then(v.tensor_copy(coef3[:, :, part], prob[:]))
                if part < NSPLIT - 1:
                    order.then(v.tensor_tensor(prob[:], prob[:], coef3[:, :, part], ALU.subtract))
            v.engine_nop().then_inc(coef_ready, 1)

            def low(n, ring):
                dve.wait_ge(hi_ready, NT + n + 1)
                v.tensor_tensor(inter2[:, ring, 1], inter[:, ring], inter2[:, ring, 0],
                                ALU.subtract).then_inc(lo_ready, 1)

            def slots(t):
                for e in range(EC):
                    n = EC * t + e
                    dve.wait_ge(g_ready, n + 1)
                    v.tensor_tensor(prod[:, e % RING], act_g[:, e % RING], psU[e % BANKS][:],
                                    ALU.mult).then_inc(prod_ready, 1)
                    if e or not first(t):
                        low(n - 1, (e - 1) % RING)
                    dve.wait_ge(prod_ready, n + 1)
                    dve.wait_ge(c_psum, n + 1)
                    if first(t) and e < RING:
                        dve.wait_ge(sh_lo, n + 1)
                    else:
                        dve.wait_ge(lo_ready, n - RING + 1)
                    v.tensor_tensor(inter[:, e % RING], prod[:, e % RING], psC[e % BANKS][:],
                                    ALU.mult).then_inc(inter_ready, 1)

            groups(v, slots)
            low(EC * NT - 1, (EC - 1) % RING)
            dve.wait_ge(down_done, NT + EC * NT)
            dve.wait_ge(y_ready, 2 * NT - 1)
            xs = flat(rows(x_sb, NT - 1))
            v.scalar_tensor_tensor(out=xs, in0=flat(psY[:]), scalar=W_UP ** -2, in1=xs,
                                   op0=ALU.mult, op1=ALU.add).then_inc(y_ready, 1)

        @block.tensor
        def _(pe):
            mm_ = nc.tensor.matmul
            for t in range(NT):
                wait_normalised(pe, steps, 3, t)
                if t >= 2:
                    pe.wait_ge(xlo_ready, t - 1)
                for j in range(TG):
                    mm = nc.tensor.transpose(turned(t)[:, j], xn[:, TG * t + j], ident[:])
                mm.then_inc(xT_psum, 1)
            pe.wait_ge(xlo_ready, NT)
            for b in range(B):
                for x_part, w_part in PARTS:
                    mm = mm_(psR[:, b], xT2[:, x_part, b], rw2[:, w_part], start=(b == 0 and x_part + w_part == 0),
                             stop=(b == B - 1 and x_part == 1), skip_group_check=True)
            mm.then_inc(r_psum, 1)

            def products(e, t, free, count):
                if free is not None:
                    pe.wait_ge(free, count)
                for kind, bank in ((0, psG), (1, psU)):
                    for w_part, x_part in PARTS:
                        mm = mm_(bank[e % BANKS][:] if e < EC else bank[t % BANKS][:], w2[:, kind, w_part, e],
                                 rows(xT2[:, x_part], t), start=(w_part + x_part == 0), stop=(w_part == 1))
                mm.then_inc(gu_psum, 1)

            def down(bank, e, ring, begin, end):
                for j in range(TG):
                    for i_part, w_part in PARTS:
                        mm = mm_(bank[:, j], inter2[:, ring, i_part, j * P:(j + 1) * P], w2[:, 2, w_part, e],
                                 start=(begin and j == 0 and i_part + w_part == 0),
                                 stop=(end and j == TG - 1 and i_part == 1), skip_group_check=True)
                mm.then_inc(down_done, 1)

            def shared(t):
                if t < BANKS:
                    products(NC - 1, t, None, 0)
                else:
                    products(NC - 1, t, sh_read, t - BANKS + 1)

            def shared_down(t):
                pe.wait_ge(sh_lo, t + 1)
                if t >= 2:
                    pe.wait_ge(y_copied, t - 1)
                down(shared_y[t % 2], NC - 1, t, True, True)

            def routed(t, e):
                n = EC * t + e
                if first(t) and e < BANKS:
                    products(e, t, sh_read, NT + n - BANKS + 1)
                else:
                    products(e, t, prod_ready, n - BANKS + 1)

            def coefficients(t, e):
                n = EC * t + e
                if first(t) and e < BANKS:
                    pe.wait_ge(coefT_ready, e + 1)
                else:
                    pe.wait_ge(inter_ready, n - BANKS + 1)
                mm_(psC[e % BANKS][:], spread[:, e].rearrange("k a f -> k (a f)"), rows(coefT, t),
                    start=True, stop=True).then_inc(c_psum, 1)

            def routed_down(t, e):
                n = EC * t + e
                pe.wait_ge(lo_ready, n + 1)
                if e == 0:
                    pe.wait_ge(y_copied, NT + t)
                down(psY, e, e % RING, e == 0, e == EC - 1)

            for t in range(NT):
                shared(t)
            routed(0, 0)
            shared_down(0)
            routed(0, 1)
            shared_down(1)
            pe.wait_ge(coef_ready, 1)
            for b in range(B):
                mm = nc.tensor.transpose(coef_bank(b), coef3[:, b].rearrange("p k e -> p (k e)"), identb[:])
                if b % 8 == 7:
                    mm.then_inc(coef_psum, 1)
            pe.wait_ge(const_ready, 2)
            shared_down(2)
            coefficients(0, 0)
            shared_down(3)
            coefficients(0, 1)

            def slots(t):
                for e in range(EC):
                    if not (first(t) and e < BANKS):
                        routed(t, e)
                        coefficients(t, e)
                    if e >= LAG:
                        routed_down(t, e - LAG)
                    elif not first(t):
                        routed_down(t - 1, EC - LAG + e)

            groups(nc.tensor, slots)
            for e in range(EC - LAG, EC):
                routed_down(NT - 1, e)


_INS = ['x', 'ctx_1024', 'fside_BxSx4_0', 'L0_xattn_Wq', 'L0_xattn_bq', 'L0_xattn_Wk', 'L0_xattn_bk',
        'L0_xattn_Wv', 'L0_xattn_bv', 'L0_xattn_Wo', 'L0_xattn_bo', 'L0_xattn_Wg', 'L0_xattn_bg',
        'L0_ffn_w1', 'L0_ffn_b1', 'L0_ffn_w2', 'L0_ffn_b2', 'L1_xattn_igate_kernel', 'L1_xattn_igate_bias',
        'L1_xattn_fgate_kernel', 'L1_xattn_fgate_bias', 'L1_ffn_router_w', 'L1_ffn_gate_w', 'L1_ffn_up_w',
        'L1_ffn_down_w', 'L1_ffn_shared_gate_w', 'L1_ffn_shared_up_w', 'L1_ffn_shared_down_w']
STAGE = 4


def kernel(**inputs):
    import numpy as _np
    import concourse.bacc as _bacc
    from concourse import mybir as _mybir
    from concourse.bass_utils import run_bass_kernel_spmd as _run

    nc = _bacc.Bacc("TRN2", target_bir_lowering=False, num_devices=1)
    arrays, tensors = {}, {}
    for name in _INS:
        a = _np.ascontiguousarray(inputs[name])
        arrays[f"in_{name}_dram"] = a
        tensors[name] = nc.dram_tensor(f"in_{name}_dram", a.shape, _mybir.dt.from_np(a.dtype),
                                       kind="ExternalInput").ap()
    out = nc.dram_tensor("out_0_dram", (B, P, P), F32, kind="ExternalOutput").ap()
    build(nc, tensors, out, STAGE)
    r = _run(nc, [arrays], core_ids=[0])
    return r.results[0]["out_0_dram"]
```
